# Optimizing a Trainium2 kernel written in Bass

```python
import numpy as np
import jax
import jax.numpy as jnp

def _softmax(x, axis=-1):
    return jax.nn.softmax(x, axis=axis)

def _gelu(x):
    return jax.nn.gelu(x, approximate=True)

def _silu(x):
    return jax.nn.silu(x)

def _sigmoid(x):
    return jax.nn.sigmoid(x)

def _layernorm(x, axis=-1, eps=1e-05):
    m = jnp.mean(x, axis=axis, keepdims=True)
    v = jnp.var(x, axis=axis, keepdims=True)
    return (x - m) / jnp.sqrt(v + eps)

def _scatter_add(tgt, idx, src, axis=0):
    return tgt.at[idx].add(src)

def _segment_sum(src, seg, n):
    return jax.ops.segment_sum(src, seg, n)
kernel_name = 'mk_prb_d1_jaxref_r8_c0a80e'

def setup_inputs(seed: int=0):
    np.random.seed(seed)
    _w = jnp.asarray

    def _L0_attn_setup():
        import jax, jax.numpy as jnp
        import numpy as np
        EPS = 1e-06
        CHUNK = 32
        N_HEADS = 16
        GATE_NORM = 16.0

        def rmsnorm(x, eps=EPS):
            return x * jax.lax.rsqrt(jnp.mean(x * x, axis=-1, keepdims=True) + eps)

        def chunk_gate_retention(q, k, v, gt, chunk_size):
            b, h, t, d = q.shape
            c = chunk_size
            n = t // c
            scale = d ** (-0.5)
            q = q.reshape(b, h, n, c, d) * scale
            k = k.reshape(b, h, n, c, d)
            v = v.reshape(b, h, n, c, d)
            g = gt.reshape(b, h, n, c)
            bc = jnp.cumsum(g, axis=-1)
            B = bc[..., -1:]
            decay = jnp.exp(bc[..., :, None] - bc[..., None, :])
            mask = jnp.tril(jnp.ones((c, c), dtype=bool))
            A = jnp.einsum('bhnid,bhnjd->bhnij', q, k) * jnp.where(mask, decay, 0.0)
            o_intra = jnp.einsum('bhnij,bhnjd->bhnid', A, v)
            kd = k * jnp.exp(B - bc)[..., None]
            kv = jnp.einsum('bhncd,bhnce->bhnde', kd, v)
            qd = q * jnp.exp(bc)[..., None]

            def step(S, inp):
                qd_n, kv_n, B_n = inp
                o_cross = jnp.einsum('bhcd,bhde->bhce', qd_n, S)
                S_new = jnp.exp(B_n)[..., None] * S + kv_n
                return (S_new, o_cross)
            S0 = jnp.zeros((b, h, d, d), dtype=q.dtype)
            inps = (jnp.moveaxis(qd, 2, 0), jnp.moveaxis(kv, 2, 0), jnp.moveaxis(B, 2, 0))
            S_last, o_cross = jax.lax.scan(step, S0, inps)
            o_cross = jnp.moveaxis(o_cross, 0, 2)
            o = (o_intra + o_cross).reshape(b, h, t, d)
            return (o, S_last)
        key = jax.random.key(seed)
        ks = jax.random.split(key, 7)
        dim, nh = (128, N_HEADS)
        s = 0.03
        return {'x': jax.random.normal(ks[0], (2, 1024, dim), dtype=jnp.float32), 'Wq': jax.random.normal(ks[1], (dim, dim), dtype=jnp.float32) * s, 'Wk': jax.random.normal(ks[2], (dim, dim), dtype=jnp.float32) * s, 'Wv': jax.random.normal(ks[3], (dim, dim), dtype=jnp.float32) * s, 'Wg': jax.random.normal(ks[4], (dim, dim), dtype=jnp.float32) * s, 'Wgt': jax.random.normal(ks[5], (dim, nh), dtype=jnp.float32) * s, 'Wo': jax.random.normal(ks[6], (dim, dim), dtype=jnp.float32) * s}
    _L0_attn_in = _L0_attn_setup()

    def _L0_ffn_setup():
        import math
        import jax
        import jax.numpy as jnp
        import numpy as np
        B, T, D = (1, 256, 128)
        H, KV, DH = (16, 4, 64)
        E, TOPK, DFF = (32, 4, 128)
        WINDOW = 128
        EPS = 1e-05
        ROPE_BASE = 150000.0
        ROPE_SCALE = 32.0

        def _rmsnorm(x, w):
            rms = jax.lax.rsqrt(jnp.mean(x * x, axis=-1, keepdims=True) + EPS)
            return w * (x * rms)

        def _apply_rope(x, sin, cos):
            x1, x2 = (x[..., ::2], x[..., 1::2])
            out = jnp.stack([x1 * cos - x2 * sin, x1 * sin + x2 * cos], axis=-1)
            return out.reshape(x.shape)
        key = jax.random.key(seed)
        ks = jax.random.split(key, 12)
        s = 0.02
        return {'x': jax.random.normal(ks[0], (B, T, D), jnp.float32), 'attn_norm_w': 1.0 + 0.02 * jax.random.normal(ks[1], (D,), jnp.float32), 'ffn_norm_w': 1.0 + 0.02 * jax.random.normal(ks[2], (D,), jnp.float32), 'qkv_w': s * jax.random.normal(ks[3], (D, H * DH + 2 * KV * DH), jnp.float32), 'qkv_b': s * jax.random.normal(ks[4], (H * DH + 2 * KV * DH,), jnp.float32), 'proj_w': s * jax.random.normal(ks[5], (H * DH, D), jnp.float32), 'proj_b': s * jax.random.normal(ks[6], (D,), jnp.float32), 'attn_sink': 0.5 * jax.random.normal(ks[7], (H,), jnp.float32), 'gate_w': s * jax.random.normal(ks[8], (D, E), jnp.float32), 'gate_b': s * jax.random.normal(ks[9], (E,), jnp.float32), 'W_up': s * jax.random.normal(ks[10], (E, D, 2 * DFF), jnp.float32), 'W_down': s * jax.random.normal(ks[11], (E, DFF, D), jnp.float32)}
    _L0_ffn_in = _L0_ffn_setup()
    _d = {'L0_attn_x': _L0_attn_in['x'], 'L0_attn_Wq': _L0_attn_in['Wq'], 'L0_attn_Wk': _L0_attn_in['Wk'], 'L0_attn_Wv': _L0_attn_in['Wv'], 'L0_attn_Wg': _L0_attn_in['Wg'], 'L0_attn_Wgt': _L0_attn_in['Wgt'], 'L0_attn_Wo': _L0_attn_in['Wo'], 'L0_ffn_attn_norm_w': _L0_ffn_in['attn_norm_w'], 'L0_ffn_ffn_norm_w': _L0_ffn_in['ffn_norm_w'], 'L0_ffn_qkv_w': _L0_ffn_in['qkv_w'], 'L0_ffn_qkv_b': _L0_ffn_in['qkv_b'], 'L0_ffn_proj_w': _L0_ffn_in['proj_w'], 'L0_ffn_proj_b': _L0_ffn_in['proj_b'], 'L0_ffn_attn_sink': _L0_ffn_in['attn_sink'], 'L0_ffn_gate_w': _L0_ffn_in['gate_w'], 'L0_ffn_gate_b': _L0_ffn_in['gate_b'], 'L0_ffn_W_up': _L0_ffn_in['W_up'], 'L0_ffn_W_down': _L0_ffn_in['W_down']}
    _x0 = _d['L0_attn_x']
    _d['L0_attn_x'] = jax.random.normal(jax.random.fold_in(jax.random.key(seed), 1), (8, 512, 128), dtype=_x0.dtype)
    del _x0
    return _d

def reference(L0_attn_x, L0_attn_Wq, L0_attn_Wk, L0_attn_Wv, L0_attn_Wg, L0_attn_Wgt, L0_attn_Wo, L0_ffn_attn_norm_w, L0_ffn_ffn_norm_w, L0_ffn_qkv_w, L0_ffn_qkv_b, L0_ffn_proj_w, L0_ffn_proj_b, L0_ffn_attn_sink, L0_ffn_gate_w, L0_ffn_gate_b, L0_ffn_W_up, L0_ffn_W_down):

    def _L0_attn_ref(x, Wq, Wk, Wv, Wg, Wgt, Wo):
        import jax, jax.numpy as jnp
        import numpy as np
        EPS = 1e-06
        CHUNK = 32
        N_HEADS = 16
        GATE_NORM = 16.0

        def rmsnorm(x, eps=EPS):
            return x * jax.lax.rsqrt(jnp.mean(x * x, axis=-1, keepdims=True) + eps)

        def chunk_gate_retention(q, k, v, gt, chunk_size):
            b, h, t, d = q.shape
            c = chunk_size
            n = t // c
            scale = d ** (-0.5)
            q = q.reshape(b, h, n, c, d) * scale
            k = k.reshape(b, h, n, c, d)
            v = v.reshape(b, h, n, c, d)
            g = gt.reshape(b, h, n, c)
            bc = jnp.cumsum(g, axis=-1)
            B = bc[..., -1:]
            decay = jnp.exp(bc[..., :, None] - bc[..., None, :])
            mask = jnp.tril(jnp.ones((c, c), dtype=bool))
            A = jnp.einsum('bhnid,bhnjd->bhnij', q, k) * jnp.where(mask, decay, 0.0)
            o_intra = jnp.einsum('bhnij,bhnjd->bhnid', A, v)
            kd = k * jnp.exp(B - bc)[..., None]
            kv = jnp.einsum('bhncd,bhnce->bhnde', kd, v)
            qd = q * jnp.exp(bc)[..., None]

            def step(S, inp):
                qd_n, kv_n, B_n = inp
                o_cross = jnp.einsum('bhcd,bhde->bhce', qd_n, S)
                S_new = jnp.exp(B_n)[..., None] * S + kv_n
                return (S_new, o_cross)
            S0 = jnp.zeros((b, h, d, d), dtype=q.dtype)
            inps = (jnp.moveaxis(qd, 2, 0), jnp.moveaxis(kv, 2, 0), jnp.moveaxis(B, 2, 0))
            S_last, o_cross = jax.lax.scan(step, S0, inps)
            o_cross = jnp.moveaxis(o_cross, 0, 2)
            o = (o_intra + o_cross).reshape(b, h, t, d)
            return (o, S_last)
        b, t, dim = x.shape
        h = N_HEADS
        d = dim // h
        q = rmsnorm(x @ Wq)
        k = rmsnorm(x @ Wk)
        v = rmsnorm(x @ Wv)
        g = x @ Wg
        gt = jax.nn.log_sigmoid(x @ Wgt) / GATE_NORM
        qr = q.reshape(b, t, h, d).transpose(0, 2, 1, 3)
        kr = k.reshape(b, t, h, d).transpose(0, 2, 1, 3)
        vr = v.reshape(b, t, h, d).transpose(0, 2, 1, 3)
        gtr = gt.transpose(0, 2, 1)
        o, _ = chunk_gate_retention(qr, kr, vr, gtr, CHUNK)
        o = rmsnorm(o)
        o = o.transpose(0, 2, 1, 3).reshape(b, t, dim)
        o = jax.nn.silu(g) * o
        return o @ Wo

    def _L0_ffn_ref(x, attn_norm_w, ffn_norm_w, qkv_w, qkv_b, proj_w, proj_b, attn_sink, gate_w, gate_b, W_up, W_down):
        import math
        import jax
        import jax.numpy as jnp
        import numpy as np
        B, T, D = (1, 256, 128)
        H, KV, DH = (16, 4, 64)
        E, TOPK, DFF = (32, 4, 128)
        WINDOW = 128
        EPS = 1e-05
        ROPE_BASE = 150000.0
        ROPE_SCALE = 32.0

        def _rmsnorm(x, w):
            rms = jax.lax.rsqrt(jnp.mean(x * x, axis=-1, keepdims=True) + EPS)
            return w * (x * rms)

        def _apply_rope(x, sin, cos):
            x1, x2 = (x[..., ::2], x[..., 1::2])
            out = jnp.stack([x1 * cos - x2 * sin, x1 * sin + x2 * cos], axis=-1)
            return out.reshape(x.shape)
        Bx, Tx, Dx = x.shape
        h = _rmsnorm(x, attn_norm_w)
        qkv = h @ qkv_w + qkv_b
        q = qkv[..., :H * DH].reshape(Bx, Tx, H, DH).transpose(0, 2, 1, 3)
        k = qkv[..., H * DH:H * DH + KV * DH].reshape(Bx, Tx, KV, DH).transpose(0, 2, 1, 3)
        v = qkv[..., H * DH + KV * DH:].reshape(Bx, Tx, KV, DH).transpose(0, 2, 1, 3)
        pos = jnp.arange(Tx, dtype=jnp.float32) / ROPE_SCALE
        inv_freq = 1.0 / ROPE_BASE ** (jnp.arange(0, DH, 2, dtype=jnp.float32) / DH)
        freqs = pos[:, None] * inv_freq[None, :]
        sin, cos = (jnp.sin(freqs), jnp.cos(freqs))
        q = _apply_rope(q, sin, cos)
        k = _apply_rope(k, sin, cos)
        rep = H // KV
        k = jnp.repeat(k, rep, axis=1)
        v = jnp.repeat(v, rep, axis=1)
        logits = jnp.einsum('bhqd,bhkd->bhqk', q, k) / math.sqrt(DH)
        i = jnp.arange(Tx)[:, None]
        j = jnp.arange(Tx)[None, :]
        mask = (j > i) | (i - j > WINDOW)
        logits = jnp.where(mask, -jnp.inf, logits)
        lse = jax.nn.logsumexp(logits, axis=-1, keepdims=True)
        denom_log = jnp.logaddexp(lse, attn_sink.reshape(1, H, 1, 1))
        attn = jnp.exp(logits - denom_log)
        y = jnp.einsum('bhqk,bhkd->bhqd', attn, v)
        y = y.transpose(0, 2, 1, 3).reshape(Bx, Tx, H * DH)
        x = x + (y @ proj_w + proj_b)
        h2 = _rmsnorm(x, ffn_norm_w).reshape(Bx * Tx, Dx)
        glogits = h2 @ gate_w + gate_b
        topv, topi = jax.lax.top_k(glogits, TOPK)
        gw = jax.nn.softmax(topv, axis=-1)
        N = Bx * Tx
        combine = jnp.zeros((N, E), x.dtype).at[jnp.arange(N)[:, None], topi].add(gw)

        def body(acc, we):
            wu, wd, ce = we
            ug = h2 @ wu
            u, g = (ug[:, :DFF], ug[:, DFF:])
            return (acc + ce[:, None] * (jax.nn.silu(g) * u @ wd), None)
        y2, _ = jax.lax.scan(body, jnp.zeros_like(h2), (W_up, W_down, combine.T))
        return x + y2.reshape(Bx, Tx, Dx)
    x = L0_attn_x
    xn = _layernorm(x, axis=-1)
    x = x + _L0_attn_ref(xn, L0_attn_Wq, L0_attn_Wk, L0_attn_Wv, L0_attn_Wg, L0_attn_Wgt, L0_attn_Wo) + _L0_ffn_ref(xn, L0_ffn_attn_norm_w, L0_ffn_ffn_norm_w, L0_ffn_qkv_w, L0_ffn_qkv_b, L0_ffn_proj_w, L0_ffn_proj_b, L0_ffn_attn_sink, L0_ffn_gate_w, L0_ffn_gate_b, L0_ffn_W_up, L0_ffn_W_down)
    return x

_drawn_inputs = setup_inputs


def setup_inputs(seed=0):
    import zlib

    import numpy as np

    out = dict(_drawn_inputs(seed))
    spreads = {}
    factors = {'L0_attn_Wgt': 200.0,
     'L0_ffn_attn_norm_w': 8.0,
     'L0_ffn_ffn_norm_w': 8.0,
     'L0_ffn_qkv_w': 6.966,
     'L0_ffn_qkv_b': 8.0,
     'L0_ffn_proj_w': 5.754,
     'L0_ffn_proj_b': 36.938,
     'L0_ffn_attn_sink': 29.173,
     'L0_ffn_gate_w': 8.0,
     'L0_ffn_gate_b': 8.0,
     'L0_ffn_W_up': 8.0,
     'L0_ffn_W_down': 8.0,
     'L0_attn_Wq': 22.682,
     'L0_attn_Wk': 22.6,
     'L0_attn_Wv': 22.654,
     'L0_attn_Wg': 26.035,
     'L0_attn_Wo': 22.603}
    for name, (base, spread) in spreads.items():
        noise = np.random.default_rng([zlib.crc32(name.encode()), seed]).standard_normal(out[name].shape)
        drawn = base * np.exp(spread * noise) if base else spread * noise
        out[name] = jnp.asarray(drawn.astype(out[name].dtype))
    for name, factor in factors.items():
        out[name] = (out[name] * factor).astype(out[name].dtype)
    return out
```

```python
from contextlib import ExitStack, contextmanager

import numpy as np

import concourse.bass as bass
from concourse import mybir

F32 = mybir.dt.float32
F32R = mybir.dt.float32r
BF16 = mybir.dt.bfloat16
I32 = mybir.dt.int32
U32 = mybir.dt.uint32
ALU = mybir.AluOpType
ACT = mybir.ActivationFunctionType
AXX = mybir.AxisListType.X

P = 128
B, T, D = 8, 512, 128
TB = T // P
NT = B * TB
LN_EPS = 1e-5
RMS_EPS_R = 1e-6
RMS_EPS_F = 1e-5
HR, DR = 16, 8
H, KV, DH = 16, 4, 64
HG = H // KV
NQ = H // 2
NCH = NQ + KV // 2
E, TOPK, DFF = 32, 4, 128
NBLK = (B * T * TOPK + E * (P - 1)) // P + 1
BPI = 16
NBLK = -(-NBLK // BPI) * BPI
SLOTS = NBLK * P
NEG = -1e30
NEG_R = -30000.0


def bc(ap, shape):
    return ap.to_broadcast(shape)


class Steps:

    def __init__(self, eng, sem):
        self.eng, self.sem, self.n = eng, sem, 0

    def __call__(self, ins):
        self.n += 1
        ins.then_inc(self.sem, 1)
        return self.n

    def wait(self, n=None):
        self.eng.wait_ge(self.sem, self.n if n is None else n)


@contextmanager
def semaphores(nc, names):
    with ExitStack() as ctx:
        s = {n: ctx.enter_context(nc.semaphore(n)) for n in names.split()}
        yield s
        for q in s.values():
            nc.gpsimd.sem_clear(q)
        nc.all_engine_barrier()


def load(nc, m, a):
    with semaphores(nc, "loaded_x loaded_w zeroed scr_zeroed prepared") as s:
        with nc.Block() as block:
            @block.sync
            def _(sp):
                sp.dma_start(m.acc[:], a["x"].rearrange("b (t p) d -> p (b t) d", p=P)).then_inc(s["loaded_x"], 16)
                for src, dst in (
                    (a["Wq"], m.wr[:, 0:128]), (a["Wk"], m.wr[:, 128:256]),
                    (a["Wv"], m.wr[:, 256:384]), (a["Wg"], m.wr[:, 384:512]),
                    (a["Wgt"], m.wgt[:]), (a["Wo"], m.wo[:]),
                    (a["qkv_w"], m.qkvw[:]), (a["gate_w"], m.gatew[:]),
                    (a["proj_w"].rearrange("(c p) n -> p c n", p=P), m.projw[:]),
                    (a["attn_norm_w"].rearrange("(p o) -> p o", o=1), m.wn[:, 0:1]),
                    (a["ffn_norm_w"].rearrange("(p o) -> p o", o=1), m.wn[:, 1:2]),
                ):
                    sp.dma_start(dst, src).then_inc(s["loaded_w"], 16)
                for n in range(NCH):
                    for half in range(2):
                        c0 = chunk_channels(n)[half]
                        src = a["qkv_b"][c0:c0 + DH]
                        rows = slice(DH * half, DH * half + DH)
                        sp.dma_start(m.qkb[rows, n:n + 1], src.rearrange("(p o) -> p o", o=1)).then_inc(s["loaded_w"], 16)
                for name in TABLES:
                    sp.dma_start(m[name][:], a[name]).then_inc(s["loaded_w"], 16)
                for q in ("loaded_x", "loaded_w"):
                    sp.wait_ge(s[q], {"loaded_x": 16, "loaded_w": 16 * (11 + 2 * NCH + len(TABLES))}[q])

            @block.scalar
            def _(act):
                n = 0
                for src, dst in ((a["qkv_b"][H * DH + KV * DH:], m.vb[:]), (a["proj_b"], m.projb[:]),
                                 (a["gate_b"], m.gateb[:]), (a["attn_sink"], m.sink[:])):
                    act.dma_start(dst, src.rearrange("(o n) -> o n", o=1).partition_broadcast(P)).then_inc(s["prepared"], 16)
                    n += 1
                act.wait_ge(s["prepared"], 16 * n)

            @block.gpsimd
            def _(pool):
                nc.gpsimd.memset(m.zero[:], 0.0).then_inc(s["zeroed"], 1)
                pool.wait_ge(s["zeroed"], 1)
                rows = NBLK // 8
                for i in range(8):
                    pool.dma_start(a["slots_x"][i * rows * P:(i + 1) * rows * P, :].rearrange("(r p) n -> p r n", p=P),
                                   bc(m.zero[:, None, :], [P, rows, D])).then_inc(s["scr_zeroed"], 16)
                pool.wait_ge(s["scr_zeroed"], 16 * 8)

        with semaphores(nc, "own ident_bf") as s2, nc.Block() as block:
            @block.vector
            def _(dve):
                own = Steps(dve, s2["own"])
                w, g = m.qkvw, m.wn[:, 0:1]
                for n in range(NCH):
                    for half in range(2):
                        c0 = chunk_channels(n)[half]
                        src = w[:, c0:c0 + DH]
                        pairs = src.rearrange("p (i two) -> p i two", two=2)
                        own(nc.vector.tensor_scalar(m.wqk[:, n, DH * half:DH * half + DH], src, g, None, ALU.mult))
                        swap = m.wqk_swap[:, n, DH * half:DH * half + DH].rearrange("p (i two) -> p i two", two=2)
                        own(nc.vector.tensor_scalar(swap[:, :, 0], pairs[:, :, 1], g, None, ALU.mult))
                        own(nc.vector.tensor_scalar(swap[:, :, 1], pairs[:, :, 0], g, None, ALU.mult))
                own(nc.vector.tensor_scalar(m.wv[:], w[:, H * DH + KV * DH:], g, None, ALU.mult))
                own(nc.vector.tensor_scalar(m.gatew[:], m.gatew[:], m.wn[:, 1:2], None, ALU.mult))
                own(nc.vector.tensor_copy(m.ident_bf[:], m.ident[:]))
                own(nc.vector.tensor_scalar(m.sink8[:], m.sink[:], float(DH) ** 0.5, None, ALU.mult))
                own(nc.vector.tensor_copy(m.future_bf[:], bc(m.future[:, None, :], [P, 4, P])))
                own(nc.vector.memset(m.tot_ones[:], 1.0))
                own(nc.vector.memset(m.minus_half[:], -0.5))
                own(nc.vector.memset(m.ones_bf[:], 1.0))
                own(nc.vector.tensor_copy(m.before_bf[:], m.before[:]))
                own.wait()

            @block.tensor
            def _(pe):
                pe.matmul(m.ps[:, 0, 0:NCH], m.swap_rows[:], m.qkb[:], start=True, stop=True).then_inc(s2["ident_bf"], 1)

            @block.scalar
            def _(act):
                act.wait_ge(s2["ident_bf"], 1)
                act.copy(m.qkb_swap[:], m.ps[:, 0, 0:NCH]).then_inc(s2["ident_bf"], 1)
                act.wait_ge(s2["ident_bf"], 2)


def chunk_channels(n):
    if n < NQ:
        pair, j = divmod(n, HG)
        return ((2 * pair) * HG + j) * DH, ((2 * pair + 1) * HG + j) * DH
    kv = 2 * (n - NQ)
    return (H + kv) * DH, (H + kv + 1) * DH


def head_place(g, j):
    return (g // 2) * HG + j, DH * (g % 2)


def normalise(nc, m):
    with nc.Fori(0, B) as b:
        with semaphores(nc, "ve_ready r1_ready ms_ready r2_ready xn_ready h_ready own xn_T h_T xT_ready z_done ev") as s:
            tiles = bass.ds(b * TB, TB)
            with nc.Block() as block:
                @block.vector
                def _(dve):
                    own = Steps(dve, s["own"])
                    for t in range(TB):
                        own(nc.vector.bn_stats(m.stats[:, t, :], m.acc[:, bass.ds(b * TB + t, 1), :].rearrange("p a d -> p (a d)")))
                    for t in range(TB):
                        own.wait(t + 1)
                        own(nc.vector.bn_aggr(m.meanvar[:, t, :], m.stats[:, t, :]))
                    own.wait()
                    nc.vector.tensor_scalar(m.ve[:, 0:TB], m.meanvar[:, :, 1], LN_EPS, None, ALU.add).then_inc(s["ve_ready"], 1)
                    dve.wait_ge(s["r1_ready"], 1)
                    own(nc.vector.tensor_tensor(m.ve[:, 4:4 + TB], m.meanvar[:, :, 1], m.r1[:, 0:TB], ALU.mult))
                    own.wait()
                    own(nc.vector.tensor_tensor(m.ve[:, 8:8 + TB], m.ve[:, 4:4 + TB], m.r1[:, 0:TB], ALU.mult))
                    own.wait()
                    nc.vector.tensor_scalar(m.ve[:, 12:12 + TB], m.ve[:, 8:8 + TB], RMS_EPS_F, None, ALU.add).then_inc(s["ms_ready"], 1)
                    for t in range(TB):
                        nc.vector.tensor_scalar(m.xs[:, t, :], m.acc[:, bass.ds(b * TB + t, 1), :].rearrange("p a d -> p (a d)"),
                                                m.meanvar[:, t, 0:1], m.r1[:, t:t + 1],
                                                ALU.subtract, ALU.mult).then_inc(s["xn_ready"], 1)
                    dve.wait_ge(s["r2_ready"], 1)
                    dve.wait_ge(s["xn_ready"], TB)
                    for t in range(TB):
                        nc.vector.tensor_scalar(m.hs[:, t, :], m.xs[:, t, :], m.r2[:, t:t + 1], None,
                                                ALU.mult).then_inc(s["h_ready"], 1)
                    own(nc.vector.tensor_copy(m.xn[:, tiles, :], m.xs[:]))
                    dve.wait_ge(s["h_T"], 1)
                    own(nc.vector.tensor_copy(m.hT[:, bass.ds(b * T, T)], m.ps[:, 1, :]))
                    dve.wait_ge(s["z_done"], 1)
                    own(nc.vector.tensor_copy(m.z[:, bass.ds(b * TB * HR, TB * HR)], m.ps[:, 2, 0:TB * HR]))

                @block.gpsimd
                def _(pool):
                    pool.wait_ge(s["ve_ready"], 1)
                    nc.gpsimd.tensor_tensor(m.r1[:, 0:TB], m.ve[:, 0:TB], m.minus_half[:, 0:TB], ALU.pow).then_inc(s["r1_ready"], 1)
                    pool.wait_ge(s["ms_ready"], 1)
                    nc.gpsimd.tensor_tensor(m.r2[:, 0:TB], m.ve[:, 12:12 + TB], m.minus_half[:, 0:TB], ALU.pow).then_inc(s["r2_ready"], 1)

                @block.tensor
                def _(pe):
                    for t in range(TB):
                        pe.wait_ge(s["xn_ready"], t + 1)
                        mm = pe.transpose(m.ps[:, 0, t * P:(t + 1) * P], m.xs[:, t, :], m.ident[:])
                    mm.then_inc(s["xn_T"], 1)
                    for t in range(TB):
                        pe.wait_ge(s["h_ready"], t + 1)
                        mm = pe.transpose(m.ps[:, 1, t * P:(t + 1) * P], m.hs[:, t, :], m.ident[:])
                    mm.then_inc(s["h_T"], 1)
                    pe.wait_ge(s["xT_ready"], 1)
                    for t in range(TB):
                        mm = pe.matmul(m.ps[:, 2, t * HR:(t + 1) * HR], m.xTs[:, t * P:(t + 1) * P], m.wgt[:], start=True, stop=True)
                    mm.then_inc(s["z_done"], 1)

                @block.scalar
                def _(act):
                    act.wait_ge(s["xn_T"], 1)
                    act.copy(m.xTs[:], m.ps[:, 0, :]).then_inc(s["xT_ready"], 1)
                    act.wait_ge(s["xT_ready"], 1)
                    act.copy(m.xT[:, bass.ds(b * T, T)], m.xTs[:]).then_inc(s["ev"], 1)


def gates(nc, m):
    with semaphores(nc, "dve e_ready l_ready g_ready bc_done rem_done tot_done exps parts_ready T_done T_free") as s:
        with nc.Block() as block:
            NC = NT * HR
            big = m.h2[:].rearrange("p t d -> p (t d)")
            @block.vector
            def _(dve):
                own = Steps(dve, s["dve"])
                a1, a2, a3 = big[:, 0:NC], big[:, NC:2 * NC], big[:, 2 * NC:3 * NC]
                own(nc.vector.scalar_tensor_tensor(out=a1, in0=m.z[:], scalar=-1.0, in1=m.z[:], op0=ALU.mult, op1=ALU.min))
                dve.wait_ge(s["e_ready"], 1)
                dve.wait_ge(s["l_ready"], 1)
                own(nc.vector.scalar_tensor_tensor(out=a1, in0=m.z[:], scalar=0.0, in1=a3, op0=ALU.min, op1=ALU.subtract))
                own.wait()
                nc.vector.tensor_scalar(m.gt[:], a1, 1.0 / 16.0, None, ALU.mult).then_inc(s["g_ready"], 1)
                dve.wait_ge(s["bc_done"], 1)
                parts = m.bc4[:, :, :].rearrange("p t (k h) -> p t k h", k=4)
                bcv = m.ps[:, 0, :].rearrange("p (t h) -> p t h", h=HR)
                own(nc.vector.tensor_copy(parts[:, :, 0, :], bcv))
                own.wait()
                own(nc.vector.tensor_tensor(parts[:, :, 1, :], bcv, parts[:, :, 0, :].bitcast(F32), ALU.subtract))
                own.wait()
                own(nc.vector.tensor_scalar(parts[:, :, 2, :], parts[:, :, 0, :].bitcast(F32), -1.0, None, ALU.mult))
                nc.vector.tensor_scalar(parts[:, :, 3, :], parts[:, :, 1, :].bitcast(F32), -1.0, None, ALU.mult).then_inc(s["parts_ready"], 1)
                dve.wait_ge(s["tot_done"], 1)
                own(nc.vector.tensor_tensor(a2.rearrange("p (t h) -> p t h", h=HR), m.ps[:, 2, :].rearrange("p (t h) -> p t h", h=HR),
                                            bc(m.row_head[:, None, :], [P, NT, HR]), ALU.mult))
                own.wait()
                own(nc.vector.tensor_reduce(m.decay_tile[:], a2.rearrange("p (t h) -> p t h", h=HR), AXX, ALU.add))
                for q in range(4):
                    dve.wait_ge(s["T_done"], q + 1)
                    own(nc.vector.tensor_scalar(m.argL[:, 4 * q:4 * q + 4, :], m.ps[:, 4 + q % 2, :].rearrange("p (q i) -> p q i", i=P),
                                                m.arg_rows[:, 0:1], m.arg_rows[:, 1:2], ALU.mult, ALU.add))
                    nc.vector.tensor_scalar(m.argR[:, 4 * q:4 * q + 4, :], m.ps[:, 4 + q % 2, :].rearrange("p (q i) -> p q i", i=P),
                                            m.arg_rows[:, 2:3], m.arg_rows[:, 3:4], ALU.mult, ALU.add).then_inc(s["T_free"], 1)

            @block.tensor
            def _(pe):
                pe.wait_ge(s["g_ready"], 1)
                pe.matmul(m.ps[:, 0, :], m.upto[:], m.gt[:], start=True, stop=True).then_inc(s["bc_done"], 1)
                pe.matmul(m.ps[:, 1, :], m.after[:], m.gt[:], start=True, stop=True).then_inc(s["rem_done"], 1)
                pe.matmul(m.ps[:, 2, :], m.tot_ones[:], m.gt[:], start=True, stop=True).then_inc(s["tot_done"], 1)
                pe.wait_ge(s["parts_ready"], 1)
                pe.wait_ge(s["dve"], 5)
                for q in range(4):
                    if q >= 2:
                        pe.wait_ge(s["T_free"], q - 1)
                    for i in range(4):
                        pair = m.bc4[:, 2 * (4 * q + i):2 * (4 * q + i) + 2, :].rearrange("p t k -> p (t k)")
                        mm = pe.transpose(m.ps[:, 4 + q % 2, i * P:(i + 1) * P], pair.bitcast(F32), m.ident[:])
                    mm.then_inc(s["T_done"], 1)

            @block.scalar
            def _(act):
                a1, a2, a3 = big[:, 0:NC], big[:, NC:2 * NC], big[:, 2 * NC:3 * NC]
                act.wait_ge(s["dve"], 1)
                act.activation(a2, a1, ACT.Exp).then_inc(s["e_ready"], 1)
                act.wait_ge(s["e_ready"], 1)
                act.activation(a3, a2, ACT.Ln, bias=1.0).then_inc(s["l_ready"], 1)
                act.wait_ge(s["bc_done"], 1)
                act.wait_ge(s["parts_ready"], 1)
                act.activation(m.e_in[:], m.ps[:, 0, :], ACT.Exp).then_inc(s["exps"], 1)
                act.wait_ge(s["rem_done"], 1)
                act.activation(m.e_out[:], m.ps[:, 1, :], ACT.Exp).then_inc(s["exps"], 1)
                act.wait_ge(s["dve"], 7)
                act.activation(m.decay_tile_e[:], m.decay_tile[:], ACT.Exp).then_inc(s["exps"], 1)


TABLES = ["ident", "rope_cos", "rope_sin", "window", "future", "upto", "after", "before",
          "row_head", "same_head", "arg_rows", "arg_head", "swap_rows"]


def tables():
    i, j = np.arange(P)[:, None], np.arange(P)[None, :]
    f = np.float32
    inv = (f(1.0) / f(150000.0) ** (np.arange(0, DH, 2, dtype=f) / f(DH))).astype(f)
    freqs = (np.arange(T, dtype=f) / f(32.0))[None, :] * inv[:, None]
    rep = (np.arange(P) % DH) // 2
    sign = np.where(np.arange(P) % 2 == 0, f(-1), f(1))[:, None]
    rows = np.arange(P) % 64
    return {
        "ident": np.eye(P, dtype=f),
        "rope_cos": np.cos(freqs).astype(f)[rep],
        "rope_sin": (np.sin(freqs).astype(f)[rep] * sign).astype(f),
        "window": np.concatenate([np.where(j >= i, 0, NEG), np.where(j <= i, 0, NEG)], 1).astype(f),
        "future": np.where(j < i, NEG_R, 0).astype(f),
        "upto": (i <= j).astype(f),
        "after": (i > j).astype(f),
        "before": (i < j).astype(f),
        "row_head": (i // DR == np.arange(HR)[None, :]).astype(f),
        "same_head": (i // DR == j // DR).astype(f),
        "arg_rows": np.stack([rows >= 32, rows < 32, rows < 32, rows >= 32], 1).astype(f),
        "arg_head": (np.arange(P)[:, None] % HR == np.arange(HR)[None, :]).astype(f),
        "swap_rows": (i == (j ^ 1)).astype(f),
    }


def attention(nc, m):
    U = TB * KV
    names = ("hs_ready qk_done rope_a rope_b rope_pool rope_dve v_done v_ready S_done mx_ready neg_ready masked exp_done "
             "sinkexp PT_a PT_b PTs_a PTs_b PV_done den_ready rinv_ready normed "
             "YT_a YT_b yTs_a yTs_b proj_done tx_ready x2_ready x2_sq ms_ready r3_ready h2_ready h2T_done h2Ts_ready gate_done gate_ready kept")
    with nc.Fori(0, B) as b:
        with semaphores(nc, names) as s:
            S = [m.ps[:, 2 * i:2 * i + 2, :].rearrange("p k n -> p (k n)").rearrange("p (j w) -> p j w", j=HG) for i in range(2)]
            with nc.Block() as block:
                @block.tensor
                def _(pe):
                    pe.wait_ge(s["hs_ready"], 1)
                    for n in range(NCH):
                        if n >= 2:
                            pe.wait_ge(s["rope_a"], n - 1)
                            pe.wait_ge(s["rope_b"], n - 1)
                        pe.matmul(m.ps[:, 2 * (n % 2), :], m.wqk[:, n, :], m.hTs[:], start=True, stop=True)
                        pe.matmul(m.ps[:, 2 * (n % 2) + 1, :], m.wqk_swap[:, n, :], m.hTs[:], start=True, stop=True).then_inc(s["qk_done"], 1)
                    for t in range(TB):
                        pe.matmul(m.ps[:, 4 + t // 2, 256 * (t % 2):256 * (t % 2) + 256], m.hTs[:, t * P:(t + 1) * P], m.wv[:],
                                  start=True, stop=True).then_inc(s["v_done"], 1)

                    def scores(u):
                        qt, g = divmod(u, KV)
                        if u == 0:
                            pe.wait_ge(s["rope_pool"], NCH // 2)
                            pe.wait_ge(s["rope_dve"], NCH // 2)
                            pe.wait_ge(s["rope_b"], NCH)
                        if u >= 2:
                            pe.wait_ge(s["mx_ready"], HG * (u - 1))
                        for j in range(HG):
                            ch, row = head_place(g, j)
                            w0 = P if qt == 0 else 0
                            keys = m.qk[row:row + DH, NQ + g // 2, (qt - 1) * P + w0:(qt + 1) * P]
                            mm = pe.matmul(S[u % 2][:, j, w0:2 * P], m.qk[row:row + DH, ch, qt * P:(qt + 1) * P], keys,
                                           start=True, stop=True)
                        mm.then_inc(s["S_done"], 1)

                    def transposes(u):
                        qt = u // KV
                        pe.wait_ge(s["exp_done"], HG * (u + 1))
                        if u == 0:
                            pe.wait_ge(s["v_ready"], TB)
                        for j in range(HG):
                            bank, done, read = ((4, "PT_a", "PTs_a"), (5, "PT_b", "PTs_b"))[j // 2]
                            if j % 2 == 0 and u >= 1:
                                pe.wait_ge(s[read], u)
                            for kt in range(1 if qt == 0 else 0, 2):
                                c = 256 * (j % 2) + P * kt
                                mm = pe.transpose(m.ps[:, bank, c:c + P], m.prob[:, u % 2, j, kt * P:(kt + 1) * P], m.ident[:])
                            if j % 2 == 1:
                                mm.then_inc(s[done], 1)

                    def values(u):
                        qt, g = divmod(u, KV)
                        pe.wait_ge(s["PTs_a"], u + 1)
                        pe.wait_ge(s["PTs_b"], u + 1)
                        if u >= 1:
                            pe.wait_ge(s["normed"], u)
                        q = (u - 6) // 4
                        if q >= 0 and (u - 6) % 4 == 0:
                            pe.wait_ge(s["x2_ready"], q + 1)
                        first = 1 if qt == 0 else 0
                        for j in range(HG):
                            for kt in range(first, 2):
                                mm = pe.matmul(m.ps[:, 6, j * DH:(j + 1) * DH], m.probT[:, u % 2, j, kt, :],
                                               m.v[:, qt - 1 + kt, g * DH:(g + 1) * DH], start=(kt == first), stop=(kt == 1))
                        mm.then_inc(s["PV_done"], 1)

                    def y_transposes(q):
                        pe.wait_ge(s["normed"], 4 * q + 4)
                        for r in range(2):
                            if r == 1:
                                pe.wait_ge(s["yTs_a"], q + 1)
                            elif q >= 1:
                                pe.wait_ge(s["gate_ready"], q)
                            for c in range(4):
                                mm = pe.transpose(m.ps[:, 7, c * P:(c + 1) * P], m.y[:, q % 2, (4 * r + c) * P:(4 * r + c + 1) * P], m.ident[:])
                            mm.then_inc(s[("YT_a", "YT_b")[r]], 1)

                    def project(q):
                        pe.wait_ge(s["yTs_a"], q + 1)
                        pe.wait_ge(s["yTs_b"], q + 1)
                        pe.wait_ge(s["normed"], min(4 * q + 6, U))
                        for c in range(8):
                            mm = pe.matmul(m.ps[:, 6, 256:256 + D], m.yT[:, c, :], m.projw[:, c, :], start=(c == 0), stop=(c == 7))
                        mm.then_inc(s["proj_done"], 1)

                    scores(0)
                    scores(1)
                    for st in range(U + 6):
                        if st < U:
                            transposes(st)
                        if 1 <= st <= U:
                            values(st - 1)
                        if st + 2 < U:
                            scores(st + 2)
                        q, k = divmod(st - 5, 4)
                        if 0 <= q < TB and k == 1:
                            project(q)
                        if 0 <= q < TB and k == 3:
                            pe.wait_ge(s["h2_ready"], q + 1)
                            pe.transpose(m.ps[:, 7, 0:P], m.h2s[:], m.ident[:]).then_inc(s["h2T_done"], 1)
                        if 1 <= q <= TB and k == 0:
                            pe.wait_ge(s["h2Ts_ready"], q)
                            pe.matmul(m.ps[:, 7, P:P + E], m.h2Ts[:], m.gatew[:], start=True, stop=True).then_inc(s["gate_done"], 1)
                        if 0 <= q < TB and k == 0:
                            y_transposes(q)

                @block.vector
                def _(dve):
                    for n in range(NCH):
                        a, c = m.ps[:, 2 * (n % 2), :], m.ps[:, 2 * (n % 2) + 1, :]
                        dve.wait_ge(s["qk_done"], n + 1)
                        if n >= 2:
                            dve.wait_ge(s[("rope_pool", "rope_dve")[n % 2]], n // 2)
                        nc.vector.scalar_tensor_tensor(out=m.rope_t[:, n % 2, :], in0=a, scalar=m.qkb[:, n:n + 1], in1=m.rope_cos[:],
                                                       op0=ALU.add, op1=ALU.mult).then_inc(s["rope_a"], 1)
                        nc.vector.scalar_tensor_tensor(out=m.qk[:, n, :], in0=c, scalar=m.qkb_swap[:, n:n + 1], in1=m.rope_sin[:],
                                                       op0=ALU.add, op1=ALU.mult).then_inc(s["rope_b"], 1)
                        if n % 2 == 1:
                            dve.wait_ge(s["rope_b"], n + 1)
                            nc.vector.tensor_tensor(m.qk[:, n, :], m.qk[:, n, :], m.rope_t[:, n % 2, :], ALU.add).then_inc(s["rope_dve"], 1)
                    for t in range(0, TB, 2):
                        dve.wait_ge(s["v_done"], t + 2)
                        for i in range(2):
                            nc.vector.tensor_tensor(m.v[:, t + i, :], m.ps[:, 4 + t // 2, 256 * i:256 * i + 256], m.vb[:], ALU.add).then_inc(s["v_ready"], 1)

                    def mask(u):
                        qt, g = divmod(u, KV)
                        w0 = P if qt == 0 else 0
                        dve.wait_ge(s["S_done"], u + 1)
                        if u >= 2:
                            dve.wait_ge(s["exp_done"], HG * (u - 1))
                            dve.wait_ge(s["sinkexp"], u - 1)
                        for j in range(HG):
                            h = g * HG + j
                            nc.vector.tensor_tensor_reduce(out=m.sm[:, u % 2, j, w0:2 * P], in0=S[u % 2][:, j, w0:2 * P],
                                                           in1=m.window[:, w0:2 * P], scale=1.0, scalar=m.sink8[:, h:h + 1],
                                                           op0=ALU.add, op1=ALU.max, accum_out=m.mx[:, u % 2, j:j + 1]).then_inc(s["mx_ready"], 1)
                        dve.wait_ge(s["mx_ready"], HG * (u + 1))
                        nc.vector.tensor_scalar(m.negmx[:, u % 2, :], m.mx[:, u % 2, :], -(float(DH) ** -0.5), None, ALU.mult).then_inc(s["neg_ready"], 1)
                        dve.wait_ge(s["neg_ready"], u + 1)
                        nc.vector.tensor_tensor(m.sinkm[:, u % 2, :], m.sink[:, g * HG:(g + 1) * HG], m.negmx[:, u % 2, :], ALU.add).then_inc(s["masked"], 1)

                    def norm(u):
                        qt, g = divmod(u, KV)
                        dve.wait_ge(s["exp_done"], HG * (u + 1))
                        dve.wait_ge(s["sinkexp"], u + 1)
                        nc.vector.tensor_tensor(m.den[:, u % 2, :], m.rowsum[:, u % 2, :], m.esink[:, u % 2, :], ALU.add).then_inc(s["den_ready"], 1)
                        dve.wait_ge(s["den_ready"], u + 1)
                        nc.vector.reciprocal(m.rden[:, u % 2, :], m.den[:, u % 2, :]).then_inc(s["rinv_ready"], 1)
                        dve.wait_ge(s["rinv_ready"], u + 1)
                        dve.wait_ge(s["PV_done"], u + 1)
                        if qt >= 2 and g == 0:
                            dve.wait_ge(s["YT_b"], qt - 1)
                        nc.vector.tensor_tensor(m.y[:, qt % 2, g * 256:(g + 1) * 256].rearrange("p (j d) -> p j d", j=HG),
                                                m.ps[:, 6, 0:256].rearrange("p (j d) -> p j d", j=HG),
                                                bc(m.rden[:, u % 2, :, None], [P, HG, DH]), ALU.mult).then_inc(s["normed"], 1)

                    mask(0)
                    for st in range(U + 6):
                        q, k = divmod(st - 5, 4)
                        if st + 1 < U:
                            mask(st + 1)
                        if 0 <= q < TB and k == 2:
                            dve.wait_ge(s["tx_ready"], q + 1)
                            dve.wait_ge(s["proj_done"], q + 1)
                            if q >= 1:
                                dve.wait_ge(s["kept"], 2 * q)
                            nc.vector.tensor_tensor(m.x2[:], m.ps[:, 6, 256:256 + D], m.tx[:], ALU.add).then_inc(s["x2_ready"], 1)
                        if st < U:
                            dve.wait_ge(s["PT_b"], st + 1)
                            if st >= 2:
                                dve.wait_ge(s["PV_done"], st - 1)
                            w0 = 1 if st < KV else 0
                            nc.vector.tensor_copy(m.probT[:, st % 2, 2:4, w0:2, :],
                                                  m.ps[:, 5, :].rearrange("p (j k i) -> p j k i", j=2, k=2)[:, :, w0:2, :]).then_inc(s["PTs_b"], 1)
                        if 1 <= st <= U:
                            norm(st - 1)
                        if 0 <= q < TB and k == 3:
                            dve.wait_ge(s["r3_ready"], q + 1)
                            if q >= 1:
                                dve.wait_ge(s["h2T_done"], q)
                            nc.vector.tensor_scalar(m.h2s[:], m.x2[:], m.r3[:, q:q + 1], None, ALU.mult).then_inc(s["h2_ready"], 1)
                        if 1 <= q <= TB and k == 0:
                            dve.wait_ge(s["gate_done"], q)
                            nc.vector.tensor_tensor(m.logit[:, bass.ds((b * TB + q - 1) * E, E)], m.ps[:, 7, P:P + E], m.gateb[:], ALU.add).then_inc(s["gate_ready"], 1)
                        if 0 <= q < TB and k == 0:
                            dve.wait_ge(s["YT_b"], q + 1)
                            if q >= 1:
                                dve.wait_ge(s["proj_done"], q)
                            nc.vector.tensor_copy(m.yT[:, 4:8, :], m.ps[:, 7, :].rearrange("p (c i) -> p c i", c=4)).then_inc(s["yTs_b"], 1)

                @block.scalar
                def _(act):
                    act.copy(m.hTs[:], m.hT[:, bass.ds(b * T, T)]).then_inc(s["hs_ready"], 1)

                    def exps(u):
                        qt, g = divmod(u, KV)
                        w0 = P if qt == 0 else 0
                        act.wait_ge(s["masked"], u + 1)
                        if u >= 2:
                            act.wait_ge(s["PT_b"], u - 1)
                            act.wait_ge(s["den_ready"], u - 1)
                        for j in range(HG):
                            nc.scalar.activation(m.prob[:, u % 2, j, w0:2 * P], m.sm[:, u % 2, j, w0:2 * P], ACT.Exp,
                                                 bias=m.negmx[:, u % 2, j:j + 1], scale=float(DH) ** -0.5,
                                                 accum_out=m.rowsum[:, u % 2, j:j + 1]).then_inc(s["exp_done"], 1)
                        nc.scalar.activation(m.esink[:, u % 2, :], m.sinkm[:, u % 2, :], ACT.Exp).then_inc(s["sinkexp"], 1)

                    exps(0)
                    for st in range(U + 6):
                        q, k = divmod(st - 5, 4)
                        if st < U:
                            act.wait_ge(s["PT_a"], st + 1)
                            if st >= 2:
                                act.wait_ge(s["PV_done"], st - 1)
                            w0 = 1 if st < KV else 0
                            nc.scalar.copy(m.probT[:, st % 2, 0:2, w0:2, :],
                                           m.ps[:, 4, :].rearrange("p (j k i) -> p j k i", j=2, k=2)[:, :, w0:2, :]).then_inc(s["PTs_a"], 1)
                        if st + 1 < U:
                            exps(st + 1)
                        if 0 <= q < TB and k == 2:
                            act.wait_ge(s["x2_ready"], q + 1)
                            if q >= 1:
                                act.wait_ge(s["x2_sq"], q)
                            nc.scalar.activation(m.sq[:, 0:D], m.x2[:], ACT.Square, accum_out=m.ssq[:, q:q + 1]).then_inc(s["x2_sq"], 1)
                        if 1 <= q <= TB and k == 0:
                            act.wait_ge(s["h2T_done"], q)
                            if q >= 2:
                                act.wait_ge(s["gate_done"], q - 1)
                            nc.scalar.copy(m.h2Ts[:], m.ps[:, 7, 0:P]).then_inc(s["h2Ts_ready"], 1)
                        if 0 <= q < TB and k == 0:
                            act.wait_ge(s["YT_a"], q + 1)
                            if q >= 1:
                                act.wait_ge(s["proj_done"], q)
                            nc.scalar.copy(m.yT[:, 0:4, :], m.ps[:, 7, :].rearrange("p (c i) -> p c i", c=4)).then_inc(s["yTs_a"], 1)

                @block.gpsimd
                def _(pool):
                    for n in range(0, NCH, 2):
                        pool.wait_ge(s["rope_a"], n + 1)
                        pool.wait_ge(s["rope_b"], n + 1)
                        nc.gpsimd.tensor_tensor(m.qk[:, n, :], m.qk[:, n, :], m.rope_t[:, n % 2, :], ALU.add).then_inc(s["rope_pool"], 1)
                    for q in range(TB):
                        tile = bass.ds(b * TB + q, 1)
                        if q >= 1:
                            pool.wait_ge(s["x2_ready"], q)
                        nc.gpsimd.tensor_tensor(m.tx[:], m.xn[:, tile, :].rearrange("p a d -> p (a d)"), m.projb[:], ALU.add).then_inc(s["tx_ready"], 1)
                        pool.wait_ge(s["x2_sq"], q + 1)
                        nc.gpsimd.tensor_scalar(m.ms3[:, q:q + 1], m.ssq[:, q:q + 1], 1.0 / D, RMS_EPS_F, ALU.mult, ALU.add).then_inc(s["ms_ready"], 1)
                        pool.wait_ge(s["ms_ready"], q + 1)
                        nc.gpsimd.tensor_tensor(m.r3[:, q:q + 1], m.ms3[:, q:q + 1], m.minus_half[:, 0:1], ALU.pow).then_inc(s["r3_ready"], 1)
                        a = m.acc[:, tile, :].rearrange("p a d -> p (a d)")
                        nc.gpsimd.tensor_tensor(a, a, m.x2[:], ALU.add).then_inc(s["kept"], 1)
                        pool.wait_ge(s["h2_ready"], q + 1)
                        nc.gpsimd.tensor_copy(m.h2[:, tile, :].rearrange("p a d -> p (a d)"), m.h2s[:]).then_inc(s["kept"], 1)


def routing(nc, m):
    TE = NT * E
    with semaphores(nc, "top own before_done count_done mask_ready exp_ready neg_ready pool") as s:
        onehot = [m.big[:, k * TE:(k + 1) * TE] for k in range(TOPK)]
        def t3(ap):
            return ap.rearrange("p (t e) -> p t e", e=E)
        with nc.Block() as block:
            @block.vector
            def _(dve):
                own = Steps(dve, s["own"])
                for t in range(NT):
                    own(nc.vector.max(m.top8[:, t, :], m.logit[:, t * E:(t + 1) * E]))
                for t in range(NT):
                    own.wait(t + 1)
                    own(nc.vector.max_index(m.idx8[:, t, :], m.top8[:, t, :], m.logit[:, t * E:(t + 1) * E]))
                own.wait()
                own(nc.vector.tensor_copy(m.idxf[:], m.idx8[:, :, 0:TOPK]))
                own.wait()
                for k in range(TOPK):
                    own(nc.vector.tensor_tensor(t3(onehot[k]), bc(m.idxf[:, :, k:k + 1], [P, NT, E]),
                                                bc(m.iota_e[:, None, :], [P, NT, E]), ALU.is_equal))
                own.wait()
                a, c = m.big[:, 4 * TE:5 * TE], m.big[:, 5 * TE:6 * TE]
                own(nc.vector.tensor_tensor(a, onehot[0], onehot[1], ALU.add))
                own(nc.vector.tensor_tensor(c, onehot[2], onehot[3], ALU.add))
                own.wait()
                nc.vector.tensor_tensor(m.chosen_bf[:], a, c, ALU.add).then_inc(s["mask_ready"], 1)
                own(nc.vector.tensor_tensor(m.gatew4[:], m.top8[:, :, 0:TOPK], bc(m.top8[:, :, 0:1], [P, NT, TOPK]), ALU.subtract))
                dve.wait_ge(s["exp_ready"], 1)
                own(nc.vector.tensor_reduce(m.gsum[:], m.gexp[:], AXX, ALU.add))
                own.wait()
                own(nc.vector.reciprocal(m.grec[:], m.gsum[:]))
                own.wait()
                own(nc.vector.tensor_tensor(m.gatew4[:], m.gexp[:], bc(m.grec[:, :, None], [P, NT, TOPK]), ALU.mult))
                dve.wait_ge(s["before_done"], 2)
                dve.wait_ge(s["count_done"], 2)
                own(nc.vector.tensor_copy(c, m.ps[:, 2:4, :].rearrange("p k n -> p (k n)")))
                own(nc.vector.memset(m.carry[:, 0:E], 0.0))
                for t in range(1, NT + 1):
                    own.wait()
                    own(nc.vector.tensor_tensor(m.carry[:, t * E:(t + 1) * E], m.carry[:, (t - 1) * E:t * E], c[:, (t - 1) * E:t * E], ALU.add))
                own.wait()
                n_e = m.carry[:, TE:TE + E]
                own(nc.vector.tensor_tensor(t3(a), bc(n_e[:, :, None], [P, E, NT]), bc(m.iota_blk[:, None, 0:NT], [P, E, NT]), ALU.is_gt))
                own.wait()
                own(nc.vector.tensor_reduce(m.nblk[:], t3(a), AXX, ALU.add))
                own.wait()
                own(nc.vector.tensor_tensor(t3(a), bc(m.nblk[:, None, :], [P, E, E]), m.upto_e[:], ALU.mult))
                own.wait()
                own(nc.vector.tensor_reduce(m.cumblk[:], t3(a), AXX, ALU.add))
                own.wait()
                own(nc.vector.tensor_tensor(m.base[:], m.cumblk[:], m.nblk[:], ALU.subtract))
                own.wait()
                own(nc.vector.tensor_scalar(m.base[:], m.base[:], float(P), None, ALU.mult))
                own(nc.vector.tensor_tensor(c, m.ps[:, 0:2, :].rearrange("p k n -> p (k n)"), m.carry[:, 0:TE], ALU.add))
                own.wait()
                own(nc.vector.tensor_tensor(t3(c), t3(c), bc(m.base[:, None, :], [P, NT, E]), ALU.add))
                own.wait()
                for k in range(TOPK):
                    own(nc.vector.tensor_tensor(onehot[k], onehot[k], c, ALU.mult))
                    own.wait()
                    own(nc.vector.tensor_reduce(m.slotf[:, :, k], t3(onehot[k]), AXX, ALU.add))
                own.wait()
                own(nc.vector.tensor_copy(m.slot[:], m.slotf[:]))
                for half in range(4):
                    n = NBLK // 4
                    v = m.big[:, 0:n * E].rearrange("p (j e) -> p j e", e=E)
                    own.wait()
                    own(nc.vector.tensor_tensor(v, bc(m.cumblk[:, None, :], [P, n, E]), bc(m.iota_j[:, half * n:(half + 1) * n, None], [P, n, E]), ALU.is_le))
                    own.wait()
                    own(nc.vector.tensor_reduce(m.blkf[:, half * n:(half + 1) * n], v, AXX, ALU.add))
                own.wait()
                own(nc.vector.tensor_scalar(m.blk[:], m.blkf[:], float(E - 1), None, ALU.min))
                own.wait()

            @block.tensor
            def _(pe):
                pe.wait_ge(s["mask_ready"], 1)
                for i in range(2):
                    pe.matmul(m.ps[:, i, :], m.before_bf[:], m.chosen_bf[:, 512 * i:512 * i + 512], start=True, stop=True).then_inc(s["before_done"], 1)
                for i in range(2):
                    pe.matmul(m.ps[:, 2 + i, :], m.ones_bf[:], m.chosen_bf[:, 512 * i:512 * i + 512], start=True, stop=True).then_inc(s["count_done"], 1)

            @block.scalar
            def _(act):
                act.wait_ge(s["own"], 2 * NT + 8)
                nc.scalar.activation(m.gexp[:], m.gatew4[:], ACT.Exp).then_inc(s["exp_ready"], 1)
                act.wait_ge(s["exp_ready"], 1)


def retention(nc, m, a):
    names = ("in_ready proj sq_done eg_done ms_ready r_ready own q4_ready k4_ready qd_ready kd_ready v_ready g_ready TQ_done TK_done TD_done "
             "TQ_ev TK_ev TD_ev arg_done A_done D_ready At_ready o_done kv_done S_ready osq_done ms16_ready r16_ready "
             "o_read og_ready TG_done TG_ev wo_done out_done rows_ready rhs_ready kv_read")
    with nc.semaphore("scattered") as scattered, nc.Fori(0, B) as b:
        with semaphores(nc, names) as s:
            BANK = [(4, 5), (2, 3)]
            with nc.Block() as block:
                @block.tensor
                def _(pe):
                    def proj(t):
                        if t == 0:
                            pe.wait_ge(s["in_ready"], 1)
                        if t >= 2:
                            pe.wait_ge(s["g_ready"], t - 1)
                            pe.wait_ge(s["v_ready"], t - 1)
                            pe.wait_ge(s["eg_done"], t - 1)
                        pe.matmul(m.ps[:, t % 2, :], m.xTs[:, t * P:(t + 1) * P], m.wr[:], start=True, stop=True).then_inc(s["proj"], 1)

                    def turn(t):
                        pe.wait_ge(s["q4_ready"], t + 1)
                        if t >= 1:
                            pe.wait_ge(s["D_ready"], 4 * t)
                            pe.wait_ge(s["At_ready"], 4 * t)
                        for c in range(4):
                            mm = pe.transpose(m.ps[:, 2, c * P:(c + 1) * P], m.q4[:, c * P:(c + 1) * P].bitcast(F32), m.ident[:])
                        mm.then_inc(s["TQ_done"], 1)
                        pe.wait_ge(s["k4_ready"], t + 1)
                        for c in range(4):
                            mm = pe.transpose(m.ps[:, 3, c * P:(c + 1) * P], m.k4[:, c * P:(c + 1) * P].bitcast(F32), m.ident[:])
                        mm.then_inc(s["TK_done"], 1)
                        pe.wait_ge(s["qd_ready"], t + 1)
                        if t >= 1:
                            pe.wait_ge(s["kv_read"], t)
                        pe.transpose(m.ps[:, 7, 0:P], m.qd[:], m.ident[:]).then_inc(s["TD_done"], 1)

                    def scores(t, hg):
                        u = 4 * t + hg
                        ba, bs = BANK[hg % 2]
                        if hg % 2 == 1 and hg == 1:
                            pe.wait_ge(s["TQ_ev"], t + 1)
                        if u >= 2:
                            pe.wait_ge(s["D_ready"], u - 1)
                        row = 64 * (t % 2)
                        if hg == 0 and t % 2 == 0:
                            pe.wait_ge(s["rhs_ready"], t // 2 + 1)
                        pe.matmul(m.ps[:, ba, :], m.ident_bf[:], m.future_bf[:].rearrange("p j i -> p (j i)"), start=True, stop=False)
                        pe.matmul(m.ps[:, ba, :], m.argLs[row:row + 64, t // 2, :],
                                  m.argRx[row:row + 64, t // 2, hg:HR:4, :],
                                  start=False, stop=True).then_inc(s["arg_done"], 1)
                        if hg == 0:
                            pe.wait_ge(s["TQ_ev"], t + 1)
                            pe.wait_ge(s["TK_ev"], t + 1)
                        if u >= 2:
                            pe.wait_ge(s["At_ready"], u - 1)
                        rows = slice(32 * hg, 32 * hg + 32)
                        for c in range(4):
                            mm = pe.matmul(m.ps[:, bs, c * P:(c + 1) * P], m.k4T[rows, c, :], m.q4T[rows, c, :], start=True, stop=True)
                        mm.then_inc(s["A_done"], 1)

                    def out_cross(t):
                        pe.wait_ge(s["TD_ev"], t + 1)
                        pe.wait_ge(s["S_ready"], t + 1)
                        if t >= 1:
                            pe.wait_ge(s["o_read"], t)
                        pe.matmul(m.ps[:, 6, 0:P], m.qdT[:], m.state[:], start=True, stop=False, skip_group_check=True)

                    def out_intra(t, hg):
                        pe.wait_ge(s["At_ready"], 4 * t + hg + 1)
                        for c in range(4):
                            h = 4 * c + hg
                            mm = pe.matmul(m.ps[:, 6, h * DR:(h + 1) * DR], m.At[:, hg % 2, c, :], m.vn[:, h * DR:(h + 1) * DR],
                                           start=False, stop=(h == HR - 1), skip_group_check=True)
                        mm.then_inc(s["o_done"], 1)

                    def update(t):
                        pe.wait_ge(s["kd_ready"], t + 1)
                        pe.matmul(m.ps[:, 7, P:2 * P], m.kd[:], m.vn[:], start=True, stop=True).then_inc(s["kv_done"], 1)

                    def finish(t):
                        pe.wait_ge(s["og_ready"], t + 1)
                        pe.transpose(m.ps[:, 7, 2 * P:3 * P], m.og[:], m.ident[:]).then_inc(s["TG_done"], 1)
                        pe.wait_ge(s["TG_ev"], t + 1)
                        pe.matmul(m.ps[:, 7, 3 * P:4 * P], m.ogT[:], m.wo[:], start=True, stop=True).then_inc(s["wo_done"], 1)

                    proj(0)
                    for t in range(TB):
                        if t + 1 < TB:
                            proj(t + 1)
                        turn(t)
                        scores(t, 0)
                        scores(t, 1)
                        out_cross(t)
                        update(t)
                        out_intra(t, 0)
                        scores(t, 2)
                        out_intra(t, 1)
                        scores(t, 3)
                        out_intra(t, 2)
                        out_intra(t, 3)
                        pe.wait_ge(s["kv_read"], t + 1)
                        finish(t)
                        pe.wait_ge(s["out_done"], t + 1)

                @block.vector
                def _(dve):
                    own = Steps(dve, s["own"])
                    own(nc.vector.memset(m.state[:], 0.0))
                    own(nc.vector.tensor_copy(m.e_in_s[:], m.e_in[:, bass.ds(b * TB * HR, TB * HR)]))
                    own(nc.vector.tensor_copy(m.e_out_s[:], m.e_out[:, bass.ds(b * TB * HR, TB * HR)]))
                    own(nc.vector.tensor_copy(m.decay_s[:], m.decay_tile_e[:, bass.ds(b * TB, TB)]))
                    own(nc.vector.tensor_copy(m.argLs[:], m.argL[:, bass.ds(2 * b, 2), :].bitcast(F32)))
                    own.wait()
                    own_state = Steps(dve, s["S_ready"])
                    own_state(nc.vector.tensor_scalar(m.state[:], m.state[:], 0.0, None, ALU.add))
                    for p in range(2):
                        nc.vector.tensor_tensor(m.argRx[:, p, :, :], bc(m.argR[:, bass.ds(2 * b + p, 1), :].bitcast(F32), [P, HR, P]),
                                                bc(m.arg_head[:, :, None], [P, HR, P]), ALU.mult).then_inc(s["rhs_ready"], 1)

                    def heads(ap):
                        return ap.rearrange("p (h d) -> p h d", d=DR)

                    for t in range(TB):
                        ps = m.ps[:, t % 2, :]
                        dve.wait_ge(s["sq_done"], 3 * (t + 1))
                        dve.wait_ge(s["eg_done"], t + 1)
                        nc.vector.tensor_scalar(m.ms3[:, 0:3], m.ssq[:, 0:3], 1.0 / D, RMS_EPS_R, ALU.mult, ALU.add).then_inc(s["ms_ready"], 1)
                        n_gate = own(nc.vector.tensor_scalar(m.sg1[:], m.eg[:], 1.0, None, ALU.add))
                        own.wait(n_gate)
                        n_gate = own(nc.vector.reciprocal(m.sg2[:], m.sg1[:]))
                        own.wait(n_gate)
                        nc.vector.tensor_tensor(m.sg[:], ps[:, 384:512], m.sg2[:], ALU.mult).then_inc(s["g_ready"], 1)
                        dve.wait_ge(s["r_ready"], t + 1)
                        if t >= 1:
                            dve.wait_ge(s["TD_done"], t)
                            dve.wait_ge(s["kv_done"], t)
                            dve.wait_ge(s["o_done"], 4 * t)
                        own(nc.vector.tensor_scalar(m.qn[:], ps[:, 0:128], m.rr[:, 0:1], float(DR) ** -0.5, ALU.mult, ALU.mult))
                        own(nc.vector.tensor_scalar(m.kn[:], ps[:, 128:256], m.rr[:, 1:2], None, ALU.mult))
                        nc.vector.tensor_scalar(m.vn[:], ps[:, 256:384], m.rr[:, 2:3], None, ALU.mult).then_inc(s["v_ready"], 1)
                        own.wait()
                        q4 = m.q4[:].rearrange("p (h r d) -> p h r d", r=4, d=DR)
                        k4 = m.k4[:].rearrange("p (h r d) -> p h r d", r=4, d=DR)
                        own(nc.vector.tensor_copy(q4[:, :, 0, :], heads(m.qn[:])))
                        own(nc.vector.tensor_copy(q4[:, :, 2, :], heads(m.qn[:])))
                        own(nc.vector.tensor_copy(k4[:, :, 0, :], heads(m.kn[:])))
                        own(nc.vector.tensor_copy(k4[:, :, 1, :], heads(m.kn[:])))
                        own.wait(own.n - 2)
                        own(nc.vector.tensor_tensor(q4[:, :, 1, :], heads(m.qn[:]), q4[:, :, 0, :].bitcast(F32), ALU.subtract))
                        nc.vector.tensor_tensor(q4[:, :, 3, :], heads(m.qn[:]), q4[:, :, 0, :].bitcast(F32), ALU.subtract).then_inc(s["q4_ready"], 1)
                        own.wait(own.n - 1)
                        own(nc.vector.tensor_tensor(k4[:, :, 2, :], heads(m.kn[:]), k4[:, :, 0, :].bitcast(F32), ALU.subtract))
                        nc.vector.tensor_tensor(k4[:, :, 3, :], heads(m.kn[:]), k4[:, :, 0, :].bitcast(F32), ALU.subtract).then_inc(s["k4_ready"], 1)
                        nc.vector.tensor_tensor(heads(m.qd[:]), heads(m.qn[:]), bc(m.e_in_s[:, t * HR:(t + 1) * HR, None], [P, HR, DR]), ALU.mult).then_inc(s["qd_ready"], 1)
                        nc.vector.tensor_tensor(heads(m.kd[:]), heads(m.kn[:]), bc(m.e_out_s[:, t * HR:(t + 1) * HR, None], [P, HR, DR]), ALU.mult).then_inc(s["kd_ready"], 1)
                        dve.wait_ge(s["TK_done"], t + 1)
                        if t >= 1:
                            dve.wait_ge(s["A_done"], 4 * t)
                        nc.vector.tensor_copy(m.k4T[:].rearrange("p c i -> p (c i)"), m.ps[:, 3, :]).then_inc(s["TK_ev"], 1)
                        for hg in range(4):
                            u = 4 * t + hg
                            dve.wait_ge(s["A_done"], u + 1)
                            dve.wait_ge(s["D_ready"], u + 1)
                            if u >= 2:
                                dve.wait_ge(s["o_done"], u - 1)
                            nc.vector.tensor_tensor(m.At[:, hg % 2, :, :].rearrange("p j i -> p (j i)"), m.ps[:, BANK[hg % 2][1], :],
                                                    m.Dm[:, hg % 2, :], ALU.mult).then_inc(s["At_ready"], 1)
                            if hg == 1:
                                dve.wait_ge(s["kv_done"], t + 1)
                                if t >= 1:
                                    dve.wait_ge(s["S_ready"], t + 1)
                                nc.vector.tensor_tensor(m.kvm[:], m.ps[:, 7, P:2 * P], m.same_head[:], ALU.mult).then_inc(s["kv_read"], 1)
                                dve.wait_ge(s["kv_read"], t + 1)
                                nc.vector.scalar_tensor_tensor(out=m.state[:], in0=m.state[:], scalar=m.decay_s[:, t:t + 1], in1=m.kvm[:],
                                                               op0=ALU.mult, op1=ALU.add).then_inc(s["S_ready"], 1)
                        dve.wait_ge(s["osq_done"], t + 1)
                        own(nc.vector.tensor_reduce(m.ms16[:], heads(m.osq[:]), AXX, ALU.add))
                        own.wait()
                        nc.vector.tensor_scalar(m.ms16b[:], m.ms16[:], 1.0 / DR, RMS_EPS_R, ALU.mult, ALU.add).then_inc(s["ms16_ready"], 1)
                        dve.wait_ge(s["r16_ready"], t + 1)
                        nc.vector.tensor_tensor(heads(m.on[:]), heads(m.ps[:, 6, 0:P]), bc(m.r16[:, :, None], [P, HR, DR]), ALU.mult).then_inc(s["o_read"], 1)
                        dve.wait_ge(s["o_read"], t + 1)
                        nc.vector.tensor_tensor(m.og[:], m.on[:], m.sg[:], ALU.mult).then_inc(s["og_ready"], 1)
                        dve.wait_ge(s["wo_done"], t + 1)
                        acc = m.acc[:, bass.ds(b * TB + t, 1), :].rearrange("p a d -> p (a d)")
                        nc.vector.tensor_tensor(acc, m.ps[:, 7, 3 * P:4 * P], acc, ALU.add).then_inc(s["out_done"], 1)

                @block.scalar
                def _(act):
                    act.copy(m.xTs[:], m.xT[:, bass.ds(b * T, T)]).then_inc(s["in_ready"], 1)

                    def squares(t):
                        act.wait_ge(s["proj"], t + 1)
                        if t >= 1:
                            act.wait_ge(s["ms_ready"], t)
                            act.wait_ge(s["g_ready"], t)
                            act.wait_ge(s["sq_done"], 3 * t)
                        for i in range(3):
                            nc.scalar.activation(m.sq[:, i * P:(i + 1) * P], m.ps[:, t % 2, i * P:(i + 1) * P], ACT.Square,
                                                 accum_out=m.ssq[:, i:i + 1]).then_inc(s["sq_done"], 1)
                        nc.scalar.activation(m.eg[:], m.ps[:, t % 2, 384:512], ACT.Exp, scale=-1.0).then_inc(s["eg_done"], 1)

                    for t in range(TB):
                        squares(t)
                        act.wait_ge(s["TQ_done"], t + 1)
                        if t >= 1:
                            act.wait_ge(s["A_done"], 4 * t)
                        nc.scalar.copy(m.q4T[:].rearrange("p c i -> p (c i)"), m.ps[:, 2, :]).then_inc(s["TQ_ev"], 1)
                        act.wait_ge(s["TD_done"], t + 1)
                        if t >= 1:
                            act.wait_ge(s["o_done"], 4 * t)
                        nc.scalar.copy(m.qdT[:], m.ps[:, 7, 0:P]).then_inc(s["TD_ev"], 1)
                        for hg in range(4):
                            u = 4 * t + hg
                            act.wait_ge(s["arg_done"], u + 1)
                            if u >= 2:
                                act.wait_ge(s["At_ready"], u - 1)
                            nc.scalar.activation(m.Dm[:, hg % 2, :], m.ps[:, BANK[hg % 2][0], :], ACT.Exp).then_inc(s["D_ready"], 1)
                        act.wait_ge(s["o_done"], 4 * t + 4)
                        if t >= 1:
                            act.wait_ge(s["ms16_ready"], t)
                        nc.scalar.activation(m.osq[:], m.ps[:, 6, 0:P], ACT.Square).then_inc(s["osq_done"], 1)
                        act.wait_ge(s["TG_done"], t + 1)
                        nc.scalar.copy(m.ogT[:], m.ps[:, 7, 2 * P:3 * P]).then_inc(s["TG_ev"], 1)

                @block.gpsimd
                def _(pool):
                    nc.gpsimd.tensor_copy(m.rows[:], m.h2[:, bass.ds(b * TB, TB), :]).then_inc(s["rows_ready"], 1)
                    nc.gpsimd.tensor_copy(m.slot_s[:], m.slot[:, bass.ds(b * TB, TB), :]).then_inc(s["rows_ready"], 1)
                    pool.wait_ge(s["rows_ready"], 2)
                    for t in range(TB):
                        pool.wait_ge(s["ms_ready"], t + 1)
                        if t >= 1:
                            pool.wait_ge(s["v_ready"], t)
                        nc.gpsimd.tensor_tensor(m.rr[:, 0:3], m.ms3[:, 0:3], m.minus_half[:, 0:3], ALU.pow).then_inc(s["r_ready"], 1)
                        for k in range(TOPK):
                            pool.indirect_dma_start(a["slots_x"][:, :], bass.IndirectOffsetOnAxis(ap=m.slot_s[:, t, k:k + 1], axis=0),
                                                    m.rows[:, t, :], None).then_inc(scattered, 16)
                        pool.wait_ge(s["ms16_ready"], t + 1)
                        if t >= 1:
                            pool.wait_ge(s["o_read"], t)
                        nc.gpsimd.tensor_tensor(m.r16[:], m.ms16b[:], m.minus_half[:, 0:HR], ALU.pow).then_inc(s["r16_ready"], 1)
                    pool.wait_ge(scattered, (b + 1) * (16 * TB * TOPK))


def experts(nc, m, a):
    names = "x_loaded_0 x_loaded_1 T_done xT_ready up_done silu_done up_read a_ready TA_done aT_ready down_done y_ready y_stored_0 y_stored_1"
    Q = 4
    with nc.Fori(0, NBLK // BPI) as i:
        with semaphores(nc, names) as s:
            def dram(t, q):
                return t[bass.ds((i * (BPI // Q) + q) * (Q * P), Q * P), :].rearrange("(r p) n -> p r n", p=P)
            with nc.Block() as block:
                @block.sync
                def _(sp):
                    for q in range(BPI // Q):
                        if q >= 2:
                            sp.wait_ge(s["T_done"], Q * (q - 1))
                        sp.dma_start(m.xblk[:, q % 2, :, :], dram(a["slots_x"], q)).then_inc(s[f"x_loaded_{q % 2}"], 16)
                        if q >= 2:
                            sp.wait_ge(s["y_ready"], Q * (q - 1))
                            sp.dma_start(dram(a["slots_y"], q - 2), m.yblk[:, q % 2, :, :]).then_inc(s[f"y_stored_{q % 2}"], 16)
                    for q in range(BPI // Q - 2, BPI // Q):
                        sp.wait_ge(s["y_ready"], Q * (q + 1))
                        sp.dma_start(dram(a["slots_y"], q), m.yblk[:, q % 2, :, :]).then_inc(s[f"y_stored_{q % 2}"], 16)
                    for q in range(2):
                        sp.wait_ge(s[f"y_stored_{q}"], 16 * (BPI // Q // 2))

                @block.tensor
                def _(pe):
                    def turn(j):
                        pe.wait_ge(s[f"x_loaded_{j // Q % 2}"], 16 * (j // Q // 2 + 1))
                        if j >= 2:
                            pe.wait_ge(s["xT_ready"], j - 1)
                        pe.transpose(m.ps[:, j % 2, 0:P], m.xblk[:, (j // Q) % 2, j % Q, :], m.ident[:]).then_inc(s["T_done"], 1)

                    def up(j, e):
                        pe.wait_ge(s["xT_ready"], j + 1)
                        if j >= 2:
                            pe.wait_ge(s["a_ready"], j - 1)
                        pe.matmul(m.ps[:, 2 + j % 2, 0:2 * DFF], m.xTb[:, j % 2, :], m.wu[:, bass.ds(e, 1), :].rearrange("p a f -> p (a f)"),
                                  start=True, stop=True).then_inc(s["up_done"], 1)

                    def down(j, e):
                        pe.wait_ge(s["a_ready"], j + 1)
                        if j >= 2:
                            pe.wait_ge(s["aT_ready"], j - 1)
                        pe.transpose(m.ps[:, 4 + j % 2, 0:P], m.ab[:, j % 2, :], m.ident[:]).then_inc(s["TA_done"], 1)
                        pe.wait_ge(s["aT_ready"], j + 1)
                        if j >= 2:
                            pe.wait_ge(s["y_ready"], j - 1)
                        pe.matmul(m.ps[:, 6 + j % 2, 0:D], m.aTb[:, j % 2, :], m.wd[:, bass.ds(e, 1), :].rearrange("p a f -> p (a f)"),
                                  start=True, stop=True).then_inc(s["down_done"], 1)

                    regs = {}
                    turn(0)
                    for j in range(BPI + 1):
                        if j + 1 < BPI:
                            turn(j + 1)
                        if j < BPI:
                            regs[j] = pe.value_load(m.blk[0:1, bass.ds(i * BPI + j, 1)], min_val=0, max_val=E - 1)
                            up(j, regs[j])
                        if j >= 1:
                            down(j - 1, regs.pop(j - 1))

                @block.scalar
                def _(act):
                    for j in range(BPI):
                        act.wait_ge(s["T_done"], j + 1)
                        if j >= 2:
                            act.wait_ge(s["up_done"], j - 1)
                        nc.scalar.copy(m.xTb[:, j % 2, :], m.ps[:, j % 2, 0:P]).then_inc(s["xT_ready"], 1)
                        act.wait_ge(s["up_done"], j + 1)
                        if j >= 2:
                            act.wait_ge(s["a_ready"], j - 1)
                        nc.scalar.activation(m.sl[:, j % 2, :], m.ps[:, 2 + j % 2, DFF:2 * DFF], ACT.Silu).then_inc(s["silu_done"], 1)

                @block.vector
                def _(dve):
                    for j in range(BPI):
                        dve.wait_ge(s["silu_done"], j + 1)
                        if j >= 2:
                            dve.wait_ge(s["TA_done"], j - 1)
                        nc.vector.tensor_tensor(m.ab[:, j % 2, :], m.ps[:, 2 + j % 2, 0:DFF], m.sl[:, j % 2, :], ALU.mult).then_inc(s["a_ready"], 1)
                        dve.wait_ge(s["TA_done"], j + 1)
                        if j >= 2:
                            dve.wait_ge(s["down_done"], j - 1)
                        nc.vector.tensor_copy(m.aTb[:, j % 2, :], m.ps[:, 4 + j % 2, 0:P]).then_inc(s["aT_ready"], 1)
                        dve.wait_ge(s["down_done"], j + 1)
                        if j >= 2 * Q:
                            dve.wait_ge(s[f"y_stored_{j // Q % 2}"], 16 * (j // Q // 2))
                        nc.vector.tensor_copy(m.yblk[:, (j // Q) % 2, j % Q, :], m.ps[:, 6 + j % 2, 0:D]).then_inc(s["y_ready"], 1)


def combine(nc, m, a):
    names = "copied added stored"
    with ExitStack() as ctx:
        gathered = [ctx.enter_context(nc.semaphore(f"gathered_{t}")) for t in range(TB)]
        b = ctx.enter_context(nc.Fori(0, B))
        with semaphores(nc, names) as s, nc.Block() as block:
            @block.gpsimd
            def _(pool):
                nc.gpsimd.tensor_copy(m.slot_s[:], m.slot[:, bass.ds(b * TB, TB), :]).then_inc(s["copied"], 1)
                pool.wait_ge(s["copied"], 1)
                for t in range(TB):
                    for k in range(TOPK):
                        pool.indirect_dma_start(m.got[:, TOPK * t + k, :], None, a["slots_y"][:, :],
                                                bass.IndirectOffsetOnAxis(ap=m.slot_s[:, t, k:k + 1], axis=0)).then_inc(gathered[t], 16)

            @block.vector
            def _(dve):
                nc.vector.tensor_copy(m.gw_s[:], m.gatew4[:, bass.ds(b * TB, TB), :]).then_inc(s["added"], 1)
                n = 1
                for t in range(TB):
                    acc = m.acc[:, bass.ds(b * TB + t, 1), :].rearrange("p a d -> p (a d)")
                    dve.wait_ge(gathered[t], (b + 1) * (16 * TOPK))
                    for k in range(TOPK):
                        dve.wait_ge(s["added"], n)
                        nc.vector.scalar_tensor_tensor(out=acc, in0=m.got[:, TOPK * t + k, :], scalar=m.gw_s[:, t, k:k + 1], in1=acc,
                                                       op0=ALU.mult, op1=ALU.add).then_inc(s["added"], 1)
                        n += 1

            @block.sync
            def _(sp):
                sp.wait_ge(s["added"], 1 + TB * TOPK)
                sp.dma_start(a["out"][bass.ds(b, 1), :, :].rearrange("a (t p) d -> p (a t) d", p=P),
                             m.acc[:, bass.ds(b * TB, TB), :]).then_inc(s["stored"], 16)
                sp.wait_ge(s["stored"], 16)


class Memory(dict):
    __getattr__ = dict.__getitem__


def program(nc, a):
    with ExitStack() as whole:
        m = Memory(names=[])

        def sb(ctx, **shapes):
            for name, shape in shapes.items():
                dt = F32
                if isinstance(shape, tuple):
                    shape, dt = shape
                m[name] = ctx.enter_context(nc.sbuf_tensor(f"{name}_{len(m.names)}", [P] + shape, dt))
                m.names.append(name)

        m["ps"] = whole.enter_context(nc.psum_tensor("ps", [P, 8, 512], F32))
        sb(whole, acc=[NT, D], xT=[NT * P], h2=[NT, D], wr=[512], wo=[D],
           ident=[P], ident_bf=([P], BF16), future_bf=([4, P], BF16), before_bf=([P], BF16), ones_bf=([P], BF16),
           same_head=[P], arg_head=[HR], minus_half=[HR], tot_ones=[P],
           e_in=[NT * HR], e_out=[NT * HR], decay_tile_e=[NT], argL=([2 * B, P], F32R), argR=([2 * B, P], F32R),
           logit=[NT * E], gatew4=[NT, TOPK], slot=([NT, TOPK], I32), blk=([NBLK], I32),
           wn=[2], xTs=[T], sq=[512], ssq=[4], ms3=[4])
        with ExitStack() as c1:
            sb(c1, xn=[NT, D], hT=[NT * P], wqk=[NCH, P], wqk_swap=[NCH, P], wv=[KV * DH], vb=[KV * DH], projw=[8, D], projb=[D],
               gateb=[E], gatew=[E], sink=[H], sink8=[H], qkb=[NCH], qkb_swap=[NCH], rope_cos=[T], rope_sin=[T], window=[2 * P], hTs=[T])
            with ExitStack() as c2:
                sb(c2, zero=[D], wgt=[HR], qkvw=[(H + 2 * KV) * DH], future=[P], upto=[P], after=[P], before=[P],
                   row_head=[HR], arg_rows=[4], swap_rows=[P],
                   stats=[TB, 6], meanvar=[TB, 2], ve=[16], r1=[TB], r2=[TB], xs=[TB, D], hs=[TB, D], z=[NT * HR])
                load(nc, m, a)
                normalise(nc, m)
                with ExitStack() as c3:
                    sb(c3, gt=[NT * HR], bc4=([NT, 4 * HR], F32R), decay_tile=[NT])
                    gates(nc, m)
            with ExitStack() as c2:
                sb(c2, qk=[NCH, T], rope_t=[2, T], v=[TB, KV * DH], sm=[2, HG, 2 * P], prob=[2, HG, 2 * P], probT=[2, HG, 2, P],
                   mx=[2, HG], negmx=[2, HG], sinkm=[2, HG], esink=[2, HG], rowsum=[2, HG], den=[2, HG], rden=[2, HG],
                   y=[2, H * DH], yT=[8, P], tx=[D], x2=[D], h2s=[D], h2Ts=[P], r3=[TB])
                attention(nc, m)
        sb(whole, wu=[E, 2 * DFF], wd=[E, D])
        with ExitStack() as c1:
            sb(c1, top8=[NT, 8], idx8=([NT, 8], U32), idxf=[NT, TOPK], big=[6 * NT * E], chosen_bf=([NT * E], BF16), gexp=[NT, TOPK],
               gsum=[NT], grec=[NT], carry=[(NT + 1) * E], nblk=[E], cumblk=[E], base=[E], slotf=[NT, TOPK], blkf=[NBLK],
               iota_e=[E], iota_blk=[NT], iota_j=[NBLK], upto_e=[E, E])
            with semaphores(nc, "tables down up scaled") as s, nc.Block() as block:
                @block.sync
                def _(sp):
                    for e0 in range(0, E, 8):
                        sp.dma_start(m.wu[:, e0:e0 + 8, :], a["W_up"][e0:e0 + 8].rearrange("e p f -> p e f")).then_inc(s["up"], 16)
                    for n, name in enumerate(ROUTING_TABLES):
                        row = a[name].rearrange("(o n) -> o n", o=1).partition_broadcast(P)
                        dst = m[name][:].rearrange("p a b -> p (a b)") if name == "upto_e" else m[name][:]
                        sp.dma_start(dst, row).then_inc(s["tables"], 16)
                    sp.wait_ge(s["tables"], 16 * len(ROUTING_TABLES))

                @block.scalar
                def _(act):
                    act.dma_start(m.wd[:], a["W_down"].rearrange("e p f -> p e f")).then_inc(s["down"], 16)
                    act.wait_ge(s["down"], 16)

                @block.vector
                def _(dve):
                    dve.wait_ge(s["up"], 16 * 4)
                    nc.vector.tensor_scalar(m.wu[:], m.wu[:], m.wn[:, 1:2], None, ALU.mult).then_inc(s["scaled"], 1)
                    dve.wait_ge(s["scaled"], 1)
            routing(nc, m)
        with ExitStack() as c1:
            sb(c1, state=[P], e_in_s=[TB * HR], e_out_s=[TB * HR], decay_s=[TB], argLs=([2, P], F32R), argRx=([2, HR, P], F32R),
               sg1=[D], sg2=[D], sg=[D], eg=[D], qn=[D], kn=[D], vn=[D], qd=[D], kd=[D], q4=([512], F32R), k4=([512], F32R),
               q4T=([4, P], F32R), k4T=([4, P], F32R), qdT=[P], At=[2, 4, P], Dm=[2, 512], kvm=[P], osq=[D], ms16=[HR], ms16b=[HR],
               r16=[HR], on=[D], og=[D], ogT=[P], rr=[4], rows=[TB, D], slot_s=([TB, TOPK], I32))
            retention(nc, m, a)
        with ExitStack() as c1:
            sb(c1, xblk=[2, 4, D], yblk=[2, 4, D], xTb=[2, P], sl=[2, DFF], ab=[2, DFF], aTb=[2, P])
            experts(nc, m, a)
        with ExitStack() as c1:
            sb(c1, slot_s=([TB, TOPK], I32), got=[TB * TOPK, D], gw_s=[TB, TOPK])
            combine(nc, m, a)


ROUTING_TABLES = ["iota_e", "iota_blk", "iota_j", "upto_e"]


def routing_tables():
    e = np.arange(E)
    return {
        "iota_e": e.astype(np.float32),
        "iota_blk": (P * np.arange(NT)).astype(np.float32),
        "iota_j": np.arange(NBLK, dtype=np.float32),
        "upto_e": (e[None, :] <= e[:, None]).astype(np.float32).reshape(-1),
    }


ATTN = ["x", "Wq", "Wk", "Wv", "Wg", "Wgt", "Wo"]
FFN = ["attn_norm_w", "ffn_norm_w", "qkv_w", "qkv_b", "proj_w", "proj_b", "attn_sink", "gate_w", "gate_b", "W_up", "W_down"]


def kernel(**inputs):
    import concourse.bacc as _bacc
    from concourse.bass_utils import run_bass_kernel_spmd as _run

    nc = _bacc.Bacc("TRN2", target_bir_lowering=False, num_devices=1)
    given = {n: inputs["L0_attn_" + n] for n in ATTN} | {n: inputs["L0_ffn_" + n] for n in FFN} | tables() | routing_tables()
    arrays, aps = {}, {}
    for name, value in given.items():
        v = np.ascontiguousarray(value)
        arrays[f"in_{name}"] = v
        aps[name] = nc.dram_tensor(f"in_{name}", v.shape, mybir.dt.from_np(v.dtype), kind="ExternalInput").ap()
    aps["slots_x"] = nc.dram_tensor("slots_x", (SLOTS, D), F32, kind="Internal").ap()
    aps["slots_y"] = nc.dram_tensor("slots_y", (SLOTS, D), F32, kind="Internal").ap()
    aps["out"] = nc.dram_tensor("out", (B, T, D), F32, kind="ExternalOutput").ap()
    program(nc, aps)
    r = _run(nc, [arrays], core_ids=[0])
    return r.results[0]["out"]
```

```python
from contextlib import ExitStack, contextmanager

import numpy as np

import concourse.bass as bass
from concourse import mybir

F32 = mybir.dt.float32
F32R = mybir.dt.float32r
BF16 = mybir.dt.bfloat16
I32 = mybir.dt.int32
U32 = mybir.dt.uint32
ALU = mybir.AluOpType
ACT = mybir.ActivationFunctionType
AXX = mybir.AxisListType.X

P = 128
B, T, D = 8, 512, 128
TB = T // P
NT = B * TB
LN_EPS = 1e-5
RMS_EPS_R = 1e-6
RMS_EPS_F = 1e-5
HR, DR = 16, 8
H, KV, DH = 16, 4, 64
HG = H // KV
NQ = H // 2
NCH = NQ + KV // 2
E, TOPK, DFF = 32, 4, 128
WE = 2 * DFF + D
NBLK = (B * T * TOPK + E * (P - 1)) // P + 1
BPI = 40
NBLK = -(-NBLK // BPI) * BPI
SLOTS = NBLK * P
NEG = -1e30
NEG_R = -30000.0


def bc(ap, shape):
    return ap.to_broadcast(shape)


class Steps:

    def __init__(self, eng, sem):
        self.eng, self.sem, self.n = eng, sem, 0

    def __call__(self, ins):
        self.n += 1
        ins.then_inc(self.sem, 1)
        return self.n

    def wait(self, n=None):
        self.eng.wait_ge(self.sem, self.n if n is None else n)


@contextmanager
def semaphores(nc, names):
    with ExitStack() as ctx:
        s = {n: ctx.enter_context(nc.semaphore(n)) for n in names.split()}
        yield s
        for q in s.values():
            nc.gpsimd.sem_clear(q)
        nc.all_engine_barrier()


def load(nc, m, a):
    with semaphores(nc, "loaded_x loaded_w zeroed prepared") as s:
        with nc.Block() as block:
            @block.sync
            def _(sp):
                sp.dma_start(m.acc[:], a["x"].rearrange("b (t p) d -> p (b t) d", p=P)).then_inc(s["loaded_x"], 16)
                for src, dst in (
                    (a["Wq"], m.wr[:, 0:128]), (a["Wk"], m.wr[:, 128:256]),
                    (a["Wv"], m.wr[:, 256:384]), (a["Wg"], m.wr[:, 384:512]),
                    (a["Wgt"], m.wgt[:]), (a["Wo"], m.wo[:]),
                    (a["qkv_w"], m.qkvw[:]), (a["gate_w"], m.gatew[:]),
                    *((a["proj_w"].rearrange("(g h j r) n -> h j r g n", g=KV, h=2, j=2)[h, j], m.projw[DH * h:DH * h + DH, j::2, :])
                      for h in range(2) for j in range(2)),
                    (a["attn_norm_w"].rearrange("(p o) -> p o", o=1), m.wn[:, 0:1]),
                    (a["ffn_norm_w"].rearrange("(p o) -> p o", o=1), m.wn[:, 1:2]),
                ):
                    sp.dma_start(dst, src).then_inc(s["loaded_w"], 16)
                for n in range(NCH):
                    for half in range(2):
                        c0 = chunk_channels(n)[half]
                        src = a["qkv_b"][c0:c0 + DH]
                        rows = slice(DH * half, DH * half + DH)
                        sp.dma_start(m.qkb[rows, n:n + 1], src.rearrange("(p o) -> p o", o=1)).then_inc(s["loaded_w"], 16)
                for name in TABLES:
                    sp.dma_start(m[name][:], a[name]).then_inc(s["loaded_w"], 16)
                sp.wait_ge(s["zeroed"], 1)
                rows = NBLK // 8
                for i in range(8):
                    sp.dma_start(a["slots_x"][i * rows * P:(i + 1) * rows * P, :].rearrange("(r p) n -> p r n", p=P),
                                 bc(m.zero[:, None, :], [P, rows, D])).then_inc(m.slots_cleared, 16)
                for q in ("loaded_x", "loaded_w"):
                    sp.wait_ge(s[q], {"loaded_x": 16, "loaded_w": 16 * (14 + 2 * NCH + len(TABLES))}[q])

            @block.scalar
            def _(act):
                n = 0
                for src, dst in ((a["qkv_b"][H * DH + KV * DH:], m.vb[:]), (a["proj_b"], m.projb[:]),
                                 (a["gate_b"], m.gateb[:]), (a["attn_sink"], m.sink[:])):
                    act.dma_start(dst, src.rearrange("(o n) -> o n", o=1).partition_broadcast(P)).then_inc(s["prepared"], 16)
                    n += 1
                act.wait_ge(s["prepared"], 16 * n)

            @block.gpsimd
            def _(pool):
                nc.gpsimd.memset(m.zero[:], 0.0).then_inc(s["zeroed"], 1)
                nc.gpsimd.memset(m.h2[:, NT:, :], 0.0).then_inc(s["zeroed"], 1)

        with semaphores(nc, "own") as s2, nc.Block() as block:
            @block.vector
            def _(dve):
                own = Steps(dve, s2["own"])
                w, g = m.qkvw, m.wn[:, 0:1]
                for n in range(NCH):
                    for half in range(2):
                        c0 = chunk_channels(n)[half]
                        src = w[:, c0:c0 + DH]
                        own(nc.vector.tensor_scalar(m.wqk[:, n, DH * half:DH * half + DH], src, g, None, ALU.mult))
                own(nc.vector.tensor_scalar(m.wv[:], w[:, H * DH + KV * DH:], g, None, ALU.mult))
                own(nc.vector.tensor_scalar(m.gatew[:], m.gatew[:], m.wn[:, 1:2], None, ALU.mult))
                own(nc.vector.tensor_copy(m.ident_bf[:], m.ident[:]))
                own(nc.vector.tensor_scalar(m.sink8[:], m.sink[:], float(DH) ** 0.5, None, ALU.mult))
                own(nc.vector.tensor_copy(m.future_bf[:], bc(m.future[:, None, :], [P, 4, P])))
                own(nc.vector.memset(m.tot_ones[:], 1.0))
                own(nc.vector.memset(m.minus_half[:], -0.5))
                own(nc.vector.memset(m.ones_bf[:], 1.0))
                own(nc.vector.tensor_copy(m.before_bf[:], m.before[:]))
                own.wait()


def chunk_channels(n):
    if n < NQ:
        pair, j = divmod(n, HG)
        return ((2 * pair) * HG + j) * DH, ((2 * pair + 1) * HG + j) * DH
    kv = 2 * (n - NQ)
    return (H + kv) * DH, (H + kv + 1) * DH


def head_place(g, j):
    return (g // 2) * HG + j, DH * (g % 2)


def normalise(nc, m):
    with nc.Fori(0, B) as b:
        with semaphores(nc, "ve_ready r1_ready ms_ready r2_ready xn_ready h_ready own xn_T h_T xT_ready z_done ev") as s:
            tiles = bass.ds(b * TB, TB)
            with nc.Block() as block:
                @block.vector
                def _(dve):
                    own = Steps(dve, s["own"])
                    for t in range(TB):
                        own(nc.vector.bn_stats(m.stats[:, t, :], m.acc[:, bass.ds(b * TB + t, 1), :].rearrange("p a d -> p (a d)")))
                    for t in range(TB):
                        own.wait(t + 1)
                        own(nc.vector.bn_aggr(m.meanvar[:, t, :], m.stats[:, t, :]))
                    own.wait()
                    nc.vector.tensor_scalar(m.ve[:, 0:TB], m.meanvar[:, :, 1], LN_EPS, None, ALU.add).then_inc(s["ve_ready"], 1)
                    dve.wait_ge(s["r1_ready"], 1)
                    own(nc.vector.tensor_tensor(m.ve[:, 4:4 + TB], m.meanvar[:, :, 1], m.r1[:, 0:TB], ALU.mult))
                    own.wait()
                    own(nc.vector.tensor_tensor(m.ve[:, 8:8 + TB], m.ve[:, 4:4 + TB], m.r1[:, 0:TB], ALU.mult))
                    own.wait()
                    nc.vector.tensor_scalar(m.ve[:, 12:12 + TB], m.ve[:, 8:8 + TB], RMS_EPS_F, None, ALU.add).then_inc(s["ms_ready"], 1)
                    for t in range(TB):
                        nc.vector.tensor_scalar(m.xs[:, t, :], m.acc[:, bass.ds(b * TB + t, 1), :].rearrange("p a d -> p (a d)"),
                                                m.meanvar[:, t, 0:1], m.r1[:, t:t + 1],
                                                ALU.subtract, ALU.mult).then_inc(s["xn_ready"], 1)
                    dve.wait_ge(s["r2_ready"], 1)
                    dve.wait_ge(s["xn_ready"], TB)
                    for t in range(TB):
                        nc.vector.tensor_scalar(m.hs[:, t, :], m.xs[:, t, :], m.r2[:, t:t + 1], None,
                                                ALU.mult).then_inc(s["h_ready"], 1)
                    own(nc.vector.tensor_copy(m.xn[:, tiles, :], m.xs[:]))
                    dve.wait_ge(s["h_T"], 1)
                    own(nc.vector.tensor_copy(m.hT[:, bass.ds(b * T, T)], m.ps[:, 1, :]))
                    dve.wait_ge(s["z_done"], 1)
                    own(nc.vector.tensor_copy(m.z[:, bass.ds(b * TB * HR, TB * HR)], m.ps[:, 2, 0:TB * HR]))

                @block.gpsimd
                def _(pool):
                    pool.wait_ge(s["ve_ready"], 1)
                    nc.gpsimd.tensor_tensor(m.r1[:, 0:TB], m.ve[:, 0:TB], m.minus_half[:, 0:TB], ALU.pow).then_inc(s["r1_ready"], 1)
                    pool.wait_ge(s["ms_ready"], 1)
                    nc.gpsimd.tensor_tensor(m.r2[:, 0:TB], m.ve[:, 12:12 + TB], m.minus_half[:, 0:TB], ALU.pow).then_inc(s["r2_ready"], 1)

                @block.tensor
                def _(pe):
                    for t in range(TB):
                        pe.wait_ge(s["xn_ready"], t + 1)
                        mm = pe.transpose(m.ps[:, 0, t * P:(t + 1) * P], m.xs[:, t, :], m.ident[:])
                    mm.then_inc(s["xn_T"], 1)
                    for t in range(TB):
                        pe.wait_ge(s["h_ready"], t + 1)
                        mm = pe.transpose(m.ps[:, 1, t * P:(t + 1) * P], m.hs[:, t, :], m.ident[:])
                    mm.then_inc(s["h_T"], 1)
                    pe.wait_ge(s["xT_ready"], 1)
                    for t in range(TB):
                        mm = pe.matmul(m.ps[:, 2, t * HR:(t + 1) * HR], m.xTs[:, t * P:(t + 1) * P], m.wgt[:], start=True, stop=True)
                    mm.then_inc(s["z_done"], 1)

                @block.scalar
                def _(act):
                    act.wait_ge(s["xn_T"], 1)
                    act.copy(m.xTs[:], m.ps[:, 0, :]).then_inc(s["xT_ready"], 1)
                    act.wait_ge(s["xT_ready"], 1)
                    act.copy(m.xT[:, bass.ds(b * T, T)], m.xTs[:]).then_inc(s["ev"], 1)


def gates(nc, m):
    with semaphores(nc, "dve e_ready l_ready g_ready bc_done rem_done tot_done exps parts_ready T_done T_free") as s:
        with nc.Block() as block:
            NC = NT * HR
            @block.vector
            def _(dve):
                own = Steps(dve, s["dve"])
                a1, a2, a3 = (buf[:].rearrange("p t d -> p (t d)") for buf in (m.xs, m.hs, m.xTs.rearrange("p (t d) -> p t d", d=P)))
                own(nc.vector.scalar_tensor_tensor(out=a1, in0=m.z[:], scalar=-1.0, in1=m.z[:], op0=ALU.mult, op1=ALU.min))
                dve.wait_ge(s["e_ready"], 1)
                dve.wait_ge(s["l_ready"], 1)
                own(nc.vector.scalar_tensor_tensor(out=a1, in0=m.z[:], scalar=0.0, in1=a3, op0=ALU.min, op1=ALU.subtract))
                own.wait()
                nc.vector.tensor_scalar(m.gt[:], a1, 1.0 / 16.0, None, ALU.mult).then_inc(s["g_ready"], 1)
                dve.wait_ge(s["bc_done"], 1)
                parts = m.bc4[:, :, :].rearrange("p t (k h) -> p t k h", k=4)
                bcv = m.ps[:, 0, :].rearrange("p (t h) -> p t h", h=HR)
                own(nc.vector.tensor_copy(parts[:, :, 0, :], bcv))
                own.wait()
                own(nc.vector.tensor_tensor(parts[:, :, 1, :], bcv, parts[:, :, 0, :].bitcast(F32), ALU.subtract))
                own.wait()
                own(nc.vector.tensor_scalar(parts[:, :, 2, :], parts[:, :, 0, :].bitcast(F32), -1.0, None, ALU.mult))
                nc.vector.tensor_scalar(parts[:, :, 3, :], parts[:, :, 1, :].bitcast(F32), -1.0, None, ALU.mult).then_inc(s["parts_ready"], 1)
                dve.wait_ge(s["tot_done"], 1)
                own(nc.vector.tensor_tensor(a2.rearrange("p (t h) -> p t h", h=HR), m.ps[:, 2, :].rearrange("p (t h) -> p t h", h=HR),
                                            bc(m.row_head[:, None, :], [P, NT, HR]), ALU.mult))
                own.wait()
                own(nc.vector.tensor_reduce(m.decay_tile[:], a2.rearrange("p (t h) -> p t h", h=HR), AXX, ALU.add))
                for q in range(4):
                    dve.wait_ge(s["T_done"], q + 1)
                    own(nc.vector.tensor_scalar(m.argL[:, 4 * q:4 * q + 4, :], m.ps[:, 4 + q % 2, :].rearrange("p (q i) -> p q i", i=P),
                                                m.arg_rows[:, 0:1], m.arg_rows[:, 1:2], ALU.mult, ALU.add))
                    nc.vector.tensor_scalar(m.argR[:, 4 * q:4 * q + 4, :], m.ps[:, 4 + q % 2, :].rearrange("p (q i) -> p q i", i=P),
                                            m.arg_rows[:, 2:3], m.arg_rows[:, 3:4], ALU.mult, ALU.add).then_inc(s["T_free"], 1)

            @block.tensor
            def _(pe):
                pe.wait_ge(s["g_ready"], 1)
                pe.matmul(m.ps[:, 0, :], m.upto[:], m.gt[:], start=True, stop=True).then_inc(s["bc_done"], 1)
                pe.matmul(m.ps[:, 1, :], m.after[:], m.gt[:], start=True, stop=True).then_inc(s["rem_done"], 1)
                pe.matmul(m.ps[:, 2, :], m.tot_ones[:], m.gt[:], start=True, stop=True).then_inc(s["tot_done"], 1)
                pe.wait_ge(s["parts_ready"], 1)
                pe.wait_ge(s["dve"], 5)
                for q in range(4):
                    if q >= 2:
                        pe.wait_ge(s["T_free"], q - 1)
                    for i in range(4):
                        pair = m.bc4[:, 2 * (4 * q + i):2 * (4 * q + i) + 2, :].rearrange("p t k -> p (t k)")
                        mm = pe.transpose(m.ps[:, 4 + q % 2, i * P:(i + 1) * P], pair.bitcast(F32), m.ident[:])
                    mm.then_inc(s["T_done"], 1)

            @block.scalar
            def _(act):
                a1, a2, a3 = (buf[:].rearrange("p t d -> p (t d)") for buf in (m.xs, m.hs, m.xTs.rearrange("p (t d) -> p t d", d=P)))
                act.wait_ge(s["dve"], 1)
                act.activation(a2, a1, ACT.Exp).then_inc(s["e_ready"], 1)
                act.wait_ge(s["e_ready"], 1)
                act.activation(a3, a2, ACT.Ln, bias=1.0).then_inc(s["l_ready"], 1)
                act.wait_ge(s["bc_done"], 1)
                act.wait_ge(s["parts_ready"], 1)
                act.activation(m.e_in[:], m.ps[:, 0, :], ACT.Exp).then_inc(s["exps"], 1)
                act.wait_ge(s["rem_done"], 1)
                act.activation(m.e_out[:], m.ps[:, 1, :], ACT.Exp).then_inc(s["exps"], 1)
                act.wait_ge(s["dve"], 7)
                act.activation(m.decay_tile_e[:], m.decay_tile[:], ACT.Exp).then_inc(s["exps"], 1)


TABLES = ["ident", "rope_cos", "rope_sin", "window", "future", "upto", "after", "before",
          "row_head", "same_head", "arg_rows", "arg_head"]


def tables():
    i, j = np.arange(P)[:, None], np.arange(P)[None, :]
    f = np.float32
    inv = (f(1.0) / f(150000.0) ** (np.arange(0, DH, 2, dtype=f) / f(DH))).astype(f)
    freqs = (np.arange(T, dtype=f) / f(32.0))[None, :] * inv[:, None]
    rep = (np.arange(P) % DH) // 2
    sign = np.where(np.arange(P) % 2 == 0, f(-1), f(1))[:, None]
    rows = np.arange(P) % 64
    return {
        "ident": np.eye(P, dtype=f),
        "rope_cos": np.cos(freqs).astype(f)[rep],
        "rope_sin": (np.sin(freqs).astype(f)[rep] * sign).astype(f),
        "window": np.concatenate([np.where(j >= i, 0, NEG), np.where(j <= i, 0, NEG)], 1).astype(f),
        "future": np.where(j < i, NEG_R, 0).astype(f),
        "upto": (i <= j).astype(f),
        "after": (i > j).astype(f),
        "before": (i < j).astype(f),
        "row_head": (i // DR == np.arange(HR)[None, :]).astype(f),
        "same_head": (i // DR == j // DR).astype(f),
        "arg_rows": np.stack([rows >= 32, rows < 32, rows < 32, rows >= 32], 1).astype(f),
        "arg_head": (np.arange(P)[:, None] % HR == np.arange(HR)[None, :]).astype(f),
    }


PREP = [("qk", n) for n in (NQ, *range(HG), NQ + 1, *range(HG, NQ))] + [("v", 0), ("v", 1)]
NP = len(PREP)


def is_rope(k):
    return PREP[k % NP][0] == "qk"


def rope_count(k):
    return sum(is_rope(i) for i in range(k))


def prepare_products(nc, m, pe, s, k, bank, banks):
    kind, n = PREP[k % NP]
    if k >= banks:
        if PREP[(k - banks) % NP][0] == "qk":
            pe.wait_ge(s["raw_ready"], rope_count(k - banks + 1))
        else:
            pe.wait_ge(s["v_ready"], k - banks + 1 - rope_count(k - banks + 1))
    if kind == "qk":
        mm = pe.matmul(m.ps[:, bank, :], m.wqk[:, n, :], m.hTs[:], start=True, stop=True)
    else:
        for i in range(2):
            t = 2 * n + i
            mm = pe.matmul(m.ps[:, bank, i * 256:(i + 1) * 256], m.hTs[:, t * P:(t + 1) * P], m.wv[:], start=True, stop=True)
    mm.then_inc(s["prep_done"], 1)


def prepare_raw(nc, m, act, s, k, bank):
    kind, n = PREP[k % NP]
    if kind == "qk":
        r = rope_count(k)
        act.wait_ge(s["prep_done"], k + 1)
        if r >= 2:
            act.wait_ge(s["cos_ready"], r - 1)
            act.wait_ge(s["sin_ready"], r - 1)
        nc.scalar.activation(m.raw[:, r % 2, :], m.ps[:, bank, :], ACT.Identity, bias=m.qkb[:, n:n + 1]).then_inc(s["raw_ready"], 1)


def prepare_swapped(nc, m, sp, s, r):
    sp.wait_ge(s["raw_ready"], r + 1)
    if r >= 2:
        sp.wait_ge(s["roped"], r - 1)
    for odd in range(2):
        sp.dma_start(m.swapped[1 - odd:P:2, r % 2, :], m.raw[odd:P:2, r % 2, :]).then_inc(s[f"swapped_{r % 2}"], 16)


def prepare_sin(nc, m, pool, s, r):
    pool.wait_ge(s[f"swapped_{r % 2}"], 32 * (r // 2 + 1))
    nc.gpsimd.tensor_tensor(m.swapped[:, r % 2, :], m.swapped[:, r % 2, :], m.rope_sin[:], ALU.mult).then_inc(s["sin_ready"], 1)


def prepare_cos(nc, m, dve, s, k, bank, buf):
    kind, n = PREP[k % NP]
    if kind == "qk":
        dve.wait_ge(s["raw_ready"], rope_count(k + 1))
        nc.vector.tensor_tensor(m.qk[:, buf, n, :], m.raw[:, rope_count(k) % 2, :], m.rope_cos[:], ALU.mult).then_inc(s["cos_ready"], 1)
    else:
        dve.wait_ge(s["prep_done"], k + 1)
        nc.vector.tensor_tensor(m.v[:, buf, 2 * n:2 * n + 2, :], m.ps[:, bank, :].rearrange("p (t c) -> p t c", t=2),
                                bc(m.vb[:, None, :], [P, 2, KV * DH]), ALU.add).then_inc(s["v_ready"], 1)


def prepare_sum(nc, m, dve, s, k, buf):
    kind, n = PREP[k % NP]
    if kind == "qk":
        r = rope_count(k)
        dve.wait_ge(s["cos_ready"], r + 1)
        dve.wait_ge(s["sin_ready"], r + 1)
        out = m.qk[:, buf, n, :]
        nc.vector.tensor_tensor(out, out, m.swapped[:, r % 2, :], ALU.add).then_inc(s["roped"], 1)


PREP_NAMES = "hs_ready prep_done raw_ready swapped_0 swapped_1 sin_ready cos_ready roped v_ready "


def prepare_first(nc, m):
    with semaphores(nc, PREP_NAMES) as s, nc.Block() as block:
        @block.scalar
        def _(act):
            act.copy(m.hTs[:], m.hT[:, 0:T]).then_inc(s["hs_ready"], 1)
            for k in range(NP):
                prepare_raw(nc, m, act, s, k, k % 4)

        @block.tensor
        def _(pe):
            pe.wait_ge(s["hs_ready"], 1)
            for k in range(NP):
                prepare_products(nc, m, pe, s, k, k % 4, 4)

        @block.sync
        def _(sp):
            for r in range(rope_count(NP)):
                prepare_swapped(nc, m, sp, s, r)

        @block.gpsimd
        def _(pool):
            for r in range(rope_count(NP)):
                prepare_sin(nc, m, pool, s, r)

        @block.vector
        def _(dve):
            for k in range(NP + 1):
                if k < NP:
                    prepare_cos(nc, m, dve, s, k, k % 4, 0)
                if k >= 1:
                    prepare_sum(nc, m, dve, s, k - 1, 0)
            dve.wait_ge(s["roped"], rope_count(NP))


def attention(nc, m):
    ROWS = 2
    UR = TB * KV
    U = ROWS * UR
    prepare_first(nc, m)
    names = (PREP_NAMES + "S_done mx_ready neg_ready masked exp_done "
             "sinkexp den_ready rinv_ready scaled PT_a PT_b PTs_a PTs_b PV_done yT_ready "
             "proj_done tx_ready x2_ready x2_sq ms_ready r3_ready h2_ready h2T_done h2Ts_ready gate_done gate_ready kept")
    PT_A, PT_B, YP, PREP_BANK = 4, 5, 6, 7
    SM = T // 2

    def place(u):
        r, rest = divmod(u, UR)
        return (r,) + divmod(rest, KV)

    def prep_step(st):
        r, n = divmod(st, UR)
        return r * NP + n if 0 <= st < U and n < NP else None

    def small(st):
        q, k = divmod(st - 5, 4)
        return (q, k) if 0 <= q < ROWS * TB else (None, None)

    with nc.Fori(0, B // ROWS) as i:
        with semaphores(nc, names) as s:
            S = [m.ps[:, 2 * n:2 * n + 2, :].rearrange("p k n -> p (k n)").rearrange("p (j w) -> p j w", j=HG) for n in range(2)]
            with nc.Block() as block:
                @block.tensor
                def _(pe):
                    def prepare(k):
                        if k % NP == 0:
                            pe.wait_ge(s["hs_ready"], k // NP + 1)
                        prepare_products(nc, m, pe, s, k, PREP_BANK, 1)

                    def scores(u):
                        r, qt, g = place(u)
                        if r >= 1 and qt == 0 and g % 2 == 0:
                            pe.wait_ge(s["roped"], rope_count((r - 1) * NP + (1 + g // 2) * (1 + HG)))
                        if u >= 2:
                            pe.wait_ge(s["mx_ready"], HG * (u - 1))
                        for j in range(HG):
                            ch, row = head_place(g, j)
                            w0 = P if qt == 0 else 0
                            keys = m.qk[row:row + DH, r, NQ + g // 2, (qt - 1) * P + w0:(qt + 1) * P]
                            mm = pe.matmul(S[u % 2][:, j, w0:2 * P], m.qk[row:row + DH, r, ch, qt * P:(qt + 1) * P], keys,
                                           start=True, stop=True)
                        mm.then_inc(s["S_done"], 1)

                    def transposes(u):
                        r, qt, g = place(u)
                        pe.wait_ge(s["scaled"], u + 1)
                        for j in range(HG):
                            bank, done, read = ((PT_A, "PT_a", "PTs_a"), (PT_B, "PT_b", "PTs_b"))[j // 2]
                            if j % 2 == 0 and u >= 1:
                                pe.wait_ge(s[read], u)
                            for kt in range(1 if qt == 0 else 0, 2):
                                c = 256 * (j % 2) + P * kt
                                mm = pe.transpose(m.ps[:, bank, c:c + P], m.prob[:, u % 3, j, kt * P:(kt + 1) * P], m.ident[:])
                            if j % 2 == 1:
                                mm.then_inc(s[done], 1)

                    def values(u):
                        r, qt, g = place(u)
                        if r >= 1 and qt == 0 and g == 0:
                            pe.wait_ge(s["v_ready"], r * NP - rope_count(r * NP))
                        pe.wait_ge(s["PTs_a"], u + 1)
                        pe.wait_ge(s["PTs_b"], u + 1)
                        if u >= 1:
                            pe.wait_ge(s["yT_ready"], u)
                        q, k = small(u)
                        if k == 0:
                            pe.wait_ge(s["x2_ready"], q + 1)
                        elif k == 2:
                            pe.wait_ge(s["h2Ts_ready"], q + 1)
                        elif k == 3:
                            pe.wait_ge(s["gate_ready"], q + 1)
                        first = 1 if qt == 0 else 0
                        for kt in range(first, 2):
                            for half in range(2):
                                mm = pe.matmul(m.ps[DH * half:DH * half + DH, YP, 0:2 * P], m.v[:, r, qt - 1 + kt, g * DH:(g + 1) * DH],
                                               m.probT[:, u % 2, 2 * half:2 * half + 2, kt, :], start=(kt == first), stop=(kt == 1),
                                               skip_group_check=True)
                        mm.then_inc(s["PV_done"], 1)

                    def small_products(st):
                        q, k = small(st)
                        if k in (0, 2, 3):
                            pe.wait_ge(s["yT_ready"], min(st, U))
                        if k == 0:
                            if q >= 1:
                                pe.wait_ge(s["gate_ready"], q)
                            for c in range(2 * KV):
                                mm = pe.matmul(m.ps[:, YP, SM:SM + D], m.yT[:, q % 2, c, :], m.projw[:, c, :], start=(c == 0), stop=(c == 2 * KV - 1))
                            mm.then_inc(s["proj_done"], 1)
                        elif k == 2:
                            pe.wait_ge(s["x2_ready"], q + 1)
                            pe.wait_ge(s["h2_ready"], q + 1)
                            pe.transpose(m.ps[:, YP, SM:SM + P], m.h2s[:], m.ident[:]).then_inc(s["h2T_done"], 1)
                        elif k == 3:
                            pe.wait_ge(s["h2Ts_ready"], q + 1)
                            pe.matmul(m.ps[:, YP, SM:SM + E], m.h2Ts[:], m.gatew[:], start=True, stop=True).then_inc(s["gate_done"], 1)

                    for u in range(3):
                        scores(u)
                    for st in range(U + 5):
                        if prep_step(st) is not None:
                            prepare(prep_step(st))
                        if st < U:
                            transposes(st)
                        if 1 <= st <= U:
                            values(st - 1)
                        if st + 3 < U:
                            scores(st + 3)
                        small_products(st)

                @block.vector
                def _(dve):
                    def mask(u):
                        r, qt, g = place(u)
                        w0 = P if qt == 0 else 0
                        dve.wait_ge(s["S_done"], u + 1)
                        if u >= 2:
                            dve.wait_ge(s["sinkexp"], u - 1)
                        if u >= 3:
                            dve.wait_ge(s["PT_b"], u - 2)
                        for j in range(HG):
                            h = g * HG + j
                            nc.vector.tensor_tensor_reduce(out=m.prob[:, u % 3, j, w0:2 * P], in0=S[u % 2][:, j, w0:2 * P],
                                                           in1=m.window[:, w0:2 * P], scale=1.0, scalar=m.sink8[:, h:h + 1],
                                                           op0=ALU.add, op1=ALU.max, accum_out=m.mx[:, u % 2, j:j + 1]).then_inc(s["mx_ready"], 1)
                        dve.wait_ge(s["mx_ready"], HG * (u + 1))
                        nc.vector.tensor_scalar(m.negmx[:, u % 2, :], m.mx[:, u % 2, :], -(float(DH) ** -0.5), None, ALU.mult).then_inc(s["neg_ready"], 1)
                        dve.wait_ge(s["neg_ready"], u + 1)
                        nc.vector.tensor_tensor(m.sinkm[:, u % 2, :], m.sink[:, g * HG:(g + 1) * HG], m.negmx[:, u % 2, :], ALU.add).then_inc(s["masked"], 1)

                    def inverse(u):
                        dve.wait_ge(s["exp_done"], HG * (u + 1))
                        dve.wait_ge(s["sinkexp"], u + 1)
                        nc.vector.tensor_tensor(m.den[:, u % 2, :], m.rowsum[:, u % 2, :], m.esink[:, u % 2, :], ALU.add).then_inc(s["den_ready"], 1)
                        dve.wait_ge(s["den_ready"], u + 1)
                        if u >= 2:
                            dve.wait_ge(s["scaled"], u - 1)
                        nc.vector.reciprocal(m.rden[:, u % 2, :], m.den[:, u % 2, :]).then_inc(s["rinv_ready"], 1)

                    mask(0)
                    mask(1)
                    inverse(0)
                    for st in range(U + 5):
                        q, k = small(st)
                        if prep_step(st - 1) is not None and is_rope(prep_step(st - 1)):
                            prepare_cos(nc, m, dve, s, prep_step(st - 1), PREP_BANK, 1 - prep_step(st - 1) // NP)
                        if st < U:
                            dve.wait_ge(s["PT_b"], st + 1)
                            if st >= 2:
                                dve.wait_ge(s["PV_done"], st - 1)
                            w0 = 1 if place(st)[1] == 0 else 0
                            nc.vector.tensor_copy(m.probT[:, st % 2, 2:4, w0:2, :],
                                                  m.ps[:, PT_B, :].rearrange("p (j k i) -> p j k i", j=2, k=2)[:, :, w0:2, :]).then_inc(s["PTs_b"], 1)
                        if st + 1 < U:
                            inverse(st + 1)
                        if prep_step(st) is not None and not is_rope(prep_step(st)):
                            prepare_cos(nc, m, dve, s, prep_step(st), PREP_BANK, 1 - prep_step(st) // NP)
                        if k == 2:
                            dve.wait_ge(s["r3_ready"], q + 1)
                            if q >= 1:
                                dve.wait_ge(s["h2T_done"], q)
                                dve.wait_ge(s["kept"], 2 * q)
                            nc.vector.tensor_scalar(m.h2s[:], m.x2[:], m.r3[:, q % TB:q % TB + 1], None, ALU.mult).then_inc(s["h2_ready"], 1)
                        if st + 2 < U:
                            mask(st + 2)
                        if prep_step(st - 2) is not None:
                            prepare_sum(nc, m, dve, s, prep_step(st - 2), 1 - prep_step(st - 2) // NP)
                        if k == 0:
                            dve.wait_ge(s["tx_ready"], q + 1)
                            dve.wait_ge(s["proj_done"], q + 1)
                            if q >= 1:
                                dve.wait_ge(s["kept"], 2 * q)
                            nc.vector.tensor_tensor(m.x2[:], m.ps[:, YP, SM:SM + D], m.tx[:], ALU.add).then_inc(s["x2_ready"], 1)
                        if k == 3:
                            dve.wait_ge(s["gate_done"], q + 1)
                            nc.vector.tensor_tensor(m.logit[:, bass.ds((i * (ROWS * TB) + q) * E, E)], m.ps[:, YP, SM:SM + E], m.gateb[:], ALU.add).then_inc(s["gate_ready"], 1)

                @block.scalar
                def _(act):
                    def exps(u):
                        r, qt, g = place(u)
                        w0 = P if qt == 0 else 0
                        act.wait_ge(s["masked"], u + 1)
                        if u >= 2:
                            act.wait_ge(s["den_ready"], u - 1)
                        for j in range(HG):
                            nc.scalar.activation(m.prob[:, u % 3, j, w0:2 * P], m.prob[:, u % 3, j, w0:2 * P], ACT.Exp,
                                                 bias=m.negmx[:, u % 2, j:j + 1], scale=float(DH) ** -0.5,
                                                 accum_out=m.rowsum[:, u % 2, j:j + 1]).then_inc(s["exp_done"], 1)
                        nc.scalar.activation(m.esink[:, u % 2, :], m.sinkm[:, u % 2, :], ACT.Exp).then_inc(s["sinkexp"], 1)

                    def next_row(r):
                        if r >= 1:
                            act.wait_ge(s["prep_done"], r * NP)
                        act.copy(m.hTs[:], m.hT[:, bass.ds((i * ROWS + r + 1) * T, T)]).then_inc(s["hs_ready"], 1)

                    next_row(0)
                    exps(0)
                    exps(1)
                    for st in range(U + 5):
                        q, k = small(st)
                        if st + 2 < U and (st + 2) % UR == 0:
                            next_row((st + 2) // UR)
                        if st < U:
                            act.wait_ge(s["PT_a"], st + 1)
                            if st >= 2:
                                act.wait_ge(s["PV_done"], st - 1)
                            w0 = 1 if place(st)[1] == 0 else 0
                            nc.scalar.copy(m.probT[:, st % 2, 0:2, w0:2, :],
                                           m.ps[:, PT_A, :].rearrange("p (j k i) -> p j k i", j=2, k=2)[:, :, w0:2, :]).then_inc(s["PTs_a"], 1)
                        if 1 <= st <= U:
                            tile, g = divmod(st - 1, KV)
                            act.wait_ge(s["PV_done"], st)
                            if tile >= 2:
                                act.wait_ge(s["proj_done"], tile - 1)
                            nc.scalar.copy(m.yT[:, tile % 2, 2 * g:2 * g + 2, :], m.ps[:, YP, 0:2 * P].rearrange("p (j i) -> p j i", j=2)).then_inc(s["yT_ready"], 1)
                        if k == 1:
                            act.wait_ge(s["x2_ready"], q + 1)
                            if q >= 1:
                                act.wait_ge(s["x2_sq"], q)
                            nc.scalar.activation(m.sq[:, 0:D], m.x2[:], ACT.Square, accum_out=m.ssq[:, q % TB:q % TB + 1]).then_inc(s["x2_sq"], 1)
                        if prep_step(st) is not None:
                            prepare_raw(nc, m, act, s, prep_step(st), PREP_BANK)
                        if st + 2 < U:
                            exps(st + 2)
                        if k == 2:
                            act.wait_ge(s["h2T_done"], q + 1)
                            if q >= 1:
                                act.wait_ge(s["gate_done"], q)
                            nc.scalar.copy(m.h2Ts[:], m.ps[:, YP, SM:SM + P]).then_inc(s["h2Ts_ready"], 1)

                @block.sync
                def _(sp):
                    for r in range(rope_count(ROWS * NP)):
                        prepare_swapped(nc, m, sp, s, r)

                @block.gpsimd
                def _(pool):
                    def scale(u):
                        w0 = P if place(u)[1] == 0 else 0
                        pool.wait_ge(s["rinv_ready"], u + 1)
                        p = m.prob[:, u % 3, :, w0:2 * P]
                        nc.gpsimd.tensor_tensor(p, p, bc(m.rden[:, u % 2, :, None], [P, HG, 2 * P - w0]), ALU.mult).then_inc(s["scaled"], 1)

                    def residual(q):
                        if q >= 1:
                            pool.wait_ge(s["x2_ready"], q)
                        nc.gpsimd.tensor_tensor(m.tx[:], m.xn[:, bass.ds(i * (ROWS * TB) + q, 1), :].rearrange("p a d -> p (a d)"), m.projb[:],
                                                ALU.add).then_inc(s["tx_ready"], 1)

                    residual(0)
                    scale(0)
                    for st in range(U + 5):
                        q, k = small(st)
                        if st + 1 < U:
                            scale(st + 1)
                        k1 = prep_step(st - 1)
                        if k1 is not None and is_rope(k1):
                            prepare_sin(nc, m, pool, s, rope_count(k1))
                        if q is None:
                            continue
                        tile = bass.ds(i * (ROWS * TB) + q, 1)
                        if k == 3 and q + 1 < ROWS * TB:
                            residual(q + 1)
                        if k == 1:
                            pool.wait_ge(s["x2_sq"], q + 1)
                            c = q % TB
                            nc.gpsimd.tensor_scalar(m.ms3[:, c:c + 1], m.ssq[:, c:c + 1], 1.0 / D, RMS_EPS_F, ALU.mult, ALU.add).then_inc(s["ms_ready"], 1)
                            pool.wait_ge(s["ms_ready"], q + 1)
                            if q >= TB:
                                pool.wait_ge(s["h2_ready"], q - TB + 1)
                            nc.gpsimd.tensor_tensor(m.r3[:, c:c + 1], m.ms3[:, c:c + 1], m.minus_half[:, 0:1], ALU.pow).then_inc(s["r3_ready"], 1)
                        if k == 2:
                            a = m.acc[:, tile, :].rearrange("p a d -> p (a d)")
                            nc.gpsimd.tensor_tensor(a, a, m.x2[:], ALU.add).then_inc(s["kept"], 1)
                            pool.wait_ge(s["h2_ready"], q + 1)
                            nc.gpsimd.tensor_copy(m.h2[:, tile, :].rearrange("p a d -> p (a d)"), m.h2s[:]).then_inc(s["kept"], 1)


def routing(nc, m):
    TE = NT * E
    with semaphores(nc, "top own before_done count_done mask_ready exp_ready neg_ready pool") as s:
        onehot = [m.big[:, k * TE:(k + 1) * TE] for k in range(TOPK)]
        def t3(ap):
            return ap.rearrange("p (t e) -> p t e", e=E)
        with nc.Block() as block:
            @block.vector
            def _(dve):
                own = Steps(dve, s["own"])
                for t in range(NT):
                    own(nc.vector.max(m.top8[:, t, :], m.logit[:, t * E:(t + 1) * E]))
                for t in range(NT):
                    own.wait(t + 1)
                    own(nc.vector.max_index(m.idx8[:, t, :], m.top8[:, t, :], m.logit[:, t * E:(t + 1) * E]))
                own.wait()
                own(nc.vector.tensor_copy(m.idxf[:], m.idx8[:, :, 0:TOPK]))
                own.wait()
                for k in range(TOPK):
                    own(nc.vector.tensor_tensor(t3(onehot[k]), bc(m.idxf[:, :, k:k + 1], [P, NT, E]),
                                                bc(m.iota_e[:, None, :], [P, NT, E]), ALU.is_equal))
                own.wait()
                a, c = m.big[:, 4 * TE:5 * TE], m.big[:, 5 * TE:6 * TE]
                own(nc.vector.tensor_tensor(a, onehot[0], onehot[1], ALU.add))
                own(nc.vector.tensor_tensor(c, onehot[2], onehot[3], ALU.add))
                own.wait()
                nc.vector.tensor_tensor(m.chosen_bf[:], a, c, ALU.add).then_inc(s["mask_ready"], 1)
                own(nc.vector.tensor_tensor(m.gatew4[:], m.top8[:, :, 0:TOPK], bc(m.top8[:, :, 0:1], [P, NT, TOPK]), ALU.subtract))
                dve.wait_ge(s["exp_ready"], 1)
                own(nc.vector.tensor_reduce(m.gsum[:], m.gexp[:], AXX, ALU.add))
                own.wait()
                own(nc.vector.reciprocal(m.grec[:], m.gsum[:]))
                own.wait()
                own(nc.vector.tensor_tensor(m.gatew4[:], m.gexp[:], bc(m.grec[:, :, None], [P, NT, TOPK]), ALU.mult))
                dve.wait_ge(s["before_done"], 2)
                dve.wait_ge(s["count_done"], 2)
                own(nc.vector.tensor_copy(c, m.ps[:, 2:4, :].rearrange("p k n -> p (k n)")))
                own(nc.vector.memset(m.carry[:, 0:E], 0.0))
                for t in range(1, NT + 1):
                    own.wait()
                    own(nc.vector.tensor_tensor(m.carry[:, t * E:(t + 1) * E], m.carry[:, (t - 1) * E:t * E], c[:, (t - 1) * E:t * E], ALU.add))
                own.wait()
                n_e = m.carry[:, TE:TE + E]
                own(nc.vector.tensor_tensor(t3(a), bc(n_e[:, :, None], [P, E, NT]), bc(m.iota_blk[:, None, 0:NT], [P, E, NT]), ALU.is_gt))
                own.wait()
                own(nc.vector.tensor_reduce(m.nblk[:], t3(a), AXX, ALU.add))
                own.wait()
                own(nc.vector.tensor_tensor(t3(a), bc(m.nblk[:, None, :], [P, E, E]), m.upto_e[:], ALU.mult))
                own.wait()
                own(nc.vector.tensor_reduce(m.cumblk[:], t3(a), AXX, ALU.add))
                own.wait()
                own(nc.vector.tensor_tensor(m.base[:], m.cumblk[:], m.nblk[:], ALU.subtract))
                own.wait()
                own(nc.vector.tensor_scalar(m.base[:], m.base[:], float(P), None, ALU.mult))
                own(nc.vector.tensor_tensor(c, m.ps[:, 0:2, :].rearrange("p k n -> p (k n)"), m.carry[:, 0:TE], ALU.add))
                own.wait()
                own(nc.vector.tensor_tensor(t3(c), t3(c), bc(m.base[:, None, :], [P, NT, E]), ALU.add))
                own.wait()
                for k in range(TOPK):
                    own(nc.vector.tensor_tensor(onehot[k], onehot[k], c, ALU.mult))
                    own.wait()
                    own(nc.vector.tensor_reduce(m.slotf[:, :, k], t3(onehot[k]), AXX, ALU.add))
                own.wait()
                own(nc.vector.tensor_copy(m.slot[:], m.slotf[:]))
                for half in range(4):
                    n = NBLK // 4
                    v = m.big[:, 0:n * E].rearrange("p (j e) -> p j e", e=E)
                    own.wait()
                    own(nc.vector.tensor_tensor(v, bc(m.cumblk[:, None, :], [P, n, E]), bc(m.iota_j[:, half * n:(half + 1) * n, None], [P, n, E]), ALU.is_le))
                    own.wait()
                    own(nc.vector.tensor_reduce(m.blkf[:, half * n:(half + 1) * n], v, AXX, ALU.add))
                own.wait()
                own(nc.vector.tensor_scalar(m.blk[:], m.blkf[:], float(E - 1), float(WE), ALU.min, ALU.mult))
                own.wait()

            @block.tensor
            def _(pe):
                pe.wait_ge(s["mask_ready"], 1)
                for i in range(2):
                    pe.matmul(m.ps[:, i, :], m.before_bf[:], m.chosen_bf[:, 512 * i:512 * i + 512], start=True, stop=True).then_inc(s["before_done"], 1)
                for i in range(2):
                    pe.matmul(m.ps[:, 2 + i, :], m.ones_bf[:], m.chosen_bf[:, 512 * i:512 * i + 512], start=True, stop=True).then_inc(s["count_done"], 1)

            @block.scalar
            def _(act):
                act.wait_ge(s["own"], 2 * NT + 8)
                nc.scalar.activation(m.gexp[:], m.gatew4[:], ACT.Exp).then_inc(s["exp_ready"], 1)
                act.wait_ge(s["exp_ready"], 1)


def retention(nc, m, a, half):
    names = ("in_ready q_proj k_proj v_proj g_proj squared eg_done ms_ready ln_ready r_ready own own_gate qn_ready kn_ready v_ready g_ready q4_hi k4_hi "
             "q4_ready k4_ready qd_ready kd_ready TQ_done TK_done TD_done TQ_ev TK_ev TD_ev arg_done A_done D_ready At_ready "
             "oT_done oT_ev o_done o_ev kv_done kvm_ready state_ready S_ready rhs_pool osq_done ms16_ready r16_ready on_ready og_ready "
             "TG_done TG_ev wo_done out_done copied rhs_ready added")
    U = TB * 4
    NCP = 3
    QB, KB, VB, GB = range(4)
    TQ, TK, OT, TD = 0, 1, (2, 3), 3
    ARG, SC = (4, 5), (6, 7)
    with semaphores(nc, "cleared") as s, nc.Block() as block:
        @block.vector
        def _(dve):
            for pad in (m.qT_by_head[:].bitcast(F32), m.state_x[:]):
                nc.vector.memset(pad, 0.0).then_inc(s["cleared"], 1)
            dve.wait_ge(s["cleared"], 2)
    with ExitStack() as ctx:
        moved = m.moved
        turn_no = ctx.enter_context(nc.Fori(0, B // 2))
        b = turn_no + half * (B // 2)
        with semaphores(nc, names) as s, nc.Block() as block:
            def t3(ap, n=P):
                return ap.rearrange("p (t n) -> p t n", n=n)

            def heads(ap):
                return ap.rearrange("p (h d) -> p h d", d=DR)

            def tile_heads(buf, t):
                return heads(buf[:, t * P:(t + 1) * P])[:, :, None, :]

            def parts(buf, t):
                return buf[:, t % 2, :].rearrange("p (h r d) -> p h r d", r=4, d=DR)

            eg = m.qdT[:]

            @block.tensor
            def _(pe):
                pe.wait_ge(s["in_ready"], 1)
                for bank, done in ((QB, "q_proj"), (KB, "k_proj"), (VB, "v_proj"), (GB, "g_proj")):
                    for t in range(TB):
                        mm = pe.matmul(m.ps[:, bank, t * P:(t + 1) * P], m.xTs[:, t * P:(t + 1) * P], m.wr[:, bank * P:(bank + 1) * P],
                                       start=True, stop=True)
                    mm.then_inc(s[done], 1)

                def turn(t):
                    pe.wait_ge(s["q4_ready"], t + 1)
                    if t == 0:
                        pe.wait_ge(s["qn_ready"], 1)
                    else:
                        pe.wait_ge(s["TQ_ev"], 4 * t)
                    if t >= 2:
                        pe.wait_ge(s["kvm_ready"], t - 1)
                    for c in range(4):
                        mm = pe.transpose(m.ps[:, TQ, c * P:(c + 1) * P], m.q4[:, t % 2, c * P:(c + 1) * P].bitcast(F32), m.ident[:])
                    mm.then_inc(s["TQ_done"], 1)
                    pe.wait_ge(s["k4_ready"], t + 1)
                    if t == 0:
                        pe.wait_ge(s["kn_ready"], 1)
                    else:
                        pe.wait_ge(s["TK_ev"], t)
                    if t >= 3:
                        pe.wait_ge(s["o_ev"], t - 2)
                    for c in range(4):
                        mm = pe.transpose(m.ps[:, TK, c * P:(c + 1) * P], m.k4[:, t % 2, c * P:(c + 1) * P].bitcast(F32), m.ident[:])
                    mm.then_inc(s["TK_done"], 1)

                def exponents(u):
                    t, c = divmod(u, 4)
                    if u >= 2:
                        pe.wait_ge(s["D_ready"], u - 1)
                    if u % 8 == 0:
                        pe.wait_ge(s[("rhs_ready", "rhs_pool")[t // 2]], 1)
                    row = 64 * (t % 2)
                    pe.matmul(m.ps[:, ARG[u % 2], :], m.ident_bf[:], m.future_bf[:].rearrange("p j i -> p (j i)"), start=True, stop=False)
                    pe.matmul(m.ps[:, ARG[u % 2], :], m.argLs[row:row + 64, t // 2, :], m.argRx[row:row + 64, t // 2, 4 * c:4 * c + 4, :],
                              start=False, stop=True).then_inc(s["arg_done"], 1)

                def scores(u):
                    t, c = divmod(u, 4)
                    if c == 0:
                        pe.wait_ge(s["TQ_ev"], 4 * (t + 1))
                        pe.wait_ge(s["TK_ev"], t + 1)
                    if u >= 2:
                        pe.wait_ge(s["At_ready"], u - 1)
                    pe.matmul(m.ps[:, SC[u % 2], :], m.k4T[:, t % 2, c, :], m.qT_by_head[:, t % 2, c, :, :], start=True, stop=True).then_inc(s["A_done"], 1)

                def out_cross(t):
                    if t == 0:
                        pe.wait_ge(s["v_ready"], 1)
                    if t >= 2:
                        pe.wait_ge(s["oT_ev"], t - 1)
                    if t >= 1:
                        pe.wait_ge(s["S_ready"], t)
                    for c in range(4):
                        pe.matmul(m.ps[:, OT[t % 2], c * P:(c + 1) * P], m.state_x[:, c, :, :].rearrange("p j e -> p (j e)"),
                                  m.qdT[:, t * P:(t + 1) * P], start=(c == 0), stop=False, skip_group_check=True)

                def out_intra(u):
                    t, c = divmod(u, 4)
                    pe.wait_ge(s["At_ready"], u + 1)
                    for j in range(4):
                        v0 = t * P + (4 * c + j) * DR
                        mm = pe.matmul(m.ps[32 * j:32 * j + DR, OT[t % 2], c * P:(c + 1) * P], m.vn[:, v0:v0 + DR], m.At[:, u % NCP, j, :],
                                       start=False, stop=(c == 3), skip_group_check=True)
                    mm.then_inc(s["oT_done"], 1)

                def turn_back(t):
                    pe.wait_ge(s["oT_ev"], t + 1)
                    pe.wait_ge(s["TK_ev"], min(t + 3, TB))
                    if t >= 2:
                        pe.wait_ge(s["o_ev"], t)
                    for c in range(4):
                        mm = pe.transpose(m.ps[:, TK, c * P:(c + 1) * P], m.oT[:, c * P:(c + 1) * P], m.ident[:])
                    mm.then_inc(s["o_done"], 1)

                def update(t):
                    pe.wait_ge(s["TQ_ev"], 4 * (t + 2))
                    pe.matmul(m.ps[:, TQ, 0:P], m.kd[:, t * P:(t + 1) * P], m.vn[:, t * P:(t + 1) * P], start=True, stop=True).then_inc(s["kv_done"], 1)

                exponents(0)
                exponents(1)
                turn(0)
                pe.wait_ge(s["qd_ready"], 1)
                pe.wait_ge(s["g_ready"], 1)
                for t in range(TB):
                    mm = pe.transpose(m.ps[:, TD, t * P:(t + 1) * P], m.qd[:, t * P:(t + 1) * P], m.ident[:])
                mm.then_inc(s["TD_done"], 1)
                scores(0)
                scores(1)
                pe.wait_ge(s["kd_ready"], 1)
                pe.wait_ge(s["TD_ev"], 1)
                for u in range(U):
                    t, c = divmod(u, 4)
                    if u + 2 < U:
                        exponents(u + 2)
                        scores(u + 2)
                    if c == 0:
                        out_cross(t)
                        if t + 1 < TB:
                            turn(t + 1)
                    if c == 2 and t + 1 < TB:
                        update(t)
                    if c == 2 and t >= 1:
                        turn_back(t - 1)
                    out_intra(u)
                turn_back(TB - 1)
                pe.wait_ge(s["og_ready"], 1)
                for t in range(TB):
                    mm = pe.transpose(m.ps[:, TQ, t * P:(t + 1) * P], m.o[:, t * P:(t + 1) * P], m.ident[:])
                mm.then_inc(s["TG_done"], 1)
                pe.wait_ge(s["TG_ev"], 1)
                for t in range(TB):
                    mm = pe.matmul(m.ps[:, TK, t * P:(t + 1) * P], m.qdT[:, t * P:(t + 1) * P], m.wo[:], start=True, stop=True)
                mm.then_inc(s["wo_done"], 1)

            @block.vector
            def _(dve):
                own = Steps(dve, s["own"])
                own(nc.vector.tensor_copy(m.argLs[:], m.argL[:, bass.ds(2 * b, 2), :].bitcast(F32)))
                nc.vector.tensor_tensor(m.argRx[:, 0, :, :], bc(m.argR[:, bass.ds(2 * b, 1), :].bitcast(F32), [P, HR, P]),
                                        bc(m.arg_head[:, :, None], [P, HR, P]), ALU.mult).then_inc(s["rhs_ready"], 1)
                own(nc.vector.tensor_copy(m.e_in_s[:], m.e_in[:, bass.ds(b * TB * HR, TB * HR)]))
                own(nc.vector.tensor_copy(m.e_out_s[:], m.e_out[:, bass.ds(b * TB * HR, TB * HR)]))
                own(nc.vector.tensor_copy(m.decay_s[:], m.decay_tile_e[:, bass.ds(b * TB, TB)]))
                own(nc.vector.memset(m.state[:], 0.0))
                own(nc.vector.memset(m.state_x[:, :, :, 0:DR], 0.0))
                own.wait()
                dve.wait_ge(s["squared"], 2 * TB)
                own(nc.vector.tensor_scalar(m.ms3[:, TB:3 * TB], m.ssq[:, TB:3 * TB], 1.0 / D, RMS_EPS_R, ALU.mult, ALU.add))
                dve.wait_ge(s["squared"], 3 * TB)
                nc.vector.tensor_scalar(m.ms3[:, 0:TB], m.ssq[:, 0:TB], float(DR) / D, DR * RMS_EPS_R, ALU.mult, ALU.add).then_inc(s["ms_ready"], 1)
                dve.wait_ge(s["eg_done"], 1)
                nc.vector.tensor_scalar(eg, eg, 1.0, None, ALU.add).then_inc(s["own_gate"], 1)
                dve.wait_ge(s["own_gate"], 1)
                nc.vector.reciprocal(m.sg[:], eg).then_inc(s["own_gate"], 1)
                dve.wait_ge(s["own_gate"], 2)
                nc.vector.tensor_tensor(m.sg[:], m.ps[:, GB, :], m.sg[:], ALU.mult).then_inc(s["g_ready"], 1)
                dve.wait_ge(s["r_ready"], 1)
                for n, (bank, dst, done) in enumerate(((QB, m.qn, "qn_ready"), (KB, m.kn, "kn_ready"), (VB, m.vn, "v_ready"))):
                    nc.vector.tensor_tensor(t3(dst[:, 0:T]), t3(m.ps[:, bank, :]), bc(m.rr[:, n * TB:(n + 1) * TB, None], [P, TB, P]), ALU.mult).then_inc(s[done], 1)

                def split(t):
                    both = [P, HR, 2, DR]
                    q4, k4 = parts(m.q4, t), parts(m.k4, t)
                    if t >= 2:
                        dve.wait_ge(s["TQ_done"], t - 1)
                        dve.wait_ge(s["TK_done"], t - 1)
                    dve.wait_ge(s["q4_hi"], t + 1)
                    nc.vector.tensor_tensor(q4[:, :, 1:4:2, :], bc(tile_heads(m.qn, t), both), q4[:, :, 0:4:2, :].bitcast(F32), ALU.subtract).then_inc(s["q4_ready"], 1)
                    dve.wait_ge(s["k4_hi"], t + 1)
                    nc.vector.tensor_tensor(k4[:, :, 2:4, :], bc(tile_heads(m.kn, t), both), k4[:, :, 0:2, :].bitcast(F32), ALU.subtract).then_inc(s["k4_ready"], 1)

                split(0)
                nc.vector.tensor_tensor(heads(m.qd[:]), heads(m.qn[:, 0:T]), bc(m.e_in_s[:, :, None], [P, TB * HR, DR]), ALU.mult).then_inc(s["qd_ready"], 1)
                nc.vector.tensor_tensor(heads(m.kd[:]), heads(m.kn[:, 0:T]), bc(m.e_out_s[:, :, None], [P, TB * HR, DR]), ALU.mult).then_inc(s["kd_ready"], 1)
                split(1)

                def k_turned(t):
                    dve.wait_ge(s["TK_done"], t + 1)
                    if t >= 2:
                        dve.wait_ge(s["A_done"], 4 * (t - 1))
                    nc.vector.tensor_copy(m.k4T[:, t % 2, :, :].rearrange("p c i -> p (c i)"), m.ps[:, TK, :]).then_inc(s["TK_ev"], 1)

                def add_choices(t):
                    acc = m.acc[:, bass.ds(turn_no * 2 * TB + t, 1), :].rearrange("p a d -> p (a d)")
                    dve.wait_ge(s["copied"], 2)
                    dve.wait_ge(moved[t], (turn_no + (1 + B // 2)) * (16 * TOPK))
                    for k in range(TOPK):
                        if k >= 1:
                            dve.wait_ge(s["added"], TOPK * t + k)
                        nc.vector.scalar_tensor_tensor(out=acc, in0=m.got[:, TOPK * t + k, :], scalar=m.gw_s[:, t, k:k + 1], in1=acc,
                                                       op0=ALU.mult, op1=ALU.add).then_inc(s["added"], 1)

                def o_turned(t):
                    dve.wait_ge(s["o_done"], t + 1)
                    nc.vector.tensor_copy(heads(m.o[:, t * P:(t + 1) * P]),
                                          m.ps[:, TK, :].rearrange("p (h e) -> p h e", e=32)[:, :, 0:DR]).then_inc(s["o_ev"], 1)

                k_turned(0)
                for u in range(U):
                    t, c = divmod(u, 4)
                    dve.wait_ge(s["A_done"], u + 1)
                    dve.wait_ge(s["D_ready"], u + 1)
                    if u >= NCP:
                        dve.wait_ge(s["oT_done"], u - NCP + 1)
                    nc.vector.tensor_tensor(m.At[:, u % NCP, :, :].rearrange("p j i -> p (j i)"), m.ps[:, SC[u % 2], :],
                                            m.Dm[:, u % 2, :], ALU.mult).then_inc(s["At_ready"], 1)
                    if t + 1 < TB and c == 0:
                        k_turned(t + 1)
                    if t + 2 < TB and c == 3:
                        split(t + 2)
                    if t + 1 < TB and c == 2:
                        dve.wait_ge(s["kv_done"], t + 1)
                        nc.vector.tensor_tensor(m.kvm[:], m.ps[:, TQ, 0:P], m.same_head[:], ALU.mult).then_inc(s["kvm_ready"], 1)
                        dve.wait_ge(s["kvm_ready"], t + 1)
                        if t >= 1:
                            dve.wait_ge(s["S_ready"], t)
                        nc.vector.scalar_tensor_tensor(out=m.state[:], in0=m.state[:], scalar=m.decay_s[:, t:t + 1], in1=m.kvm[:],
                                                       op0=ALU.mult, op1=ALU.add).then_inc(s["state_ready"], 1)
                        dve.wait_ge(s["state_ready"], t + 1)
                        dve.wait_ge(s["oT_done"], 4 * t + 1)
                        nc.vector.tensor_copy(m.state_x[:, :, :, 0:DR], m.state[:].rearrange("p (c j e) -> p c j e", c=4, j=4)).then_inc(s["S_ready"], 1)
                    if t >= 1 and c == 3:
                        o_turned(t - 1)
                    if half == 1 and u >= 5 and u % 2 == 1:
                        add_choices((u - 5) // 2)
                o_turned(TB - 1)
                dve.wait_ge(s["osq_done"], 1)
                own(nc.vector.tensor_reduce(m.ms16[:], heads(m.sq[:]), AXX, ALU.add))
                own.wait()
                nc.vector.tensor_scalar(m.ms16[:], m.ms16[:], 1.0 / DR, RMS_EPS_R, ALU.mult, ALU.add).then_inc(s["ms16_ready"], 1)
                dve.wait_ge(s["r16_ready"], 1)
                nc.vector.tensor_tensor(heads(m.sq[:]), heads(m.o[:]), bc(m.r16[:, :, None], [P, TB * HR, DR]), ALU.mult).then_inc(s["on_ready"], 1)
                dve.wait_ge(s["on_ready"], 1)
                nc.vector.tensor_tensor(m.o[:], m.sq[:], m.sg[:], ALU.mult).then_inc(s["og_ready"], 1)
                if half == 1:
                    add_choices(2 * TB - 2)
                    add_choices(2 * TB - 1)
                dve.wait_ge(s["wo_done"], 1)
                if half == 1:
                    dve.wait_ge(s["added"], 2 * TB * TOPK)
                acc = m.acc[:, bass.ds(b * TB, TB), :]
                nc.vector.tensor_tensor(acc, t3(m.ps[:, TK, :]), acc, ALU.add).then_inc(s["out_done"], 1)
            @block.scalar
            def _(act):
                act.copy(m.xTs[:], m.xT[:, bass.ds(b * T, T)]).then_inc(s["in_ready"], 1)
                for n, (bank, done) in ((2, (VB, "v_proj")), (1, (KB, "k_proj")), (0, (QB, "q_proj"))):
                    act.wait_ge(s[done], 1)
                    for t in range(TB):
                        if n < 2:
                            act.wait_ge(s["squared"], (1 - n) * TB + t + 1)
                        nc.scalar.activation(m.sq[:, t * P:(t + 1) * P], m.ps[:, bank, t * P:(t + 1) * P], ACT.Square,
                                             accum_out=m.ssq[:, n * TB + t:n * TB + t + 1]).then_inc(s["squared"], 1)
                act.wait_ge(s["g_proj"], 1)
                nc.scalar.activation(eg, m.ps[:, GB, :], ACT.Exp, scale=-1.0).then_inc(s["eg_done"], 1)
                act.wait_ge(s["ms_ready"], 1)
                nc.scalar.activation(m.rr[:], m.ms3[:], ACT.Ln).then_inc(s["ln_ready"], 1)
                act.wait_ge(s["ln_ready"], 1)
                nc.scalar.activation(m.rr[:], m.rr[:], ACT.Exp, scale=-0.5).then_inc(s["r_ready"], 1)

                def high_parts(t):
                    both = [P, HR, 2, DR]
                    if t == 0:
                        act.wait_ge(s["qn_ready"], 1)
                    if t >= 2:
                        act.wait_ge(s["TQ_done"], t - 1)
                        act.wait_ge(s["TK_done"], t - 1)
                        act.wait_ge(s["k4_ready"], t - 1)
                    nc.scalar.copy(parts(m.q4, t)[:, :, 0:4:2, :], bc(tile_heads(m.qn, t), both)).then_inc(s["q4_hi"], 1)
                    if t == 0:
                        act.wait_ge(s["kn_ready"], 1)
                    nc.scalar.copy(parts(m.k4, t)[:, :, 0:2, :], bc(tile_heads(m.kn, t), both)).then_inc(s["k4_hi"], 1)

                high_parts(0)
                high_parts(1)

                def decay(u):
                    act.wait_ge(s["arg_done"], u + 1)
                    if u >= 2:
                        act.wait_ge(s["At_ready"], u - 1)
                    nc.scalar.activation(m.Dm[:, u % 2, :], m.ps[:, ARG[u % 2], :], ACT.Exp).then_inc(s["D_ready"], 1)

                def q_turned(t):
                    act.wait_ge(s["TQ_done"], t + 1)
                    if t >= 2:
                        act.wait_ge(s["A_done"], 4 * (t - 1))
                    for j in range(4):
                        rows = slice(32 * j, 32 * j + 32)
                        nc.scalar.copy(m.qT_by_head[rows, t % 2, :, j, :], m.ps[rows, TQ, :].rearrange("p (c i) -> p c i", c=4)).then_inc(s["TQ_ev"], 1)

                def oT_out(t):
                    act.wait_ge(s["oT_done"], 4 * (t + 1))
                    if t >= 1:
                        act.wait_ge(s["o_done"], t)
                    nc.scalar.copy(m.oT[:], m.ps[:, OT[t % 2], :]).then_inc(s["oT_ev"], 1)

                decay(0)
                decay(1)
                q_turned(0)
                act.wait_ge(s["TD_done"], 1)
                nc.scalar.copy(m.qdT[:], m.ps[:, TD, :]).then_inc(s["TD_ev"], 1)
                for u in range(U):
                    if u + 2 < U:
                        decay(u + 2)
                    t, c = divmod(u, 4)
                    if c == 0 and t + 1 < TB:
                        q_turned(t + 1)
                    if c == 1 and t >= 1:
                        oT_out(t - 1)
                    if c == 2 and t + 2 < TB:
                        high_parts(t + 2)
                oT_out(TB - 1)
                act.wait_ge(s["o_ev"], TB)
                act.wait_ge(s["squared"], 3 * TB)
                nc.scalar.activation(m.sq[:], m.o[:], ACT.Square).then_inc(s["osq_done"], 1)
                act.wait_ge(s["ms16_ready"], 1)
                nc.scalar.activation(m.r16[:], m.ms16[:], ACT.Ln).then_inc(s["ln_ready"], 1)
                act.wait_ge(s["ln_ready"], 2)
                nc.scalar.activation(m.r16[:], m.r16[:], ACT.Exp, scale=-0.5).then_inc(s["r16_ready"], 1)
                act.wait_ge(s["TG_done"], 1)
                nc.scalar.copy(m.qdT[:], m.ps[:, TQ, :]).then_inc(s["TG_ev"], 1)

            @block.gpsimd
            def _(pool):
                two = bass.ds(turn_no * 2 * TB, 2 * TB)
                nc.gpsimd.tensor_copy(m.slot_s[:], m.slot[:, two, :]).then_inc(s["copied"], 1)
                if half == 0:
                    nc.gpsimd.tensor_copy(m.rows[:], m.h2[:, two, :]).then_inc(s["copied"], 1)
                else:
                    nc.gpsimd.tensor_copy(m.gw_s[:], m.gatew4[:, two, :]).then_inc(s["copied"], 1)
                pool.wait_ge(s["copied"], 2)
                pool.wait_ge(m.slots_cleared, 16 * 8)

                def move(t):
                    for k in range(TOPK):
                        slots = bass.IndirectOffsetOnAxis(ap=m.slot_s[:, t, k:k + 1], axis=0)
                        if half == 0:
                            ins = pool.indirect_dma_start(a["slots_x"][:, :], slots, m.rows[:, t, :], None)
                        else:
                            ins = pool.indirect_dma_start(m.got[:, TOPK * t + k, :], None, a["slots_y"][:, :], slots)
                        ins.then_inc(moved[t], 16)

                nc.gpsimd.tensor_tensor(m.argRx[:, 1, :, :], bc(m.argR[:, bass.ds(2 * b + 1, 1), :].bitcast(F32), [P, HR, P]),
                                        bc(m.arg_head[:, :, None], [P, HR, P]), ALU.mult).then_inc(s["rhs_pool"], 1)
                for t in range(2 * TB):
                    move(t)
                for t in range(2 * TB):
                    pool.wait_ge(moved[t], (turn_no + (1 + half * (B // 2))) * (16 * TOPK))

            if half == 1:
                @block.sync
                def _(sp):
                    sp.wait_ge(s["added"], 2 * TB * TOPK)
                    sp.wait_ge(s["out_done"], 1)
                    sp.dma_start(a["out"][bass.ds(turn_no * 2, 2), :, :].rearrange("a (t p) d -> p (a t) d", p=P),
                                 m.acc[:, bass.ds(turn_no * 2 * TB, 2 * TB), :]).then_inc(m.stored, 16)


def experts(nc, m, a):
    names = ("x_loaded_0 x_loaded_1 x_loaded_2 x_loaded_3 T_done xT_ready up_done silu_done a_ready TA_done aT_ready down_done y_ready "
             "y_stored_0 y_stored_1 y_stored_2 y_stored_3")
    Q = 4
    NQB = 4
    PAIRS = BPI // 2
    with nc.Fori(0, NBLK // BPI) as i:
        with semaphores(nc, names) as s:
            def dram(t, q):
                return t[bass.ds((i * (BPI // Q) + q) * (Q * P), Q * P), :].rearrange("(r p) n -> p r n", p=P)

            def two(ap, n):
                return ap.rearrange("p (r n) -> p r n", n=n)

            with nc.Block() as block:
                @block.sync
                def _(sp):
                    def load_rows(q):
                        if q >= NQB:
                            sp.wait_ge(s["T_done"], 2 * (q - NQB + 1))
                        sp.dma_start(m.xblk[:, q % NQB, :, :], dram(a["slots_x"], q)).then_inc(s[f"x_loaded_{q % NQB}"], 16)

                    for q in range(NQB):
                        load_rows(q)
                    for q in range(BPI // Q):
                        sp.wait_ge(s["y_ready"], 2 * (q + 1))
                        sp.dma_start(dram(a["slots_y"], q), m.yblk[:, q % NQB, :, :]).then_inc(s[f"y_stored_{q % NQB}"], 16)
                        if q + NQB < BPI // Q:
                            load_rows(q + NQB)
                    for q in range(NQB):
                        sp.wait_ge(s[f"y_stored_{q}"], 16 * len(range(q, BPI // Q, NQB)))

                @block.tensor
                def _(pe):
                    regs = {}

                    def turn(p):
                        q = p // 2
                        if p % 2 == 0:
                            pe.wait_ge(s[f"x_loaded_{q % NQB}"], 16 * (q // NQB + 1))
                        if p >= 2:
                            pe.wait_ge(s["xT_ready"], p - 1)
                        for r in range(2):
                            mm = pe.transpose(m.ps[:, p % 2, r * P:(r + 1) * P], m.xblk[:, q % NQB, 2 * (p % 2) + r, :], m.ident[:])
                        mm.then_inc(s["T_done"], 1)

                    def up(p):
                        pe.wait_ge(s["xT_ready"], p + 1)
                        if p >= 2:
                            pe.wait_ge(s["a_ready"], p - 1)
                        for r in range(2):
                            mm = pe.matmul(m.ps[:, 2 + p % 2, 256 * r:256 * r + 256], m.xTb[:, p % 2, r, :],
                                           m.we[:, bass.ds(regs[p][r], 2 * DFF)], start=True, stop=True)
                        mm.then_inc(s["up_done"], 1)

                    def turn_a(p):
                        pe.wait_ge(s["a_ready"], p + 1)
                        if p >= 2:
                            pe.wait_ge(s["aT_ready"], p - 1)
                        for r in range(2):
                            mm = pe.transpose(m.ps[:, 4 + p % 2, r * P:(r + 1) * P], m.ab[:, p % 2, r, :], m.ident[:])
                        mm.then_inc(s["TA_done"], 1)

                    def down(p):
                        pe.wait_ge(s["aT_ready"], p + 1)
                        if p >= 2:
                            pe.wait_ge(s["y_ready"], p - 1)
                        for r in range(2):
                            mm = pe.matmul(m.ps[:, 6 + p % 2, r * P:(r + 1) * P], m.aTb[:, p % 2, r, :],
                                           m.we[:, bass.ds(regs[p][r] + 2 * DFF, D)], start=True, stop=True)
                        mm.then_inc(s["down_done"], 1)
                        regs.pop(p)

                    def numbers(p):
                        _, values = nc.values_load_multi_w_load_instructions(
                            m.blk[0:1, bass.ds(i * BPI + 2 * p, 8)], engines=(mybir.EngineType.PE,), min_val=0, max_val=(E - 1) * WE)
                        for n in range(4):
                            regs[p + n] = values[2 * n:2 * n + 2]

                    numbers(0)
                    turn(0)
                    turn(1)
                    up(0)
                    turn(2)
                    up(1)
                    for p in range(PAIRS):
                        turn_a(p)
                        if p + 2 < PAIRS:
                            up(p + 2)
                        if p + 3 < PAIRS:
                            turn(p + 3)
                        down(p)
                        if p % 4 == 0 and p + 4 < PAIRS:
                            numbers(p + 4)

                @block.scalar
                def _(act):
                    def x_turned(p):
                        act.wait_ge(s["T_done"], p + 1)
                        if p >= 2:
                            act.wait_ge(s["up_done"], p - 1)
                        nc.scalar.copy(m.xTb[:, p % 2, :, :], two(m.ps[:, p % 2, 0:2 * P], P)).then_inc(s["xT_ready"], 1)

                    x_turned(0)
                    x_turned(1)
                    for p in range(PAIRS):
                        act.wait_ge(s["up_done"], p + 1)
                        if p >= 2:
                            act.wait_ge(s["a_ready"], p - 1)
                        nc.scalar.activation(m.sl[:, p % 2, :, :], two(m.ps[:, 2 + p % 2, :], 2 * DFF)[:, :, DFF:], ACT.Silu).then_inc(s["silu_done"], 1)
                        if p + 2 < PAIRS:
                            x_turned(p + 2)

                @block.vector
                def _(dve):
                    def a_turned(p):
                        dve.wait_ge(s["TA_done"], p + 1)
                        if p >= 2:
                            dve.wait_ge(s["down_done"], p - 1)
                        nc.vector.tensor_copy(m.aTb[:, p % 2, :, :], two(m.ps[:, 4 + p % 2, 0:2 * P], P)).then_inc(s["aT_ready"], 1)

                    def y_out(p):
                        q = p // 2
                        dve.wait_ge(s["down_done"], p + 1)
                        if q >= NQB and p % 2 == 0:
                            dve.wait_ge(s[f"y_stored_{q % NQB}"], 16 * (q // NQB))
                        nc.vector.tensor_copy(m.yblk[:, q % NQB, 2 * (p % 2):2 * (p % 2) + 2, :], two(m.ps[:, 6 + p % 2, 0:2 * P], P)).then_inc(s["y_ready"], 1)

                    for p in range(PAIRS):
                        dve.wait_ge(s["silu_done"], p + 1)
                        if p >= 2:
                            dve.wait_ge(s["TA_done"], p - 1)
                        nc.vector.tensor_tensor(m.ab[:, p % 2, :, :], two(m.ps[:, 2 + p % 2, :], 2 * DFF)[:, :, 0:DFF], m.sl[:, p % 2, :, :], ALU.mult).then_inc(s["a_ready"], 1)
                        a_turned(p)
                        if p >= 1:
                            y_out(p - 1)
                    y_out(PAIRS - 1)


class Memory(dict):
    __getattr__ = dict.__getitem__


def program(nc, a):
    with ExitStack() as whole:
        m = Memory(names=[])

        def sb(ctx, **shapes):
            for name, shape in shapes.items():
                dt = F32
                if isinstance(shape, tuple):
                    shape, dt = shape
                m[name] = ctx.enter_context(nc.sbuf_tensor(f"{name}_{len(m.names)}", [P] + shape, dt))
                m.names.append(name)

        m["ps"] = whole.enter_context(nc.psum_tensor("ps", [P, 8, 512], F32))
        m["slots_cleared"] = whole.enter_context(nc.semaphore("slots_cleared"))
        m["stored"] = whole.enter_context(nc.semaphore("stored"))
        m["moved"] = [whole.enter_context(nc.semaphore(f"moved_{n}")) for n in range(2 * TB)]
        sb(whole, acc=[NT, D], xT=[NT * P], h2=[NT + TB, D], wr=[512], wo=[D],
           ident=[P], ident_bf=([P], BF16), future_bf=([4, P], BF16), before_bf=([P], BF16), ones_bf=([P], BF16),
           same_head=[P], arg_head=[HR], minus_half=[TB * HR], tot_ones=[P],
           e_in=[NT * HR], e_out=[NT * HR], decay_tile_e=[NT], argL=([2 * B, P], F32R), argR=([2 * B, P], F32R),
           logit=[NT * E], gatew4=[NT, TOPK], slot=([NT, TOPK], I32), blk=([NBLK], I32),
           zero=[D], wn=[2], xTs=[T], sq=[512], ssq=[3 * TB], ms3=[3 * TB])
        m["hT"] = m.h2[:].rearrange("p t d -> p (t d)")
        with ExitStack() as c1:
            sb(c1, xn=[NT, D], wqk=[NCH, P], wv=[KV * DH], vb=[KV * DH], projw=[8, D], projb=[D],
               gateb=[E], gatew=[E], sink=[H], sink8=[H], qkb=[NCH], rope_cos=[T], rope_sin=[T], window=[2 * P], hTs=[T])
            with ExitStack() as c2:
                sb(c2, wgt=[HR], qkvw=[(H + 2 * KV) * DH], future=[P], upto=[P], after=[P], before=[P],
                   row_head=[HR], arg_rows=[4],
                   stats=[TB, 6], meanvar=[TB, 2], ve=[16], r1=[TB], r2=[TB], xs=[TB, D], hs=[TB, D], z=[NT * HR])
                load(nc, m, a)
                normalise(nc, m)
                with ExitStack() as c3:
                    sb(c3, gt=[NT * HR], bc4=([NT, 4 * HR], F32R), decay_tile=[NT])
                    gates(nc, m)
            with ExitStack() as c2:
                sb(c2, qk=[2, NCH, T], raw=[2, T], swapped=[2, T], v=[2, TB, KV * DH], prob=[3, HG, 2 * P], probT=[2, HG, 2, P],
                   mx=[2, HG], negmx=[2, HG], sinkm=[2, HG], esink=[2, HG], rowsum=[2, HG], den=[2, HG], rden=[2, HG],
                   yT=[2, 2 * KV, P], tx=[D], x2=[D], h2s=[D], h2Ts=[P], r3=[TB])
                attention(nc, m)
        sb(whole, we=[E * WE])
        w3 = m.we[:].rearrange("p (e f) -> p e f", f=WE)
        with ExitStack() as c1:
            sb(c1, top8=[NT, 8], idx8=([NT, 8], U32), idxf=[NT, TOPK], big=[6 * NT * E], chosen_bf=([NT * E], BF16), gexp=[NT, TOPK],
               gsum=[NT], grec=[NT], carry=[(NT + 1) * E], nblk=[E], cumblk=[E], base=[E], slotf=[NT, TOPK], blkf=[NBLK],
               iota_e=[E], iota_blk=[NT], iota_j=[NBLK], upto_e=[E, E])
            with semaphores(nc, "tables down up scaled") as s, nc.Block() as block:
                @block.sync
                def _(sp):
                    for e0 in range(0, E, 8):
                        sp.dma_start(w3[:, e0:e0 + 8, 0:2 * DFF], a["W_up"][e0:e0 + 8].rearrange("e p f -> p e f")).then_inc(s["up"], 16)
                    for n, name in enumerate(ROUTING_TABLES):
                        row = a[name].rearrange("(o n) -> o n", o=1).partition_broadcast(P)
                        dst = m[name][:].rearrange("p a b -> p (a b)") if name == "upto_e" else m[name][:]
                        sp.dma_start(dst, row).then_inc(s["tables"], 16)
                    sp.wait_ge(s["tables"], 16 * len(ROUTING_TABLES))

                @block.scalar
                def _(act):
                    act.dma_start(w3[:, :, 2 * DFF:], a["W_down"].rearrange("e p f -> p e f")).then_inc(s["down"], 16)
                    act.wait_ge(s["down"], 16)

                @block.vector
                def _(dve):
                    dve.wait_ge(s["up"], 16 * 4)
                    nc.vector.tensor_scalar(w3[:, :, 0:2 * DFF], w3[:, :, 0:2 * DFF], m.wn[:, 1:2], None, ALU.mult).then_inc(s["scaled"], 1)
                    dve.wait_ge(s["scaled"], 1)
            routing(nc, m)
        def retention_half(half):
            with ExitStack() as c1:
                sb(c1, state=[P], e_in_s=[TB * HR], e_out_s=[TB * HR], decay_s=[TB], argLs=([2, P], F32R), argRx=([2, HR, P], F32R),
                   state_x=[4, 4, 32], sg=[T], vn=[T], qd=[T], kd=[T], q4=([2, 512], F32R), k4=([2, 512], F32R),
                   qT_by_head=([2, 4, 4, P], F32R), k4T=([2, 4, P], F32R), qdT=[T], At=[3, 4, P], Dm=[2, 512], kvm=[P], ms16=[TB * HR],
                   r16=[TB * HR], rr=[3 * TB], rows=[2 * TB, D], slot_s=([2 * TB, TOPK], I32), gw_s=[2 * TB, TOPK])
                m["qn"], m["kn"] = m.logit[:, 0:T], m.logit[:, T:2 * T]
                m["oT"] = m.h2[:, NT:, :].rearrange("p t d -> p (t d)")
                m["o"] = m.qd
                retention(nc, m, a, half)

        retention_half(0)
        with ExitStack() as c1:
            sb(c1, xblk=[4, 4, D], yblk=[4, 4, D], xTb=[2, 2, P], sl=[2, 2, DFF], ab=[2, 2, DFF], aTb=[2, 2, P])
            experts(nc, m, a)
        m["got"] = m.h2
        retention_half(1)
        with nc.Block() as block:
            @block.sync
            def _(sp):
                sp.wait_ge(m.stored, 16 * (B // 2))


ROUTING_TABLES = ["iota_e", "iota_blk", "iota_j", "upto_e"]


def routing_tables():
    e = np.arange(E)
    return {
        "iota_e": e.astype(np.float32),
        "iota_blk": (P * np.arange(NT)).astype(np.float32),
        "iota_j": np.arange(NBLK, dtype=np.float32),
        "upto_e": (e[None, :] <= e[:, None]).astype(np.float32).reshape(-1),
    }


ATTN = ["x", "Wq", "Wk", "Wv", "Wg", "Wgt", "Wo"]
FFN = ["attn_norm_w", "ffn_norm_w", "qkv_w", "qkv_b", "proj_w", "proj_b", "attn_sink", "gate_w", "gate_b", "W_up", "W_down"]


def kernel(**inputs):
    import concourse.bacc as _bacc
    from concourse.bass_utils import run_bass_kernel_spmd as _run

    nc = _bacc.Bacc("TRN2", target_bir_lowering=False, num_devices=1)
    given = {n: inputs["L0_attn_" + n] for n in ATTN} | {n: inputs["L0_ffn_" + n] for n in FFN} | tables() | routing_tables()
    arrays, aps = {}, {}
    for name, value in given.items():
        v = np.ascontiguousarray(value)
        arrays[f"in_{name}"] = v
        aps[name] = nc.dram_tensor(f"in_{name}", v.shape, mybir.dt.from_np(v.dtype), kind="ExternalInput").ap()
    aps["slots_x"] = nc.dram_tensor("slots_x", (SLOTS, D), F32, kind="Internal").ap()
    aps["slots_y"] = nc.dram_tensor("slots_y", (SLOTS, D), F32, kind="Internal").ap()
    aps["out"] = nc.dram_tensor("out", (B, T, D), F32, kind="ExternalOutput").ap()
    program(nc, aps)
    r = _run(nc, [arrays], core_ids=[0])
    return r.results[0]["out"]
```

```python
from contextlib import ExitStack, contextmanager

import numpy as np

import concourse.bass as bass
from concourse import mybir

F32 = mybir.dt.float32
F32R = mybir.dt.float32r
BF16 = mybir.dt.bfloat16
I32 = mybir.dt.int32
U32 = mybir.dt.uint32
ALU = mybir.AluOpType
ACT = mybir.ActivationFunctionType
AXX = mybir.AxisListType.X

P = 128
B, T, D = 8, 512, 128
TB = T // P
NT = B * TB
LN_EPS = 1e-5
RMS_EPS_R = 1e-6
RMS_EPS_F = 1e-5
HR, DR = 16, 8
H, KV, DH = 16, 4, 64
HG = H // KV
NQ = H // 2
NCH = NQ + KV // 2
E, TOPK, DFF = 32, 4, 128
WE = 2 * DFF + D
NBLK = (B * T * TOPK + E * (P - 1)) // P + 1
BPI = 80
NBLK = -(-NBLK // BPI) * BPI
SLOTS = NBLK * P
NEG = -1e30
NEG_R = -30000.0


def bc(ap, shape):
    return ap.to_broadcast(shape)


class Steps:

    def __init__(self, eng, sem):
        self.eng, self.sem, self.n = eng, sem, 0

    def __call__(self, ins):
        self.n += 1
        ins.then_inc(self.sem, 1)
        return self.n

    def wait(self, n=None):
        self.eng.wait_ge(self.sem, self.n if n is None else n)


@contextmanager
def semaphores(nc, names):
    with ExitStack() as ctx:
        s = {n: ctx.enter_context(nc.semaphore(n)) for n in names.split()}
        yield s
        for q in s.values():
            nc.gpsimd.sem_clear(q)
        nc.all_engine_barrier()


def load(nc, m, a):
    names = "loaded_x loaded_first zeroed filled"
    with semaphores(nc, names) as s, nc.Block() as block:
        @block.sync
        def _(sp):
            n = 4
            for i in range(n):
                tiles = slice(i * NT // n, (i + 1) * NT // n)
                sp.dma_start(m.acc[:, tiles, :], a["x"].rearrange("b (t p) d -> p (b t) d", p=P)[:, tiles, :]).then_inc(s["loaded_x"], 16)
            for src, dst in ((a["Wgt"], m.wgt[:]), (a["ident"], m.ident[:])):
                sp.dma_start(dst, src).then_inc(s["loaded_first"], 16)
            for name in TABLES[1:]:
                sp.dma_start(m[name][:], a[name]).then_inc(m.tables_loaded, 16)
            sp.wait_ge(s["zeroed"], 2)
            rows = NBLK // 8
            for i in range(8):
                sp.dma_start(a["slots_x"][i * rows * P:(i + 1) * rows * P, :].rearrange("(r p) n -> p r n", p=P),
                             bc(m.zero[:, None, :], [P, rows, D])).then_inc(m.slots_cleared, 16)
            sp.wait_ge(s["loaded_x"], 16 * n)
            sp.wait_ge(s["loaded_first"], 16 * 2)

        @block.scalar
        def _(act):
            for src, dst in weight_loads(m, a):
                act.dma_start(dst, src, allow_slow_non_contiguous=True).then_inc(m.weights_loaded, 16)

        @block.gpsimd
        def _(pool):
            nc.gpsimd.memset(m.zero[:], 0.0).then_inc(s["zeroed"], 1)
            nc.gpsimd.memset(m.h2[:, NT:, :], 0.0).then_inc(s["zeroed"], 1)

        @block.vector
        def _(dve):
            nc.vector.memset(m.tot_ones[:], 1.0).then_inc(s["filled"], 1)
            nc.vector.memset(m.minus_half[:], -0.5).then_inc(s["filled"], 1)
            nc.vector.memset(m.ones_bf[:], 1.0).then_inc(s["filled"], 1)
            dve.wait_ge(s["filled"], 3)


def weight_loads(m, a):
    def column(v):
        return v.rearrange("(p o) -> p o", o=1)

    def every_row(v):
        return v.rearrange("(o n) -> o n", o=1).partition_broadcast(P)

    q_b = a["qkv_b"][0:H * DH].rearrange("(pair h j r) -> h r pair j", pair=KV // 2, h=2, j=HG)
    k_b = a["qkv_b"][H * DH:H * DH + KV * DH].rearrange("(pair h r) -> h r pair", pair=KV // 2, h=2)
    yield column(a["attn_norm_w"]), m.wn[:, 0:1]
    yield column(a["ffn_norm_w"]), m.wn[:, 1:2]
    yield a["qkv_w"], m.qkvw[:]
    for h in range(2):
        rows = slice(DH * h, DH * h + DH)
        for pair in range(KV // 2):
            yield q_b[h][:, pair, :], m.qkb[rows, pair * HG:(pair + 1) * HG]
        yield k_b[h], m.qkb[rows, NQ:]
    yield every_row(a["qkv_b"][H * DH + KV * DH:]), m.vb[:]
    yield every_row(a["proj_b"]), m.projb[:]
    yield every_row(a["gate_b"]), m.gateb[:]
    yield every_row(a["attn_sink"]), m.sink[:]
    yield a["gate_w"], m.gatew[:]
    for h in range(2):
        for j in range(2):
            yield (a["proj_w"].rearrange("(g h j r) n -> h j r g n", g=KV, h=2, j=2)[h, j],
                   m.projw[DH * h:DH * h + DH, j::2, :])
    for n, name in enumerate(("Wq", "Wk", "Wv", "Wg")):
        yield a[name], m.wr[:, n * P:(n + 1) * P]
    yield a["Wo"], m.wo[:]


def fold(nc, m, a):
    with semaphores(nc, "own") as s, nc.Block() as block:
        @block.vector
        def _(dve):
            own = Steps(dve, s["own"])
            dve.wait_ge(m.tables_loaded, 16 * (len(TABLES) - 1))
            own(nc.vector.tensor_copy(m.ident_bf[:], m.ident[:]))
            own(nc.vector.tensor_copy(m.future_bf[:], bc(m.future[:, None, :], [P, 4, P])))
            own(nc.vector.tensor_copy(m.before_bf[:], m.before[:]))
            dve.wait_ge(m.weights_loaded, 16 * len(list(weight_loads(m, a))))
            w, g = m.qkvw, m.wn[:, 0:1]
            for half in range(2):
                cols = slice(DH * half, DH * half + DH)
                for pair in range(KV // 2):
                    c0 = (2 * pair + half) * HG * DH
                    own(nc.vector.tensor_scalar(m.wqk[:, pair * HG:(pair + 1) * HG, cols],
                                                w[:, c0:c0 + HG * DH].rearrange("p (j r) -> p j r", j=HG), g, None, ALU.mult))
                keys = w[:, H * DH:(H + KV) * DH].rearrange("p (pair h r) -> p pair h r", pair=KV // 2, h=2)
                own(nc.vector.tensor_scalar(m.wqk[:, NQ:, cols], keys[:, :, half, :], g, None, ALU.mult))
            own(nc.vector.tensor_scalar(m.wv[:], w[:, (H + KV) * DH:], g, None, ALU.mult))
            own(nc.vector.tensor_scalar(m.gatew[:], m.gatew[:], m.wn[:, 1:2], None, ALU.mult))
            own(nc.vector.tensor_scalar(m.sink8[:], m.sink[:], float(DH) ** 0.5, None, ALU.mult))
            own.wait()


def head_place(g, j):
    return (g // 2) * HG + j, DH * (g % 2)


def normalise(nc, m):
    NB = 2 * TB
    with nc.Fori(0, NT // NB) as b:
        with semaphores(nc, "ve_ready r1_ready ms_ready r2_ready xn_ready h_ready own xn_T h_T xT_ready z_done ev") as s:
            tiles = bass.ds(b * NB, NB)
            with nc.Block() as block:
                @block.vector
                def _(dve):
                    own = Steps(dve, s["own"])
                    for t in range(NB):
                        own(nc.vector.bn_stats(m.stats[:, t, :], m.acc[:, bass.ds(b * NB + t, 1), :].rearrange("p a d -> p (a d)")))
                    for t in range(NB):
                        own.wait(t + 1)
                        own(nc.vector.bn_aggr(m.meanvar[:, t, :], m.stats[:, t, :]))
                    own.wait()
                    nc.vector.tensor_scalar(m.ve[:, 0:NB], m.meanvar[:, :, 1], LN_EPS, None, ALU.add).then_inc(s["ve_ready"], 1)
                    dve.wait_ge(s["r1_ready"], 1)
                    own(nc.vector.tensor_tensor(m.ve[:, NB:2 * NB], m.meanvar[:, :, 1], m.r1[:, 0:NB], ALU.mult))
                    own.wait()
                    own(nc.vector.tensor_tensor(m.ve[:, 2 * NB:3 * NB], m.ve[:, NB:2 * NB], m.r1[:, 0:NB], ALU.mult))
                    own.wait()
                    nc.vector.tensor_scalar(m.ve[:, 3 * NB:4 * NB], m.ve[:, 2 * NB:3 * NB], RMS_EPS_F, None, ALU.add).then_inc(s["ms_ready"], 1)
                    for t in range(NB):
                        nc.vector.tensor_scalar(m.xs[:, t, :], m.acc[:, bass.ds(b * NB + t, 1), :].rearrange("p a d -> p (a d)"),
                                                m.meanvar[:, t, 0:1], m.r1[:, t:t + 1],
                                                ALU.subtract, ALU.mult).then_inc(s["xn_ready"], 1)
                    dve.wait_ge(s["r2_ready"], 1)
                    dve.wait_ge(s["xn_ready"], NB)
                    for t in range(NB):
                        nc.vector.tensor_scalar(m.hs[:, t, :], m.xs[:, t, :], m.r2[:, t:t + 1], None,
                                                ALU.mult).then_inc(s["h_ready"], 1)
                    own(nc.vector.tensor_copy(m.xn[:, tiles, :], m.xs[:]))
                    dve.wait_ge(s["h_T"], 1)
                    own(nc.vector.tensor_copy(m.hT[:, bass.ds(b * NB * P, NB * P)], m.ps[:, 2:4, :].rearrange("p k n -> p (k n)")))
                    dve.wait_ge(s["z_done"], 1)
                    own(nc.vector.tensor_copy(m.z[:, bass.ds(b * NB * HR, NB * HR)], m.ps[:, 4, 0:NB * HR]))

                @block.gpsimd
                def _(pool):
                    pool.wait_ge(s["ve_ready"], 1)
                    nc.gpsimd.tensor_tensor(m.r1[:, 0:NB], m.ve[:, 0:NB], m.minus_half[:, 0:NB], ALU.pow).then_inc(s["r1_ready"], 1)
                    pool.wait_ge(s["ms_ready"], 1)
                    nc.gpsimd.tensor_tensor(m.r2[:, 0:NB], m.ve[:, 3 * NB:4 * NB], m.minus_half[:, 0:NB], ALU.pow).then_inc(s["r2_ready"], 1)

                @block.tensor
                def _(pe):
                    for t in range(NB):
                        pe.wait_ge(s["xn_ready"], t + 1)
                        mm = pe.transpose(m.ps[:, t // 4, t % 4 * P:(t % 4 + 1) * P], m.xs[:, t, :], m.ident[:])
                    mm.then_inc(s["xn_T"], 1)
                    for t in range(NB):
                        pe.wait_ge(s["h_ready"], t + 1)
                        mm = pe.transpose(m.ps[:, 2 + t // 4, t % 4 * P:(t % 4 + 1) * P], m.hs[:, t, :], m.ident[:])
                    mm.then_inc(s["h_T"], 1)
                    pe.wait_ge(s["xT_ready"], 1)
                    for t in range(NB):
                        mm = pe.matmul(m.ps[:, 4, t * HR:(t + 1) * HR], m.xT2[:, t * P:(t + 1) * P], m.wgt[:], start=True, stop=True)
                    mm.then_inc(s["z_done"], 1)

                @block.scalar
                def _(act):
                    act.wait_ge(s["xn_T"], 1)
                    act.copy(m.xT2[:], m.ps[:, 0:2, :].rearrange("p k n -> p (k n)")).then_inc(s["xT_ready"], 1)
                    act.wait_ge(s["xT_ready"], 1)
                    act.copy(m.xT[:, bass.ds(b * NB * P, NB * P)], m.xT2[:]).then_inc(s["ev"], 1)


def gates(nc, m):
    with semaphores(nc, "dve e_ready l_ready g_ready bc_done rem_done tot_done exps parts_ready T_done T_free") as s:
        with nc.Block() as block:
            NC = NT * HR
            @block.vector
            def _(dve):
                own = Steps(dve, s["dve"])
                a1, a2, a3 = (buf[:, 0:NT * HR] for buf in (m.xs.rearrange("p t d -> p (t d)"), m.hs.rearrange("p t d -> p (t d)"), m.xT2))
                own(nc.vector.scalar_tensor_tensor(out=a1, in0=m.z[:], scalar=-1.0, in1=m.z[:], op0=ALU.mult, op1=ALU.min))
                dve.wait_ge(s["e_ready"], 1)
                dve.wait_ge(s["l_ready"], 1)
                own(nc.vector.scalar_tensor_tensor(out=a1, in0=m.z[:], scalar=0.0, in1=a3, op0=ALU.min, op1=ALU.subtract))
                own.wait()
                nc.vector.tensor_scalar(m.gt[:], a1, 1.0 / 16.0, None, ALU.mult).then_inc(s["g_ready"], 1)
                dve.wait_ge(s["bc_done"], 1)
                parts = m.bc4[:, :, :].rearrange("p t (k h) -> p t k h", k=4)
                bcv = m.ps[:, 0, :].rearrange("p (t h) -> p t h", h=HR)
                own(nc.vector.tensor_copy(parts[:, :, 0, :], bcv))
                own.wait()
                own(nc.vector.tensor_tensor(parts[:, :, 1, :], bcv, parts[:, :, 0, :].bitcast(F32), ALU.subtract))
                own.wait()
                own(nc.vector.tensor_scalar(parts[:, :, 2, :], parts[:, :, 0, :].bitcast(F32), -1.0, None, ALU.mult))
                nc.vector.tensor_scalar(parts[:, :, 3, :], parts[:, :, 1, :].bitcast(F32), -1.0, None, ALU.mult).then_inc(s["parts_ready"], 1)
                dve.wait_ge(s["tot_done"], 1)
                own(nc.vector.tensor_tensor(a2.rearrange("p (t h) -> p t h", h=HR), m.ps[:, 2, :].rearrange("p (t h) -> p t h", h=HR),
                                            bc(m.row_head[:, None, :], [P, NT, HR]), ALU.mult))
                own.wait()
                own(nc.vector.tensor_reduce(m.decay_tile[:], a2.rearrange("p (t h) -> p t h", h=HR), AXX, ALU.add))
                for q in range(4):
                    dve.wait_ge(s["T_done"], q + 1)
                    own(nc.vector.tensor_scalar(m.argL[:, 4 * q:4 * q + 4, :], m.ps[:, 4 + q % 2, :].rearrange("p (q i) -> p q i", i=P),
                                                m.arg_rows[:, 0:1], m.arg_rows[:, 1:2], ALU.mult, ALU.add))
                    nc.vector.tensor_scalar(m.argR[:, 4 * q:4 * q + 4, :], m.ps[:, 4 + q % 2, :].rearrange("p (q i) -> p q i", i=P),
                                            m.arg_rows[:, 2:3], m.arg_rows[:, 3:4], ALU.mult, ALU.add).then_inc(s["T_free"], 1)

            @block.tensor
            def _(pe):
                pe.wait_ge(s["g_ready"], 1)
                pe.matmul(m.ps[:, 0, :], m.upto[:], m.gt[:], start=True, stop=True).then_inc(s["bc_done"], 1)
                pe.matmul(m.ps[:, 1, :], m.after[:], m.gt[:], start=True, stop=True).then_inc(s["rem_done"], 1)
                pe.matmul(m.ps[:, 2, :], m.tot_ones[:], m.gt[:], start=True, stop=True).then_inc(s["tot_done"], 1)
                pe.wait_ge(s["parts_ready"], 1)
                pe.wait_ge(s["dve"], 5)
                for q in range(4):
                    if q >= 2:
                        pe.wait_ge(s["T_free"], q - 1)
                    for i in range(4):
                        pair = m.bc4[:, 2 * (4 * q + i):2 * (4 * q + i) + 2, :].rearrange("p t k -> p (t k)")
                        mm = pe.transpose(m.ps[:, 4 + q % 2, i * P:(i + 1) * P], pair.bitcast(F32), m.ident[:])
                    mm.then_inc(s["T_done"], 1)

            @block.scalar
            def _(act):
                a1, a2, a3 = (buf[:, 0:NT * HR] for buf in (m.xs.rearrange("p t d -> p (t d)"), m.hs.rearrange("p t d -> p (t d)"), m.xT2))
                act.wait_ge(s["dve"], 1)
                act.activation(a2, a1, ACT.Exp).then_inc(s["e_ready"], 1)
                act.wait_ge(s["e_ready"], 1)
                act.activation(a3, a2, ACT.Ln, bias=1.0).then_inc(s["l_ready"], 1)
                act.wait_ge(s["bc_done"], 1)
                act.wait_ge(s["parts_ready"], 1)
                act.activation(m.e_in[:], m.ps[:, 0, :], ACT.Exp).then_inc(s["exps"], 1)
                act.wait_ge(s["rem_done"], 1)
                act.activation(m.e_out[:], m.ps[:, 1, :], ACT.Exp).then_inc(s["exps"], 1)
                act.wait_ge(s["dve"], 7)
                act.activation(m.decay_tile_e[:], m.decay_tile[:], ACT.Exp).then_inc(s["exps"], 1)


TABLES = ["ident", "rope_cos", "rope_sin", "window", "future", "upto", "after", "before",
          "row_head", "same_head", "arg_rows", "arg_head"]


def tables():
    i, j = np.arange(P)[:, None], np.arange(P)[None, :]
    f = np.float32
    inv = (f(1.0) / f(150000.0) ** (np.arange(0, DH, 2, dtype=f) / f(DH))).astype(f)
    freqs = (np.arange(T, dtype=f) / f(32.0))[None, :] * inv[:, None]
    rep = (np.arange(P) % DH) // 2
    sign = np.where(np.arange(P) % 2 == 0, f(-1), f(1))[:, None]
    rows = np.arange(P) % 64
    return {
        "ident": np.eye(P, dtype=f),
        "rope_cos": np.cos(freqs).astype(f)[rep],
        "rope_sin": (np.sin(freqs).astype(f)[rep] * sign).astype(f),
        "window": np.concatenate([np.where(j >= i, 0, NEG), np.where(j <= i, 0, NEG)], 1).astype(f),
        "future": np.where(j < i, NEG_R, 0).astype(f),
        "upto": (i <= j).astype(f),
        "after": (i > j).astype(f),
        "before": (i < j).astype(f),
        "row_head": (i // DR == np.arange(HR)[None, :]).astype(f),
        "same_head": (i // DR == j // DR).astype(f),
        "arg_rows": np.stack([rows >= 32, rows < 32, rows < 32, rows >= 32], 1).astype(f),
        "arg_head": (np.arange(P)[:, None] % HR == np.arange(HR)[None, :]).astype(f),
    }


PREP = [("qk", n) for n in (NQ, *range(HG), NQ + 1, *range(HG, NQ))] + [("v", 0), ("v", 1)]
NP = len(PREP)


def is_rope(k):
    return PREP[k % NP][0] == "qk"


def rope_count(k):
    return sum(is_rope(i) for i in range(k))


def prepare_products(nc, m, pe, s, k, bank, banks):
    kind, n = PREP[k % NP]
    if k >= banks:
        if PREP[(k - banks) % NP][0] == "qk":
            pe.wait_ge(s["raw_ready"], rope_count(k - banks + 1))
        else:
            pe.wait_ge(s["v_ready"], k - banks + 1 - rope_count(k - banks + 1))
    if kind == "qk":
        mm = pe.matmul(m.ps[:, bank, :], m.wqk[:, n, :], m.hTs[:], start=True, stop=True)
    else:
        for i in range(2):
            t = 2 * n + i
            mm = pe.matmul(m.ps[:, bank, i * 256:(i + 1) * 256], m.hTs[:, t * P:(t + 1) * P], m.wv[:], start=True, stop=True)
    mm.then_inc(s["prep_done"], 1)


def prepare_raw(nc, m, act, s, k, bank):
    kind, n = PREP[k % NP]
    if kind == "qk":
        r = rope_count(k)
        act.wait_ge(s["prep_done"], k + 1)
        if r >= 2:
            act.wait_ge(s["cos_ready"], r - 1)
            act.wait_ge(s["sin_ready"], r - 1)
        nc.scalar.activation(m.raw[:, r % 2, :], m.ps[:, bank, :], ACT.Identity, bias=m.qkb[:, n:n + 1]).then_inc(s["raw_ready"], 1)


def prepare_swapped(nc, m, sp, s, r):
    sp.wait_ge(s["raw_ready"], r + 1)
    if r >= 2:
        sp.wait_ge(s["roped"], r - 1)
    for odd in range(2):
        sp.dma_start(m.swapped[1 - odd:P:2, r % 2, :], m.raw[odd:P:2, r % 2, :]).then_inc(s[f"swapped_{r % 2}"], 16)


def prepare_sin(nc, m, pool, s, r):
    pool.wait_ge(s[f"swapped_{r % 2}"], 32 * (r // 2 + 1))
    nc.gpsimd.tensor_tensor(m.swapped[:, r % 2, :], m.swapped[:, r % 2, :], m.rope_sin[:], ALU.mult).then_inc(s["sin_ready"], 1)


def prepare_cos(nc, m, dve, s, k, bank, buf):
    kind, n = PREP[k % NP]
    if kind == "qk":
        dve.wait_ge(s["raw_ready"], rope_count(k + 1))
        nc.vector.tensor_tensor(m.qk[:, buf, n, :], m.raw[:, rope_count(k) % 2, :], m.rope_cos[:], ALU.mult).then_inc(s["cos_ready"], 1)
    else:
        dve.wait_ge(s["prep_done"], k + 1)
        nc.vector.tensor_tensor(m.v[:, buf, 2 * n:2 * n + 2, :], m.ps[:, bank, :].rearrange("p (t c) -> p t c", t=2),
                                bc(m.vb[:, None, :], [P, 2, KV * DH]), ALU.add).then_inc(s["v_ready"], 1)


def prepare_sum(nc, m, dve, s, k, buf):
    kind, n = PREP[k % NP]
    if kind == "qk":
        r = rope_count(k)
        dve.wait_ge(s["cos_ready"], r + 1)
        dve.wait_ge(s["sin_ready"], r + 1)
        out = m.qk[:, buf, n, :]
        nc.vector.tensor_tensor(out, out, m.swapped[:, r % 2, :], ALU.add).then_inc(s["roped"], 1)


PREP_NAMES = "hs_ready prep_done raw_ready swapped_0 swapped_1 sin_ready cos_ready roped v_ready "


def prepare_first(nc, m):
    with semaphores(nc, PREP_NAMES) as s, nc.Block() as block:
        @block.scalar
        def _(act):
            act.copy(m.hTs[:], m.hT[:, 0:T]).then_inc(s["hs_ready"], 1)
            for k in range(NP):
                prepare_raw(nc, m, act, s, k, k % 4)

        @block.tensor
        def _(pe):
            pe.wait_ge(s["hs_ready"], 1)
            for k in range(NP):
                prepare_products(nc, m, pe, s, k, k % 4, 4)

        @block.sync
        def _(sp):
            for r in range(rope_count(NP)):
                prepare_swapped(nc, m, sp, s, r)

        @block.gpsimd
        def _(pool):
            for r in range(rope_count(NP)):
                prepare_sin(nc, m, pool, s, r)

        @block.vector
        def _(dve):
            for k in range(NP + 1):
                if k < NP:
                    prepare_cos(nc, m, dve, s, k, k % 4, 0)
                if k >= 1:
                    prepare_sum(nc, m, dve, s, k - 1, 0)
            dve.wait_ge(s["roped"], rope_count(NP))


def attention(nc, m):
    ROWS = 4
    UR = TB * KV
    U = ROWS * UR
    prepare_first(nc, m)
    names = (PREP_NAMES + "S_done mx_ready neg_ready masked exp_done "
             "sinkexp den_ready rinv_ready scaled PT_a PT_b PTs_a PTs_b PV_done yT_ready "
             "proj_done tx_ready x2_ready x2_sq ms_ready r3_ready h2_ready h2T_done h2Ts_ready gate_done gate_ready kept")
    PT_A, PT_B, YP, PREP_BANK = 4, 5, 6, 7
    SM = T // 2

    def place(u):
        r, rest = divmod(u, UR)
        return (r,) + divmod(rest, KV)

    def prep_step(st):
        r, n = divmod(st, UR)
        return r * NP + n if 0 <= st < U and n < NP else None

    def small(st):
        q, k = divmod(st - 5, 4)
        return (q, k) if 0 <= q < ROWS * TB else (None, None)

    with nc.Fori(0, B // ROWS) as i:
        with semaphores(nc, names) as s:
            S = [m.ps[:, 2 * n:2 * n + 2, :].rearrange("p k n -> p (k n)").rearrange("p (j w) -> p j w", j=HG) for n in range(2)]
            with nc.Block() as block:
                @block.tensor
                def _(pe):
                    def prepare(k):
                        if k % NP == 0:
                            pe.wait_ge(s["hs_ready"], k // NP + 1)
                        prepare_products(nc, m, pe, s, k, PREP_BANK, 1)

                    def scores(u):
                        r, qt, g = place(u)
                        if r >= 1 and qt == 0 and g % 2 == 0:
                            pe.wait_ge(s["roped"], rope_count((r - 1) * NP + (1 + g // 2) * (1 + HG)))
                        if u >= 2:
                            pe.wait_ge(s["mx_ready"], HG * (u - 1))
                        for j in range(HG):
                            ch, row = head_place(g, j)
                            w0 = P if qt == 0 else 0
                            keys = m.qk[row:row + DH, r % 2, NQ + g // 2, (qt - 1) * P + w0:(qt + 1) * P]
                            mm = pe.matmul(S[u % 2][:, j, w0:2 * P], m.qk[row:row + DH, r % 2, ch, qt * P:(qt + 1) * P], keys,
                                           start=True, stop=True)
                        mm.then_inc(s["S_done"], 1)

                    def transposes(u):
                        r, qt, g = place(u)
                        pe.wait_ge(s["scaled"], u + 1)
                        for j in range(HG):
                            bank, done, read = ((PT_A, "PT_a", "PTs_a"), (PT_B, "PT_b", "PTs_b"))[j // 2]
                            if j % 2 == 0 and u >= 1:
                                pe.wait_ge(s[read], u)
                            for kt in range(1 if qt == 0 else 0, 2):
                                c = 256 * (j % 2) + P * kt
                                mm = pe.transpose(m.ps[:, bank, c:c + P], m.prob[:, u % 3, j, kt * P:(kt + 1) * P], m.ident[:])
                            if j % 2 == 1:
                                mm.then_inc(s[done], 1)

                    def values(u):
                        r, qt, g = place(u)
                        if r >= 1 and qt == 0 and g == 0:
                            pe.wait_ge(s["v_ready"], r * NP - rope_count(r * NP))
                        pe.wait_ge(s["PTs_a"], u + 1)
                        pe.wait_ge(s["PTs_b"], u + 1)
                        if u >= 1:
                            pe.wait_ge(s["yT_ready"], u)
                        q, k = small(u)
                        if k == 0:
                            pe.wait_ge(s["x2_ready"], q + 1)
                        elif k == 2:
                            pe.wait_ge(s["h2Ts_ready"], q + 1)
                        elif k == 3:
                            pe.wait_ge(s["gate_ready"], q + 1)
                        first = 1 if qt == 0 else 0
                        for kt in range(first, 2):
                            for half in range(2):
                                mm = pe.matmul(m.ps[DH * half:DH * half + DH, YP, 0:2 * P], m.v[:, r % 2, qt - 1 + kt, g * DH:(g + 1) * DH],
                                               m.probT[:, u % 2, 2 * half:2 * half + 2, kt, :], start=(kt == first), stop=(kt == 1),
                                               skip_group_check=True)
                        mm.then_inc(s["PV_done"], 1)

                    def small_products(st):
                        q, k = small(st)
                        if k in (0, 2, 3):
                            pe.wait_ge(s["yT_ready"], min(st, U))
                        if k == 0:
                            if q >= 1:
                                pe.wait_ge(s["gate_ready"], q)
                            for c in range(2 * KV):
                                mm = pe.matmul(m.ps[:, YP, SM:SM + D], m.yT[:, q % 2, c, :], m.projw[:, c, :], start=(c == 0), stop=(c == 2 * KV - 1))
                            mm.then_inc(s["proj_done"], 1)
                        elif k == 2:
                            pe.wait_ge(s["x2_ready"], q + 1)
                            pe.wait_ge(s["h2_ready"], q + 1)
                            pe.transpose(m.ps[:, YP, SM:SM + P], m.h2s[:], m.ident[:]).then_inc(s["h2T_done"], 1)
                        elif k == 3:
                            pe.wait_ge(s["h2Ts_ready"], q + 1)
                            pe.matmul(m.ps[:, YP, SM:SM + E], m.h2Ts[:], m.gatew[:], start=True, stop=True).then_inc(s["gate_done"], 1)

                    for u in range(3):
                        scores(u)
                    for st in range(U + 5):
                        if st < U:
                            transposes(st)
                        if prep_step(st) is not None:
                            prepare(prep_step(st))
                        if 1 <= st <= U:
                            values(st - 1)
                        if st + 3 < U:
                            scores(st + 3)
                        small_products(st)

                @block.vector
                def _(dve):
                    def mask(u):
                        r, qt, g = place(u)
                        w0 = P if qt == 0 else 0
                        dve.wait_ge(s["S_done"], u + 1)
                        if u >= 2:
                            dve.wait_ge(s["sinkexp"], u - 1)
                        if u >= 3:
                            dve.wait_ge(s["PT_b"], u - 2)
                        for j in range(HG):
                            h = g * HG + j
                            nc.vector.tensor_tensor_reduce(out=m.prob[:, u % 3, j, w0:2 * P], in0=S[u % 2][:, j, w0:2 * P],
                                                           in1=m.window[:, w0:2 * P], scale=1.0, scalar=m.sink8[:, h:h + 1],
                                                           op0=ALU.add, op1=ALU.max, accum_out=m.mx[:, u % 2, j:j + 1]).then_inc(s["mx_ready"], 1)
                        dve.wait_ge(s["mx_ready"], HG * (u + 1))
                        nc.vector.tensor_scalar(m.negmx[:, u % 2, :], m.mx[:, u % 2, :], -(float(DH) ** -0.5), None, ALU.mult).then_inc(s["neg_ready"], 1)
                        dve.wait_ge(s["neg_ready"], u + 1)
                        nc.vector.tensor_tensor(m.sinkm[:, u % 2, :], m.sink[:, g * HG:(g + 1) * HG], m.negmx[:, u % 2, :], ALU.add).then_inc(s["masked"], 1)

                    def inverse(u):
                        dve.wait_ge(s["exp_done"], HG * (u + 1))
                        dve.wait_ge(s["sinkexp"], u + 1)
                        nc.vector.tensor_tensor(m.den[:, u % 2, :], m.rowsum[:, u % 2, :], m.esink[:, u % 2, :], ALU.add).then_inc(s["den_ready"], 1)
                        dve.wait_ge(s["den_ready"], u + 1)
                        if u >= 2:
                            dve.wait_ge(s["scaled"], u - 1)
                        nc.vector.reciprocal(m.rden[:, u % 2, :], m.den[:, u % 2, :]).then_inc(s["rinv_ready"], 1)

                    mask(0)
                    mask(1)
                    inverse(0)
                    for st in range(U + 5):
                        q, k = small(st)
                        if prep_step(st - 1) is not None and is_rope(prep_step(st - 1)):
                            prepare_cos(nc, m, dve, s, prep_step(st - 1), PREP_BANK, (1 + prep_step(st - 1) // NP) % 2)
                        if st < U:
                            dve.wait_ge(s["PT_b"], st + 1)
                            if st >= 2:
                                dve.wait_ge(s["PV_done"], st - 1)
                            w0 = 1 if place(st)[1] == 0 else 0
                            nc.vector.tensor_copy(m.probT[:, st % 2, 2:4, w0:2, :],
                                                  m.ps[:, PT_B, :].rearrange("p (j k i) -> p j k i", j=2, k=2)[:, :, w0:2, :]).then_inc(s["PTs_b"], 1)
                        if prep_step(st) is not None and not is_rope(prep_step(st)):
                            prepare_cos(nc, m, dve, s, prep_step(st), PREP_BANK, (1 + prep_step(st) // NP) % 2)
                        if st + 1 < U:
                            inverse(st + 1)
                        if k == 2:
                            dve.wait_ge(s["r3_ready"], q + 1)
                            if q >= 1:
                                dve.wait_ge(s["h2T_done"], q)
                                dve.wait_ge(s["kept"], 2 * q)
                            nc.vector.tensor_scalar(m.h2s[:], m.x2[:], m.r3[:, q % TB:q % TB + 1], None, ALU.mult).then_inc(s["h2_ready"], 1)
                        if st + 2 < U:
                            mask(st + 2)
                        if prep_step(st - 2) is not None:
                            prepare_sum(nc, m, dve, s, prep_step(st - 2), (1 + prep_step(st - 2) // NP) % 2)
                        if k == 0:
                            dve.wait_ge(s["tx_ready"], q + 1)
                            dve.wait_ge(s["proj_done"], q + 1)
                            if q >= 1:
                                dve.wait_ge(s["kept"], 2 * q)
                            nc.vector.tensor_tensor(m.x2[:], m.ps[:, YP, SM:SM + D], m.tx[:], ALU.add).then_inc(s["x2_ready"], 1)
                        if k == 3:
                            dve.wait_ge(s["gate_done"], q + 1)
                            nc.vector.tensor_tensor(m.logit[:, bass.ds((i * (ROWS * TB) + q) * E, E)], m.ps[:, YP, SM:SM + E], m.gateb[:], ALU.add).then_inc(s["gate_ready"], 1)

                @block.scalar
                def _(act):
                    def exps(u):
                        r, qt, g = place(u)
                        w0 = P if qt == 0 else 0
                        act.wait_ge(s["masked"], u + 1)
                        if u >= 2:
                            act.wait_ge(s["den_ready"], u - 1)
                        for j in range(HG):
                            nc.scalar.activation(m.prob[:, u % 3, j, w0:2 * P], m.prob[:, u % 3, j, w0:2 * P], ACT.Exp,
                                                 bias=m.negmx[:, u % 2, j:j + 1], scale=float(DH) ** -0.5,
                                                 accum_out=m.rowsum[:, u % 2, j:j + 1]).then_inc(s["exp_done"], 1)
                        nc.scalar.activation(m.esink[:, u % 2, :], m.sinkm[:, u % 2, :], ACT.Exp).then_inc(s["sinkexp"], 1)

                    def next_row(r):
                        if r >= 1:
                            act.wait_ge(s["prep_done"], r * NP)
                        act.copy(m.hTs[:], m.hT[:, bass.ds((i * ROWS + r + 1) * T, T)]).then_inc(s["hs_ready"], 1)

                    next_row(0)
                    exps(0)
                    exps(1)
                    for st in range(U + 5):
                        q, k = small(st)
                        if st + 2 < U and (st + 2) % UR == 0:
                            next_row((st + 2) // UR)
                        if st < U:
                            act.wait_ge(s["PT_a"], st + 1)
                            if st >= 2:
                                act.wait_ge(s["PV_done"], st - 1)
                            w0 = 1 if place(st)[1] == 0 else 0
                            nc.scalar.copy(m.probT[:, st % 2, 0:2, w0:2, :],
                                           m.ps[:, PT_A, :].rearrange("p (j k i) -> p j k i", j=2, k=2)[:, :, w0:2, :]).then_inc(s["PTs_a"], 1)
                        if 1 <= st <= U:
                            tile, g = divmod(st - 1, KV)
                            act.wait_ge(s["PV_done"], st)
                            if tile >= 2:
                                act.wait_ge(s["proj_done"], tile - 1)
                            nc.scalar.copy(m.yT[:, tile % 2, 2 * g:2 * g + 2, :], m.ps[:, YP, 0:2 * P].rearrange("p (j i) -> p j i", j=2)).then_inc(s["yT_ready"], 1)
                        if k == 1:
                            act.wait_ge(s["x2_ready"], q + 1)
                            if q >= 1:
                                act.wait_ge(s["x2_sq"], q)
                            nc.scalar.activation(m.sq[:, 0:D], m.x2[:], ACT.Square, accum_out=m.ssq[:, q % TB:q % TB + 1]).then_inc(s["x2_sq"], 1)
                        if prep_step(st) is not None:
                            prepare_raw(nc, m, act, s, prep_step(st), PREP_BANK)
                        if st + 2 < U:
                            exps(st + 2)
                        if k == 2:
                            act.wait_ge(s["h2T_done"], q + 1)
                            if q >= 1:
                                act.wait_ge(s["gate_done"], q)
                            nc.scalar.copy(m.h2Ts[:], m.ps[:, YP, SM:SM + P]).then_inc(s["h2Ts_ready"], 1)

                @block.sync
                def _(sp):
                    for r in range(rope_count(ROWS * NP)):
                        prepare_swapped(nc, m, sp, s, r)

                @block.gpsimd
                def _(pool):
                    def scale(u):
                        w0 = P if place(u)[1] == 0 else 0
                        pool.wait_ge(s["rinv_ready"], u + 1)
                        p = m.prob[:, u % 3, :, w0:2 * P]
                        nc.gpsimd.tensor_tensor(p, p, bc(m.rden[:, u % 2, :, None], [P, HG, 2 * P - w0]), ALU.mult).then_inc(s["scaled"], 1)

                    def residual(q):
                        if q >= 1:
                            pool.wait_ge(s["x2_ready"], q)
                        nc.gpsimd.tensor_tensor(m.tx[:], m.xn[:, bass.ds(i * (ROWS * TB) + q, 1), :].rearrange("p a d -> p (a d)"), m.projb[:],
                                                ALU.add).then_inc(s["tx_ready"], 1)

                    residual(0)
                    scale(0)
                    for st in range(U + 5):
                        q, k = small(st)
                        if st + 1 < U:
                            scale(st + 1)
                        k1 = prep_step(st - 1)
                        if k1 is not None and is_rope(k1):
                            prepare_sin(nc, m, pool, s, rope_count(k1))
                        if q is None:
                            continue
                        tile = bass.ds(i * (ROWS * TB) + q, 1)
                        if k == 3 and q + 1 < ROWS * TB:
                            residual(q + 1)
                        if k == 1:
                            pool.wait_ge(s["x2_sq"], q + 1)
                            c = q % TB
                            nc.gpsimd.tensor_scalar(m.ms3[:, c:c + 1], m.ssq[:, c:c + 1], 1.0 / D, RMS_EPS_F, ALU.mult, ALU.add).then_inc(s["ms_ready"], 1)
                            pool.wait_ge(s["ms_ready"], q + 1)
                            if q >= TB:
                                pool.wait_ge(s["h2_ready"], q - TB + 1)
                            nc.gpsimd.tensor_tensor(m.r3[:, c:c + 1], m.ms3[:, c:c + 1], m.minus_half[:, 0:1], ALU.pow).then_inc(s["r3_ready"], 1)
                        if k == 2:
                            a = m.acc[:, tile, :].rearrange("p a d -> p (a d)")
                            nc.gpsimd.tensor_tensor(a, a, m.x2[:], ALU.add).then_inc(s["kept"], 1)
                            pool.wait_ge(s["h2_ready"], q + 1)
                            nc.gpsimd.tensor_copy(m.h2[:, tile, :].rearrange("p a d -> p (a d)"), m.h2s[:]).then_inc(s["kept"], 1)


def routing(nc, m):
    TE = NT * E
    with semaphores(nc, "own before_done count_done mask_ready exp_ready pool cum_ready cum_T slots_ready ended_ready expert_done scaled") as s:
        onehot = [m.big[:, k * TE:(k + 1) * TE] for k in range(TOPK)]
        def t3(ap):
            return ap.rearrange("p (t e) -> p t e", e=E)
        with nc.Block() as block:
            @block.vector
            def _(dve):
                own = Steps(dve, s["own"])
                for t in range(NT):
                    own(nc.vector.max(m.top8[:, t, :], m.logit[:, t * E:(t + 1) * E]))
                for t in range(NT):
                    own.wait(t + 1)
                    own(nc.vector.max_index(m.idx8[:, t, :], m.top8[:, t, :], m.logit[:, t * E:(t + 1) * E]))
                own.wait()
                own(nc.vector.tensor_copy(m.idxf[:], m.idx8[:, :, 0:TOPK]))
                own.wait()
                for k in range(TOPK):
                    own(nc.vector.tensor_tensor(t3(onehot[k]), bc(m.idxf[:, :, k:k + 1], [P, NT, E]),
                                                bc(m.iota_e[:, None, :], [P, NT, E]), ALU.is_equal))
                own.wait()
                a, c = m.big[:, 4 * TE:5 * TE], m.big[:, 5 * TE:6 * TE]
                own(nc.vector.tensor_tensor(a, onehot[0], onehot[1], ALU.add))
                own(nc.vector.tensor_tensor(c, onehot[2], onehot[3], ALU.add))
                own.wait()
                nc.vector.tensor_tensor(m.chosen_bf[:], a, c, ALU.add).then_inc(s["mask_ready"], 1)
                own(nc.vector.tensor_tensor(m.gatew4[:], m.top8[:, :, 0:TOPK], bc(m.top8[:, :, 0:1], [P, NT, TOPK]), ALU.subtract))
                dve.wait_ge(s["exp_ready"], 1)
                own(nc.vector.tensor_reduce(m.gsum[:], m.gexp[:], AXX, ALU.add))
                own.wait()
                own(nc.vector.reciprocal(m.grec[:], m.gsum[:]))
                own.wait()
                own(nc.vector.tensor_tensor(m.gatew4[:], m.gexp[:], bc(m.grec[:, :, None], [P, NT, TOPK]), ALU.mult))
                dve.wait_ge(s["before_done"], 2)
                dve.wait_ge(s["count_done"], 2)
                own(nc.vector.tensor_copy(c, m.ps[:, 2:4, :].rearrange("p k n -> p (k n)")))
                own(nc.vector.memset(m.carry[:, 0:E], 0.0))
                for t in range(1, NT + 1):
                    own.wait()
                    own(nc.vector.tensor_tensor(m.carry[:, t * E:(t + 1) * E], m.carry[:, (t - 1) * E:t * E], c[:, (t - 1) * E:t * E], ALU.add))
                own.wait()
                n_e = m.carry[:, TE:TE + E]
                own(nc.vector.tensor_tensor(t3(a), bc(n_e[:, :, None], [P, E, NT]), bc(m.iota_blk[:, None, 0:NT], [P, E, NT]), ALU.is_gt))
                own.wait()
                own(nc.vector.tensor_reduce(m.nblk[:], t3(a), AXX, ALU.add))
                own.wait()
                own(nc.vector.tensor_tensor(t3(a), bc(m.nblk[:, None, :], [P, E, E]), m.upto_e[:], ALU.mult))
                own.wait()
                nc.vector.tensor_reduce(m.cumblk[:], t3(a), AXX, ALU.add).then_inc(s["cum_ready"], 1)
                dve.wait_ge(s["cum_ready"], 1)
                own(nc.vector.tensor_tensor(m.base[:], m.cumblk[:], m.nblk[:], ALU.subtract))
                own.wait()
                own(nc.vector.tensor_scalar(m.base[:], m.base[:], float(P), None, ALU.mult))
                own(nc.vector.tensor_tensor(c, m.ps[:, 0:2, :].rearrange("p k n -> p (k n)"), m.carry[:, 0:TE], ALU.add))
                own.wait()
                nc.vector.tensor_tensor(t3(c), t3(c), bc(m.base[:, None, :], [P, NT, E]), ALU.add).then_inc(s["slots_ready"], 1)
                dve.wait_ge(s["slots_ready"], 1)
                for k in range(2):
                    own(nc.vector.tensor_tensor(onehot[k], onehot[k], c, ALU.mult))
                    own.wait()
                    own(nc.vector.tensor_reduce(m.slotf[:, :, k], t3(onehot[k]), AXX, ALU.add))
                dve.wait_ge(s["cum_T"], 1)
                own(nc.vector.tensor_copy(m.cumT[0:E, :], m.ps[0:E, 4, 0:1]))
                own.wait()
                nc.vector.tensor_scalar(m.ended[0:E, :], m.iota_j[0:E, :], m.cumT[0:E, :], None, ALU.is_ge).then_inc(s["ended_ready"], 1)
                for k in range(2, TOPK):
                    dve.wait_ge(s["pool"], k - 1)
                    own(nc.vector.tensor_reduce(m.slotf[:, :, k], t3(onehot[k]), AXX, ALU.add))
                own.wait()
                own(nc.vector.tensor_copy(m.slot[:], m.slotf[:]))
                dve.wait_ge(s["expert_done"], 1)
                own(nc.vector.tensor_scalar(m.blk[:], m.ps[:, 5, 0:NBLK], float(E - 1), float(WE), ALU.min, ALU.mult))
                own.wait()

            @block.gpsimd
            def _(pool):
                for k in range(2, TOPK):
                    pool.wait_ge(s["slots_ready"], 1)
                    nc.gpsimd.tensor_tensor(onehot[k], onehot[k], m.big[:, 5 * TE:6 * TE], ALU.mult).then_inc(s["pool"], 1)

            @block.tensor
            def _(pe):
                pe.wait_ge(s["mask_ready"], 1)
                for i in range(2):
                    pe.matmul(m.ps[:, i, :], m.before_bf[:], m.chosen_bf[:, 512 * i:512 * i + 512], start=True, stop=True).then_inc(s["before_done"], 1)
                for i in range(2):
                    pe.matmul(m.ps[:, 2 + i, :], m.ones_bf[:], m.chosen_bf[:, 512 * i:512 * i + 512], start=True, stop=True).then_inc(s["count_done"], 1)
                pe.wait_ge(s["cum_ready"], 1)
                pe.transpose(m.ps[0:E, 4, 0:P], m.cumblk[:], m.ident[:]).then_inc(s["cum_T"], 1)
                pe.wait_ge(s["ended_ready"], 1)
                pe.matmul(m.ps[:, 5, 0:NBLK], m.tot_ones[0:E, :], m.ended[0:E, :], start=True, stop=True).then_inc(s["expert_done"], 1)

            @block.scalar
            def _(act):
                act.wait_ge(s["own"], 2 * NT + 8)
                nc.scalar.activation(m.gexp[:], m.gatew4[:], ACT.Exp).then_inc(s["exp_ready"], 1)
                act.wait_ge(s["exp_ready"], 1)
                act.wait_ge(m.up_loaded, 16 * 4)
                act.wait_ge(m.down_loaded, 16)
                up = m.we[:].rearrange("p (e f) -> p e f", f=WE)[:, :, 0:2 * DFF]
                nc.scalar.activation(up, up, ACT.Copy, scale=m.wn[:, 1:2]).then_inc(s["scaled"], 1)
                act.wait_ge(s["scaled"], 1)


def retention(nc, m, a, half):
    names = ("in_ready q_proj k_proj v_proj g_proj squared eg_done ms_ready ln_ready r_ready own own_gate qn_ready kn_ready v_ready g_ready q4_hi k4_hi "
             "q4_ready k4_ready qd_ready kd_ready TQ_done TK_done TD_done TQ_ev TK_ev TD_ev arg_done A_done D_ready At_ready "
             "oT_done oT_ev o_done o_ev kv_done kvm_ready state_ready S_ready rhs_pool osq_done ms16_ready r16_ready on_ready og_ready "
             "TG_done TG_ev wo_done out_done copied rhs_ready added")
    U = TB * 4
    NCP = 3
    QB, KB, VB, GB = range(4)
    TQ, TK, OT, TD = 0, 1, (2, 3), 3
    ARG, SC = (4, 5), (6, 7)
    with semaphores(nc, "cleared") as s, nc.Block() as block:
        @block.vector
        def _(dve):
            for pad in (m.qT_by_head[:].bitcast(F32), m.state_x[:]):
                nc.vector.memset(pad, 0.0).then_inc(s["cleared"], 1)
            dve.wait_ge(s["cleared"], 2)
    with ExitStack() as ctx:
        moved = m.moved
        turn_no = ctx.enter_context(nc.Fori(0, B // 2))
        b = turn_no + half * (B // 2)
        with semaphores(nc, names) as s, nc.Block() as block:
            def t3(ap, n=P):
                return ap.rearrange("p (t n) -> p t n", n=n)

            def heads(ap):
                return ap.rearrange("p (h d) -> p h d", d=DR)

            def tile_heads(buf, t):
                return heads(buf[:, t * P:(t + 1) * P])[:, :, None, :]

            def parts(buf, t):
                return buf[:, t % 2, :].rearrange("p (h r d) -> p h r d", r=4, d=DR)

            eg = m.qdT[:]

            @block.tensor
            def _(pe):
                pe.wait_ge(s["in_ready"], 1)
                for bank, done in ((QB, "q_proj"), (KB, "k_proj"), (VB, "v_proj"), (GB, "g_proj")):
                    for t in range(TB):
                        mm = pe.matmul(m.ps[:, bank, t * P:(t + 1) * P], m.xTs[:, t * P:(t + 1) * P], m.wr[:, bank * P:(bank + 1) * P],
                                       start=True, stop=True)
                    mm.then_inc(s[done], 1)

                def turn(t):
                    pe.wait_ge(s["q4_ready"], t + 1)
                    if t == 0:
                        pe.wait_ge(s["qn_ready"], 1)
                    else:
                        pe.wait_ge(s["TQ_ev"], 4 * t)
                    if t >= 2:
                        pe.wait_ge(s["kvm_ready"], t - 1)
                    for c in range(4):
                        mm = pe.transpose(m.ps[:, TQ, c * P:(c + 1) * P], m.q4[:, t % 2, c * P:(c + 1) * P].bitcast(F32), m.ident[:])
                    mm.then_inc(s["TQ_done"], 1)
                    pe.wait_ge(s["k4_ready"], t + 1)
                    if t == 0:
                        pe.wait_ge(s["kn_ready"], 1)
                    else:
                        pe.wait_ge(s["TK_ev"], t)
                    if t >= 3:
                        pe.wait_ge(s["o_ev"], t - 2)
                    for c in range(4):
                        mm = pe.transpose(m.ps[:, TK, c * P:(c + 1) * P], m.k4[:, t % 2, c * P:(c + 1) * P].bitcast(F32), m.ident[:])
                    mm.then_inc(s["TK_done"], 1)

                def exponents(u):
                    t, c = divmod(u, 4)
                    if u >= 2:
                        pe.wait_ge(s["D_ready"], u - 1)
                    if u % 8 == 0:
                        pe.wait_ge(s[("rhs_ready", "rhs_pool")[t // 2]], 1)
                    row = 64 * (t % 2)
                    pe.matmul(m.ps[:, ARG[u % 2], :], m.ident_bf[:], m.future_bf[:].rearrange("p j i -> p (j i)"), start=True, stop=False)
                    pe.matmul(m.ps[:, ARG[u % 2], :], m.argLs[row:row + 64, t // 2, :], m.argRx[row:row + 64, t // 2, 4 * c:4 * c + 4, :],
                              start=False, stop=True).then_inc(s["arg_done"], 1)

                def scores(u):
                    t, c = divmod(u, 4)
                    if c == 0:
                        pe.wait_ge(s["TQ_ev"], 4 * (t + 1))
                        pe.wait_ge(s["TK_ev"], t + 1)
                    if u >= 2:
                        pe.wait_ge(s["At_ready"], u - 1)
                    pe.matmul(m.ps[:, SC[u % 2], :], m.k4T[:, t % 2, c, :], m.qT_by_head[:, t % 2, c, :, :], start=True, stop=True).then_inc(s["A_done"], 1)

                def out_cross(t):
                    if t == 0:
                        pe.wait_ge(s["v_ready"], 1)
                    if t >= 2:
                        pe.wait_ge(s["oT_ev"], t - 1)
                    if t >= 1:
                        pe.wait_ge(s["S_ready"], t)
                    for c in range(4):
                        pe.matmul(m.ps[:, OT[t % 2], c * P:(c + 1) * P], m.state_x[:, c, :, :].rearrange("p j e -> p (j e)"),
                                  m.qdT[:, t * P:(t + 1) * P], start=(c == 0), stop=False, skip_group_check=True)

                def out_intra(u):
                    t, c = divmod(u, 4)
                    pe.wait_ge(s["At_ready"], u + 1)
                    for j in range(4):
                        v0 = t * P + (4 * c + j) * DR
                        mm = pe.matmul(m.ps[32 * j:32 * j + DR, OT[t % 2], c * P:(c + 1) * P], m.vn[:, v0:v0 + DR], m.At[:, u % NCP, j, :],
                                       start=False, stop=(c == 3), skip_group_check=True)
                    mm.then_inc(s["oT_done"], 1)

                def turn_back(t):
                    pe.wait_ge(s["oT_ev"], t + 1)
                    pe.wait_ge(s["TK_ev"], min(t + 3, TB))
                    if t >= 2:
                        pe.wait_ge(s["o_ev"], t)
                    for c in range(4):
                        mm = pe.transpose(m.ps[:, TK, c * P:(c + 1) * P], m.oT[:, c * P:(c + 1) * P], m.ident[:])
                    mm.then_inc(s["o_done"], 1)

                def update(t):
                    pe.wait_ge(s["TQ_ev"], 4 * (t + 2))
                    pe.matmul(m.ps[:, TQ, 0:P], m.kd[:, t * P:(t + 1) * P], m.vn[:, t * P:(t + 1) * P], start=True, stop=True).then_inc(s["kv_done"], 1)

                exponents(0)
                exponents(1)
                turn(0)
                pe.wait_ge(s["qd_ready"], 1)
                pe.wait_ge(s["g_ready"], 1)
                for t in range(TB):
                    mm = pe.transpose(m.ps[:, TD, t * P:(t + 1) * P], m.qd[:, t * P:(t + 1) * P], m.ident[:])
                mm.then_inc(s["TD_done"], 1)
                scores(0)
                scores(1)
                pe.wait_ge(s["kd_ready"], 1)
                pe.wait_ge(s["TD_ev"], 1)
                for u in range(U):
                    t, c = divmod(u, 4)
                    if c == 0:
                        out_cross(t)
                    if u + 2 < U:
                        exponents(u + 2)
                        scores(u + 2)
                    if c == 0 and t + 1 < TB:
                        turn(t + 1)
                    if c == 2 and t + 1 < TB:
                        update(t)
                    if c == 2 and t >= 1:
                        turn_back(t - 1)
                    out_intra(u)
                turn_back(TB - 1)
                pe.wait_ge(s["og_ready"], 1)
                for t in range(TB):
                    mm = pe.transpose(m.ps[:, TQ, t * P:(t + 1) * P], m.o[:, t * P:(t + 1) * P], m.ident[:])
                mm.then_inc(s["TG_done"], 1)
                pe.wait_ge(s["TG_ev"], 1)
                for t in range(TB):
                    mm = pe.matmul(m.ps[:, TK, t * P:(t + 1) * P], m.qdT[:, t * P:(t + 1) * P], m.wo[:], start=True, stop=True)
                mm.then_inc(s["wo_done"], 1)

            @block.vector
            def _(dve):
                own = Steps(dve, s["own"])
                own(nc.vector.tensor_copy(m.argLs[:], m.argL[:, bass.ds(2 * b, 2), :].bitcast(F32)))
                nc.vector.tensor_tensor(m.argRx[:, 0, :, :], bc(m.argR[:, bass.ds(2 * b, 1), :].bitcast(F32), [P, HR, P]),
                                        bc(m.arg_head[:, :, None], [P, HR, P]), ALU.mult).then_inc(s["rhs_ready"], 1)
                own(nc.vector.tensor_copy(m.e_in_s[:], m.e_in[:, bass.ds(b * TB * HR, TB * HR)]))
                own(nc.vector.tensor_copy(m.e_out_s[:], m.e_out[:, bass.ds(b * TB * HR, TB * HR)]))
                own(nc.vector.tensor_copy(m.decay_s[:], m.decay_tile_e[:, bass.ds(b * TB, TB)]))
                own(nc.vector.memset(m.state[:], 0.0))
                own(nc.vector.memset(m.state_x[:, :, :, 0:DR], 0.0))
                own.wait()
                dve.wait_ge(s["squared"], TB)
                own(nc.vector.tensor_scalar(m.ms3[:, 0:TB], m.ssq[:, 0:TB], float(DR) / D, DR * RMS_EPS_R, ALU.mult, ALU.add))
                dve.wait_ge(s["squared"], 3 * TB)
                nc.vector.tensor_scalar(m.ms3[:, TB:3 * TB], m.ssq[:, TB:3 * TB], 1.0 / D, RMS_EPS_R, ALU.mult, ALU.add).then_inc(s["ms_ready"], 1)
                dve.wait_ge(s["eg_done"], 1)
                nc.vector.tensor_scalar(eg, eg, 1.0, None, ALU.add).then_inc(s["own_gate"], 1)
                dve.wait_ge(s["own_gate"], 1)
                nc.vector.reciprocal(m.sg[:], eg).then_inc(s["own_gate"], 1)
                dve.wait_ge(s["own_gate"], 2)
                nc.vector.tensor_tensor(m.sg[:], m.ps[:, GB, :], m.sg[:], ALU.mult).then_inc(s["g_ready"], 1)
                dve.wait_ge(s["r_ready"], 1)
                for n, (bank, dst, done) in enumerate(((QB, m.qn, "qn_ready"), (KB, m.kn, "kn_ready"), (VB, m.vn, "v_ready"))):
                    nc.vector.tensor_tensor(t3(dst[:, 0:T]), t3(m.ps[:, bank, :]), bc(m.rr[:, n * TB:(n + 1) * TB, None], [P, TB, P]), ALU.mult).then_inc(s[done], 1)

                def split(t):
                    both = [P, HR, 2, DR]
                    q4, k4 = parts(m.q4, t), parts(m.k4, t)
                    if t >= 2:
                        dve.wait_ge(s["TQ_done"], t - 1)
                        dve.wait_ge(s["TK_done"], t - 1)
                    dve.wait_ge(s["q4_hi"], t + 1)
                    nc.vector.tensor_tensor(q4[:, :, 1:4:2, :], bc(tile_heads(m.qn, t), both), q4[:, :, 0:4:2, :].bitcast(F32), ALU.subtract).then_inc(s["q4_ready"], 1)
                    dve.wait_ge(s["k4_hi"], t + 1)
                    nc.vector.tensor_tensor(k4[:, :, 2:4, :], bc(tile_heads(m.kn, t), both), k4[:, :, 0:2, :].bitcast(F32), ALU.subtract).then_inc(s["k4_ready"], 1)

                split(0)
                nc.vector.tensor_tensor(heads(m.qd[:]), heads(m.qn[:, 0:T]), bc(m.e_in_s[:, :, None], [P, TB * HR, DR]), ALU.mult).then_inc(s["qd_ready"], 1)
                nc.vector.tensor_tensor(heads(m.kd[:]), heads(m.kn[:, 0:T]), bc(m.e_out_s[:, :, None], [P, TB * HR, DR]), ALU.mult).then_inc(s["kd_ready"], 1)
                split(1)

                def k_turned(t):
                    dve.wait_ge(s["TK_done"], t + 1)
                    if t >= 2:
                        dve.wait_ge(s["A_done"], 4 * (t - 1))
                    nc.vector.tensor_copy(m.k4T[:, t % 2, :, :].rearrange("p c i -> p (c i)"), m.ps[:, TK, :]).then_inc(s["TK_ev"], 1)

                def add_choices(t0):
                    dve.wait_ge(s["copied"], 2)
                    for t in (t0, t0 + 1):
                        dve.wait_ge(moved[t], (turn_no + (1 + B // 2)) * (16 * TOPK))
                    for k in range(TOPK):
                        for t in (t0, t0 + 1):
                            acc = m.acc[:, bass.ds(turn_no * 2 * TB + t, 1), :].rearrange("p a d -> p (a d)")
                            if k >= 1:
                                dve.wait_ge(s["added"], TOPK * t0 + 2 * k + t - t0 - 1)
                            nc.vector.scalar_tensor_tensor(out=acc, in0=m.got[:, TOPK * t + k, :], scalar=m.gw_s[:, t, k:k + 1], in1=acc,
                                                           op0=ALU.mult, op1=ALU.add).then_inc(s["added"], 1)

                def o_turned(t):
                    dve.wait_ge(s["o_done"], t + 1)
                    nc.vector.tensor_copy(heads(m.o[:, t * P:(t + 1) * P]),
                                          m.ps[:, TK, :].rearrange("p (h e) -> p h e", e=32)[:, :, 0:DR]).then_inc(s["o_ev"], 1)

                k_turned(0)
                for u in range(U):
                    t, c = divmod(u, 4)
                    dve.wait_ge(s["A_done"], u + 1)
                    dve.wait_ge(s["D_ready"], u + 1)
                    if u >= NCP:
                        dve.wait_ge(s["oT_done"], u - NCP + 1)
                    nc.vector.tensor_tensor(m.At[:, u % NCP, :, :].rearrange("p j i -> p (j i)"), m.ps[:, SC[u % 2], :],
                                            m.Dm[:, u % 2, :], ALU.mult).then_inc(s["At_ready"], 1)
                    if t + 1 < TB and c == 1:
                        k_turned(t + 1)
                    if t + 2 < TB and c == 3:
                        split(t + 2)
                    if t + 1 < TB and c == 2:
                        dve.wait_ge(s["kv_done"], t + 1)
                        nc.vector.tensor_tensor(m.kvm[:], m.ps[:, TQ, 0:P], m.same_head[:], ALU.mult).then_inc(s["kvm_ready"], 1)
                        dve.wait_ge(s["kvm_ready"], t + 1)
                        if t >= 1:
                            dve.wait_ge(s["S_ready"], t)
                        nc.vector.scalar_tensor_tensor(out=m.state[:], in0=m.state[:], scalar=m.decay_s[:, t:t + 1], in1=m.kvm[:],
                                                       op0=ALU.mult, op1=ALU.add).then_inc(s["state_ready"], 1)
                        dve.wait_ge(s["state_ready"], t + 1)
                        dve.wait_ge(s["oT_done"], 4 * t + 1)
                        nc.vector.tensor_copy(m.state_x[:, :, :, 0:DR], m.state[:].rearrange("p (c j e) -> p c j e", c=4, j=4)).then_inc(s["S_ready"], 1)
                    if t >= 1 and c == 3:
                        o_turned(t - 1)
                    if half == 1 and u in (9, 12, 15):
                        add_choices(2 * (u // 3 - 3))
                o_turned(TB - 1)
                dve.wait_ge(s["osq_done"], 1)
                own(nc.vector.tensor_reduce(m.ms16[:], heads(m.sq[:]), AXX, ALU.add))
                own.wait()
                nc.vector.tensor_scalar(m.ms16[:], m.ms16[:], 1.0 / DR, RMS_EPS_R, ALU.mult, ALU.add).then_inc(s["ms16_ready"], 1)
                dve.wait_ge(s["r16_ready"], 1)
                nc.vector.tensor_tensor(heads(m.sq[:]), heads(m.o[:]), bc(m.r16[:, :, None], [P, TB * HR, DR]), ALU.mult).then_inc(s["on_ready"], 1)
                dve.wait_ge(s["on_ready"], 1)
                nc.vector.tensor_tensor(m.o[:], m.sq[:], m.sg[:], ALU.mult).then_inc(s["og_ready"], 1)
                if half == 1:
                    add_choices(2 * TB - 2)
                dve.wait_ge(s["wo_done"], 1)
                if half == 1:
                    dve.wait_ge(s["added"], 2 * TB * TOPK)
                acc = m.acc[:, bass.ds(b * TB, TB), :]
                nc.vector.tensor_tensor(acc, t3(m.ps[:, TK, :]), acc, ALU.add).then_inc(s["out_done"], 1)
            @block.scalar
            def _(act):
                act.copy(m.xTs[:], m.xT[:, bass.ds(b * T, T)]).then_inc(s["in_ready"], 1)
                for n, (bank, done) in enumerate(((QB, "q_proj"), (KB, "k_proj"), (VB, "v_proj"))):
                    act.wait_ge(s[done], 1)
                    for t in range(TB):
                        if n >= 1:
                            act.wait_ge(s["squared"], (n - 1) * TB + t + 1)
                        nc.scalar.activation(m.sq[:, t * P:(t + 1) * P], m.ps[:, bank, t * P:(t + 1) * P], ACT.Square,
                                             accum_out=m.ssq[:, n * TB + t:n * TB + t + 1]).then_inc(s["squared"], 1)
                act.wait_ge(s["g_proj"], 1)
                nc.scalar.activation(eg, m.ps[:, GB, :], ACT.Exp, scale=-1.0).then_inc(s["eg_done"], 1)
                act.wait_ge(s["ms_ready"], 1)
                nc.scalar.activation(m.rr[:], m.ms3[:], ACT.Ln).then_inc(s["ln_ready"], 1)
                act.wait_ge(s["ln_ready"], 1)
                nc.scalar.activation(m.rr[:], m.rr[:], ACT.Exp, scale=-0.5).then_inc(s["r_ready"], 1)

                def high_parts(t):
                    both = [P, HR, 2, DR]
                    if t == 0:
                        act.wait_ge(s["qn_ready"], 1)
                    if t >= 2:
                        act.wait_ge(s["TQ_done"], t - 1)
                        act.wait_ge(s["TK_done"], t - 1)
                        act.wait_ge(s["k4_ready"], t - 1)
                    nc.scalar.copy(parts(m.q4, t)[:, :, 0:4:2, :], bc(tile_heads(m.qn, t), both)).then_inc(s["q4_hi"], 1)
                    if t == 0:
                        act.wait_ge(s["kn_ready"], 1)
                    nc.scalar.copy(parts(m.k4, t)[:, :, 0:2, :], bc(tile_heads(m.kn, t), both)).then_inc(s["k4_hi"], 1)

                high_parts(0)
                high_parts(1)

                def decay(u):
                    act.wait_ge(s["arg_done"], u + 1)
                    if u >= 2:
                        act.wait_ge(s["At_ready"], u - 1)
                    nc.scalar.activation(m.Dm[:, u % 2, :], m.ps[:, ARG[u % 2], :], ACT.Exp).then_inc(s["D_ready"], 1)

                def q_turned(t):
                    act.wait_ge(s["TQ_done"], t + 1)
                    if t >= 2:
                        act.wait_ge(s["A_done"], 4 * (t - 1))
                    for j in range(4):
                        rows = slice(32 * j, 32 * j + 32)
                        nc.scalar.copy(m.qT_by_head[rows, t % 2, :, j, :], m.ps[rows, TQ, :].rearrange("p (c i) -> p c i", c=4)).then_inc(s["TQ_ev"], 1)

                def oT_out(t):
                    act.wait_ge(s["oT_done"], 4 * (t + 1))
                    if t >= 1:
                        act.wait_ge(s["o_done"], t)
                    nc.scalar.copy(m.oT[:], m.ps[:, OT[t % 2], :]).then_inc(s["oT_ev"], 1)

                decay(0)
                decay(1)
                q_turned(0)
                act.wait_ge(s["TD_done"], 1)
                nc.scalar.copy(m.qdT[:], m.ps[:, TD, :]).then_inc(s["TD_ev"], 1)
                for u in range(U):
                    if u + 2 < U:
                        decay(u + 2)
                    t, c = divmod(u, 4)
                    if c == 0 and t + 1 < TB:
                        q_turned(t + 1)
                    if c == 0 and t >= 1:
                        oT_out(t - 1)
                    if c == 2 and t + 2 < TB:
                        high_parts(t + 2)
                oT_out(TB - 1)
                act.wait_ge(s["o_ev"], TB)
                act.wait_ge(s["squared"], 3 * TB)
                nc.scalar.activation(m.sq[:], m.o[:], ACT.Square).then_inc(s["osq_done"], 1)
                act.wait_ge(s["ms16_ready"], 1)
                nc.scalar.activation(m.r16[:], m.ms16[:], ACT.Ln).then_inc(s["ln_ready"], 1)
                act.wait_ge(s["ln_ready"], 2)
                nc.scalar.activation(m.r16[:], m.r16[:], ACT.Exp, scale=-0.5).then_inc(s["r16_ready"], 1)
                act.wait_ge(s["TG_done"], 1)
                nc.scalar.copy(m.qdT[:], m.ps[:, TQ, :]).then_inc(s["TG_ev"], 1)

            @block.gpsimd
            def _(pool):
                two = bass.ds(turn_no * 2 * TB, 2 * TB)
                nc.gpsimd.tensor_copy(m.slot_s[:], m.slot[:, two, :]).then_inc(s["copied"], 1)
                if half == 0:
                    nc.gpsimd.tensor_copy(m.rows[:], m.h2[:, two, :]).then_inc(s["copied"], 1)
                else:
                    nc.gpsimd.tensor_copy(m.gw_s[:], m.gatew4[:, two, :]).then_inc(s["copied"], 1)
                pool.wait_ge(s["copied"], 2)
                pool.wait_ge(m.slots_cleared, 16 * 8)

                def move(t):
                    for k in range(TOPK):
                        slots = bass.IndirectOffsetOnAxis(ap=m.slot_s[:, t, k:k + 1], axis=0)
                        if half == 0:
                            ins = pool.indirect_dma_start(a["slots_x"][:, :], slots, m.rows[:, t, :], None)
                        else:
                            ins = pool.indirect_dma_start(m.got[:, TOPK * t + k, :], None, a["slots_y"][:, :], slots)
                        ins.then_inc(moved[t], 16)

                nc.gpsimd.tensor_tensor(m.argRx[:, 1, :, :], bc(m.argR[:, bass.ds(2 * b + 1, 1), :].bitcast(F32), [P, HR, P]),
                                        bc(m.arg_head[:, :, None], [P, HR, P]), ALU.mult).then_inc(s["rhs_pool"], 1)
                for t in range(2 * TB):
                    move(t)
                for t in range(2 * TB):
                    pool.wait_ge(moved[t], (turn_no + (1 + half * (B // 2))) * (16 * TOPK))

            if half == 1:
                @block.sync
                def _(sp):
                    sp.wait_ge(s["added"], 2 * TB * TOPK)
                    sp.wait_ge(s["out_done"], 1)
                    sp.dma_start(a["out"][bass.ds(turn_no * 2, 2), :, :].rearrange("a (t p) d -> p (a t) d", p=P),
                                 m.acc[:, bass.ds(turn_no * 2 * TB, 2 * TB), :]).then_inc(m.stored, 16)


def experts(nc, m, a):
    names = ("x_loaded_0 x_loaded_1 x_loaded_2 x_loaded_3 T_done xT_ready up_done silu_done a_ready TA_done aT_ready down_done y_ready "
             "y_stored_0 y_stored_1 y_stored_2 y_stored_3 blocks_copied")
    Q = 4
    NQB = 4
    PAIRS = BPI // 2
    with nc.Fori(0, NBLK // BPI) as i:
        with semaphores(nc, names) as s:
            def dram(t, q):
                return t[bass.ds((i * (BPI // Q) + q) * (Q * P), Q * P), :].rearrange("(r p) n -> p r n", p=P)

            def two(ap, n):
                return ap.rearrange("p (r n) -> p r n", n=n)

            with nc.Block() as block:
                @block.sync
                def _(sp):
                    def load_rows(q):
                        if q >= NQB:
                            sp.wait_ge(s["T_done"], 2 * (q - NQB + 1))
                        sp.dma_start(m.xblk[:, q % NQB, :, :], dram(a["slots_x"], q)).then_inc(s[f"x_loaded_{q % NQB}"], 16)

                    for q in range(NQB):
                        load_rows(q)
                    for q in range(BPI // Q):
                        sp.wait_ge(s["y_ready"], 2 * (q + 1))
                        sp.dma_start(dram(a["slots_y"], q), m.yblk[:, q % NQB, :, :]).then_inc(s[f"y_stored_{q % NQB}"], 16)
                        if q + NQB < BPI // Q:
                            load_rows(q + NQB)
                    for q in range(NQB):
                        sp.wait_ge(s[f"y_stored_{q}"], 16 * len(range(q, BPI // Q, NQB)))

                @block.tensor
                def _(pe):
                    regs = {}

                    def turn(p):
                        q = p // 2
                        if p % 2 == 0:
                            pe.wait_ge(s[f"x_loaded_{q % NQB}"], 16 * (q // NQB + 1))
                        if p >= 2:
                            pe.wait_ge(s["xT_ready"], p - 1)
                        for r in range(2):
                            mm = pe.transpose(m.ps[:, p % 2, r * P:(r + 1) * P], m.xblk[:, q % NQB, 2 * (p % 2) + r, :], m.ident[:])
                        mm.then_inc(s["T_done"], 1)

                    def up(p):
                        pe.wait_ge(s["xT_ready"], p + 1)
                        if p >= 2:
                            pe.wait_ge(s["a_ready"], p - 1)
                        for r in range(2):
                            mm = pe.matmul(m.ps[:, 2 + p % 2, 256 * r:256 * r + 256], m.xTb[:, p % 2, r, :],
                                           m.we[:, bass.ds(regs[p][r], 2 * DFF)], start=True, stop=True)
                        mm.then_inc(s["up_done"], 1)

                    def turn_a(p):
                        pe.wait_ge(s["a_ready"], p + 1)
                        if p >= 2:
                            pe.wait_ge(s["aT_ready"], p - 1)
                        for r in range(2):
                            mm = pe.transpose(m.ps[:, 4 + p % 2, r * P:(r + 1) * P], m.ab[:, p % 2, r, :], m.ident[:])
                        mm.then_inc(s["TA_done"], 1)

                    def down(p):
                        pe.wait_ge(s["aT_ready"], p + 1)
                        if p >= 2:
                            pe.wait_ge(s["y_ready"], p - 1)
                        for r in range(2):
                            mm = pe.matmul(m.ps[:, 6 + p % 2, r * P:(r + 1) * P], m.aTb[:, p % 2, r, :],
                                           m.we[:, bass.ds(regs[p][r] + 2 * DFF, D)], start=True, stop=True)
                        mm.then_inc(s["down_done"], 1)
                        regs.pop(p)

                    def numbers(p):
                        _, values = nc.values_load_multi_w_load_instructions(
                            m.blk_s[0:1, 2 * p:2 * p + 8], engines=(mybir.EngineType.PE,), min_val=0, max_val=(E - 1) * WE)
                        for n in range(4):
                            regs[p + n] = values[2 * n:2 * n + 2]

                    pe.wait_ge(s["blocks_copied"], 1)
                    numbers(0)
                    numbers(4)
                    turn(0)
                    turn(1)
                    up(0)
                    turn(2)
                    up(1)
                    for p in range(PAIRS):
                        turn_a(p)
                        if p + 2 < PAIRS:
                            up(p + 2)
                        if p % 4 == 0 and p + 8 < PAIRS:
                            numbers(p + 8)
                        if p + 3 < PAIRS:
                            turn(p + 3)
                        down(p)

                @block.scalar
                def _(act):
                    def x_turned(p):
                        act.wait_ge(s["T_done"], p + 1)
                        if p >= 2:
                            act.wait_ge(s["up_done"], p - 1)
                        nc.scalar.copy(m.xTb[:, p % 2, :, :], two(m.ps[:, p % 2, 0:2 * P], P)).then_inc(s["xT_ready"], 1)

                    x_turned(0)
                    x_turned(1)
                    for p in range(PAIRS):
                        act.wait_ge(s["up_done"], p + 1)
                        if p >= 2:
                            act.wait_ge(s["a_ready"], p - 1)
                        nc.scalar.activation(m.sl[:, p % 2, :, :], two(m.ps[:, 2 + p % 2, :], 2 * DFF)[:, :, DFF:], ACT.Silu).then_inc(s["silu_done"], 1)
                        if p + 2 < PAIRS:
                            x_turned(p + 2)

                @block.vector
                def _(dve):
                    def a_turned(p):
                        dve.wait_ge(s["TA_done"], p + 1)
                        if p >= 2:
                            dve.wait_ge(s["down_done"], p - 1)
                        nc.vector.tensor_copy(m.aTb[:, p % 2, :, :], two(m.ps[:, 4 + p % 2, 0:2 * P], P)).then_inc(s["aT_ready"], 1)

                    def y_out(p):
                        q = p // 2
                        dve.wait_ge(s["down_done"], p + 1)
                        if q >= NQB and p % 2 == 0:
                            dve.wait_ge(s[f"y_stored_{q % NQB}"], 16 * (q // NQB))
                        nc.vector.tensor_copy(m.yblk[:, q % NQB, 2 * (p % 2):2 * (p % 2) + 2, :], two(m.ps[:, 6 + p % 2, 0:2 * P], P)).then_inc(s["y_ready"], 1)

                    nc.vector.tensor_copy(m.blk_s[:], m.blk[:, bass.ds(i * BPI, BPI)]).then_inc(s["blocks_copied"], 1)
                    for p in range(PAIRS):
                        dve.wait_ge(s["silu_done"], p + 1)
                        if p >= 2:
                            dve.wait_ge(s["TA_done"], p - 1)
                        nc.vector.tensor_tensor(m.ab[:, p % 2, :, :], two(m.ps[:, 2 + p % 2, :], 2 * DFF)[:, :, 0:DFF], m.sl[:, p % 2, :, :], ALU.mult).then_inc(s["a_ready"], 1)
                        a_turned(p)
                        if p >= 1:
                            y_out(p - 1)
                    y_out(PAIRS - 1)


class Memory(dict):
    __getattr__ = dict.__getitem__


def program(nc, a):
    with ExitStack() as whole:
        m = Memory(names=[])

        def sb(ctx, **shapes):
            for name, shape in shapes.items():
                dt = F32
                if isinstance(shape, tuple):
                    shape, dt = shape
                m[name] = ctx.enter_context(nc.sbuf_tensor(f"{name}_{len(m.names)}", [P] + shape, dt))
                m.names.append(name)

        m["ps"] = whole.enter_context(nc.psum_tensor("ps", [P, 8, 512], F32))
        m["slots_cleared"] = whole.enter_context(nc.semaphore("slots_cleared"))
        for name in ("tables_loaded", "weights_loaded", "up_loaded", "down_loaded"):
            m[name] = whole.enter_context(nc.semaphore(name))
        m["stored"] = whole.enter_context(nc.semaphore("stored"))
        m["moved"] = [whole.enter_context(nc.semaphore(f"moved_{n}")) for n in range(2 * TB)]
        sb(whole, acc=[NT, D], xT=[NT * P], h2=[NT + TB, D], wr=[512], wo=[D],
           ident=[P], ident_bf=([P], BF16), future_bf=([4, P], BF16), before_bf=([P], BF16), ones_bf=([P], BF16),
           same_head=[P], arg_head=[HR], minus_half=[TB * HR], tot_ones=[P],
           e_in=[NT * HR], e_out=[NT * HR], decay_tile_e=[NT], argL=([2 * B, P], F32R), argR=([2 * B, P], F32R),
           logit=[NT * E], gatew4=[NT, TOPK], slot=([NT, TOPK], I32), blk=([NBLK], I32),
           zero=[D], wn=[2], xTs=[T], sq=[512], ssq=[3 * TB], ms3=[3 * TB])
        m["hT"] = m.h2[:].rearrange("p t d -> p (t d)")
        with ExitStack() as c1:
            sb(c1, xn=[NT, D], wqk=[NCH, P], wv=[KV * DH], vb=[KV * DH], projw=[8, D], projb=[D],
               gateb=[E], gatew=[E], sink=[H], sink8=[H], qkb=[NCH], rope_cos=[T], rope_sin=[T], window=[2 * P], hTs=[T])
            with ExitStack() as c2:
                sb(c2, wgt=[HR], qkvw=[(H + 2 * KV) * DH], future=[P], upto=[P], after=[P], before=[P],
                   row_head=[HR], arg_rows=[4],
                   stats=[2 * TB, 6], meanvar=[2 * TB, 2], ve=[8 * TB], r1=[2 * TB], r2=[2 * TB], xs=[2 * TB, D], hs=[2 * TB, D],
                   xT2=[2 * T], z=[NT * HR])
                load(nc, m, a)
                normalise(nc, m)
                fold(nc, m, a)
                with ExitStack() as c3:
                    sb(c3, gt=[NT * HR], bc4=([NT, 4 * HR], F32R), decay_tile=[NT])
                    gates(nc, m)
            with ExitStack() as c2:
                sb(c2, qk=[2, NCH, T], raw=[2, T], swapped=[2, T], v=[2, TB, KV * DH], prob=[3, HG, 2 * P], probT=[2, HG, 2, P],
                   mx=[2, HG], negmx=[2, HG], sinkm=[2, HG], esink=[2, HG], rowsum=[2, HG], den=[2, HG], rden=[2, HG],
                   yT=[2, 2 * KV, P], tx=[D], x2=[D], h2s=[D], h2Ts=[P], r3=[TB])
                attention(nc, m)
        sb(whole, we=[E * WE])
        w3 = m.we[:].rearrange("p (e f) -> p e f", f=WE)
        with ExitStack() as c1:
            sb(c1, top8=[NT, 8], idx8=([NT, 8], U32), idxf=[NT, TOPK], big=[6 * NT * E], chosen_bf=([NT * E], BF16), gexp=[NT, TOPK],
               gsum=[NT], grec=[NT], carry=[(NT + 1) * E], nblk=[E], cumblk=[E], base=[E], slotf=[NT, TOPK], cumT=[1], ended=[NBLK],
               iota_e=[E], iota_blk=[NT], iota_j=[NBLK], upto_e=[E, E])
            with semaphores(nc, "tables") as s, nc.Block() as block:
                @block.sync
                def _(sp):
                    for n, name in enumerate(ROUTING_TABLES):
                        row = a[name].rearrange("(o n) -> o n", o=1).partition_broadcast(P)
                        dst = m[name][:].rearrange("p a b -> p (a b)") if name == "upto_e" else m[name][:]
                        sp.dma_start(dst, row).then_inc(s["tables"], 16)
                    for e0 in range(0, E, 8):
                        sp.dma_start(w3[:, e0:e0 + 8, 0:2 * DFF], a["W_up"][e0:e0 + 8].rearrange("e p f -> p e f")).then_inc(m.up_loaded, 16)
                    sp.wait_ge(s["tables"], 16 * len(ROUTING_TABLES))

                @block.scalar
                def _(act):
                    act.dma_start(w3[:, :, 2 * DFF:], a["W_down"].rearrange("e p f -> p e f")).then_inc(m.down_loaded, 16)
            routing(nc, m)

        def retention_half(half):
            with ExitStack() as c1:
                sb(c1, state=[P], e_in_s=[TB * HR], e_out_s=[TB * HR], decay_s=[TB], argLs=([2, P], F32R), argRx=([2, HR, P], F32R),
                   state_x=[4, 4, 32], sg=[T], vn=[T], qd=[T], kd=[T], q4=([2, 512], F32R), k4=([2, 512], F32R),
                   qT_by_head=([2, 4, 4, P], F32R), k4T=([2, 4, P], F32R), qdT=[T], At=[3, 4, P], Dm=[2, 512], kvm=[P], ms16=[TB * HR],
                   r16=[TB * HR], rr=[3 * TB], rows=[2 * TB, D], slot_s=([2 * TB, TOPK], I32), gw_s=[2 * TB, TOPK])
                m["qn"], m["kn"] = m.logit[:, 0:T], m.logit[:, T:2 * T]
                m["oT"] = m.h2[:, NT:, :].rearrange("p t d -> p (t d)")
                m["o"] = m.qd
                retention(nc, m, a, half)

        retention_half(0)
        with ExitStack() as c1:
            sb(c1, blk_s=([BPI], I32), xblk=[4, 4, D], yblk=[4, 4, D], xTb=[2, 2, P], sl=[2, 2, DFF], ab=[2, 2, DFF], aTb=[2, 2, P])
            experts(nc, m, a)
        m["got"] = m.h2
        retention_half(1)
        with nc.Block() as block:
            @block.sync
            def _(sp):
                sp.wait_ge(m.stored, 16 * (B // 2))


ROUTING_TABLES = ["iota_e", "iota_blk", "iota_j", "upto_e"]


def routing_tables():
    e = np.arange(E)
    return {
        "iota_e": e.astype(np.float32),
        "iota_blk": (P * np.arange(NT)).astype(np.float32),
        "iota_j": np.arange(NBLK, dtype=np.float32),
        "upto_e": (e[None, :] <= e[:, None]).astype(np.float32).reshape(-1),
    }


ATTN = ["x", "Wq", "Wk", "Wv", "Wg", "Wgt", "Wo"]
FFN = ["attn_norm_w", "ffn_norm_w", "qkv_w", "qkv_b", "proj_w", "proj_b", "attn_sink", "gate_w", "gate_b", "W_up", "W_down"]


def kernel(**inputs):
    import concourse.bacc as _bacc
    from concourse.bass_utils import run_bass_kernel_spmd as _run

    nc = _bacc.Bacc("TRN2", target_bir_lowering=False, num_devices=1)
    given = {n: inputs["L0_attn_" + n] for n in ATTN} | {n: inputs["L0_ffn_" + n] for n in FFN} | tables() | routing_tables()
    arrays, aps = {}, {}
    for name, value in given.items():
        v = np.ascontiguousarray(value)
        arrays[f"in_{name}"] = v
        aps[name] = nc.dram_tensor(f"in_{name}", v.shape, mybir.dt.from_np(v.dtype), kind="ExternalInput").ap()
    aps["slots_x"] = nc.dram_tensor("slots_x", (SLOTS, D), F32, kind="Internal").ap()
    aps["slots_y"] = nc.dram_tensor("slots_y", (SLOTS, D), F32, kind="Internal").ap()
    aps["out"] = nc.dram_tensor("out", (B, T, D), F32, kind="ExternalOutput").ap()
    program(nc, aps)
    r = _run(nc, [arrays], core_ids=[0])
    return r.results[0]["out"]
```
